# Optimizing a Trainium2 kernel written in Bass

```python
import numpy as np
import jax
import jax.numpy as jnp

def _softmax(x, axis=-1):
    return jax.nn.softmax(x, axis=axis)

def _gelu(x):
    return jax.nn.gelu(x, approximate=True)

def _silu(x):
    return jax.nn.silu(x)

def _sigmoid(x):
    return jax.nn.sigmoid(x)

def _layernorm(x, axis=-1, eps=1e-05):
    m = jnp.mean(x, axis=axis, keepdims=True)
    v = jnp.var(x, axis=axis, keepdims=True)
    return (x - m) / jnp.sqrt(v + eps)

def _scatter_add(tgt, idx, src, axis=0):
    return tgt.at[idx].add(src)

def _segment_sum(src, seg, n):
    return jax.ops.segment_sum(src, seg, n)
kernel_name = 'mk_lm_tower_d1_tok_ids2048_r4_9b2d18'

def setup_inputs(seed: int=0):
    np.random.seed(seed)
    _w = jnp.asarray

    def _rec_inputs():
        import jax
        import jax.numpy as jnp
        _rk = jax.random.key(seed)
        x = jax.random.randint(jax.random.fold_in(_rk, 1), (64, 128), 0, 127998, jnp.int32)
        return x
    x = _rec_inputs()

    def _L0_tok_setup():
        import jax, jax.numpy as jnp
        import numpy as np
        VOCAB, D_MODEL, RANK = (32000, 512, 16)
        B, S = (4, 1024)
        key = jax.random.key(seed)
        k1, k2, k3, k4 = jax.random.split(key, 4)
        x = jax.random.randint(k1, (B, S), 0, VOCAB, dtype=jnp.int64)
        base_weight = jax.random.normal(k2, (VOCAB, D_MODEL), dtype=jnp.float32) * 0.02
        lora_A = jax.random.normal(k3, (RANK, VOCAB), dtype=jnp.float32) * 0.02
        lora_B = jax.random.normal(k4, (D_MODEL, RANK), dtype=jnp.float32) * 0.02
        return {'x': x, 'base_weight': base_weight, 'lora_A': lora_A, 'lora_B': lora_B}
    _L0_tok_all = _L0_tok_setup()
    _L0_tok_in = {k: v for k, v in _L0_tok_all.items() if k in ('base_weight', 'lora_A', 'lora_B')}
    del _L0_tok_all

    def _L0_attn_setup():
        import jax, jax.numpy as jnp
        import numpy as np
        import math
        D_MODEL = 512
        N_HEADS = 16
        Q_PROJ = D_MODEL // 4
        KV_PROJ = D_MODEL // 4
        DH = D_MODEL // N_HEADS
        LN_EPS = 1e-05

        def _layernorm(x, gamma, beta):
            mu = jnp.mean(x, axis=-1, keepdims=True)
            var = jnp.var(x, axis=-1, keepdims=True)
            return (x - mu) * jax.lax.rsqrt(var + LN_EPS) * gamma + beta
        key = jax.random.key(seed)
        ks = jax.random.split(key, 7)
        B, S = (2, 512)
        x = jax.random.normal(ks[0], (B, S, D_MODEL), dtype=jnp.float32)
        W_dq = 0.01 * jax.random.normal(ks[1], (D_MODEL, Q_PROJ), dtype=jnp.float32)
        W_uq = 0.01 * jax.random.normal(ks[2], (Q_PROJ, D_MODEL), dtype=jnp.float32)
        W_dkv = 0.01 * jax.random.normal(ks[3], (D_MODEL, KV_PROJ), dtype=jnp.float32)
        W_ukv = 0.01 * jax.random.normal(ks[4], (KV_PROJ, 2 * D_MODEL), dtype=jnp.float32)
        W_o = 0.01 * jax.random.normal(ks[5], (D_MODEL, D_MODEL), dtype=jnp.float32)
        q_ln_g = jnp.ones((Q_PROJ,), jnp.float32)
        q_ln_b = jnp.zeros((Q_PROJ,), jnp.float32)
        kv_ln_g = jnp.ones((KV_PROJ,), jnp.float32)
        kv_ln_b = jnp.zeros((KV_PROJ,), jnp.float32)
        return {'x': x, 'W_dq': W_dq, 'W_uq': W_uq, 'q_ln_g': q_ln_g, 'q_ln_b': q_ln_b, 'W_dkv': W_dkv, 'W_ukv': W_ukv, 'kv_ln_g': kv_ln_g, 'kv_ln_b': kv_ln_b, 'W_o': W_o}
    _L0_attn_all = _L0_attn_setup()
    _L0_attn_in = {k: v for k, v in _L0_attn_all.items() if k in ('W_dq', 'W_uq', 'q_ln_g', 'q_ln_b', 'W_dkv', 'W_ukv', 'kv_ln_g', 'kv_ln_b', 'W_o')}
    del _L0_attn_all

    def _L0_ffn_setup():
        import jax, jax.numpy as jnp
        import numpy as np
        B, S, EMB = (4, 512, 512)
        LAT, HID = (128, 256)
        E, K = (16, 8)
        SCALE = 2.5

        def _w(key, shape, fan_in):
            return jax.random.normal(key, shape, jnp.float32) * fan_in ** (-0.5)

        def _sqrelu(x):
            return jnp.square(jax.nn.relu(x))
        key = jax.random.key(seed)
        ks = jax.random.split(key, 11)
        return {'x': jax.random.normal(ks[0], (B, S, EMB), jnp.float32), 'sw1': _w(ks[1], (HID, EMB), EMB), 'swg': _w(ks[2], (HID, EMB), EMB), 'sw2': _w(ks[3], (EMB, HID), HID), 'rw1': _w(ks[4], (E, HID, LAT), LAT), 'rwg': _w(ks[5], (E, HID, LAT), LAT), 'rw2': _w(ks[6], (E, LAT, HID), HID), 'Wg': _w(ks[7], (E, EMB), EMB), 'Wdown': _w(ks[8], (LAT, EMB), EMB), 'Wup': _w(ks[9], (EMB, LAT), LAT), 'biases': jnp.zeros((E,), jnp.float32)}
    _L0_ffn_all = _L0_ffn_setup()
    _L0_ffn_in = {k: v for k, v in _L0_ffn_all.items() if k in ('sw1', 'swg', 'sw2', 'rw1', 'rwg', 'rw2', 'Wg', 'Wdown', 'Wup', 'biases')}
    del _L0_ffn_all
    return {'x': x, 'L0_tok_base_weight': _L0_tok_in['base_weight'], 'L0_tok_lora_A': _L0_tok_in['lora_A'], 'L0_tok_lora_B': _L0_tok_in['lora_B'], 'L0_attn_W_dq': _L0_attn_in['W_dq'], 'L0_attn_W_uq': _L0_attn_in['W_uq'], 'L0_attn_q_ln_g': _L0_attn_in['q_ln_g'], 'L0_attn_q_ln_b': _L0_attn_in['q_ln_b'], 'L0_attn_W_dkv': _L0_attn_in['W_dkv'], 'L0_attn_W_ukv': _L0_attn_in['W_ukv'], 'L0_attn_kv_ln_g': _L0_attn_in['kv_ln_g'], 'L0_attn_kv_ln_b': _L0_attn_in['kv_ln_b'], 'L0_attn_W_o': _L0_attn_in['W_o'], 'L0_ffn_sw1': _L0_ffn_in['sw1'], 'L0_ffn_swg': _L0_ffn_in['swg'], 'L0_ffn_sw2': _L0_ffn_in['sw2'], 'L0_ffn_rw1': _L0_ffn_in['rw1'], 'L0_ffn_rwg': _L0_ffn_in['rwg'], 'L0_ffn_rw2': _L0_ffn_in['rw2'], 'L0_ffn_Wg': _L0_ffn_in['Wg'], 'L0_ffn_Wdown': _L0_ffn_in['Wdown'], 'L0_ffn_Wup': _L0_ffn_in['Wup'], 'L0_ffn_biases': _L0_ffn_in['biases']}

def reference(x, L0_tok_base_weight, L0_tok_lora_A, L0_tok_lora_B, L0_attn_W_dq, L0_attn_W_uq, L0_attn_q_ln_g, L0_attn_q_ln_b, L0_attn_W_dkv, L0_attn_W_ukv, L0_attn_kv_ln_g, L0_attn_kv_ln_b, L0_attn_W_o, L0_ffn_sw1, L0_ffn_swg, L0_ffn_sw2, L0_ffn_rw1, L0_ffn_rwg, L0_ffn_rw2, L0_ffn_Wg, L0_ffn_Wdown, L0_ffn_Wup, L0_ffn_biases):
    import jax
    import jax.numpy as jnp

    def _L0_tok_ref(x, base_weight, lora_A, lora_B):
        import jax, jax.numpy as jnp
        import numpy as np
        VOCAB, D_MODEL, RANK = (32000, 512, 16)
        B, S = (4, 1024)
        base_out = base_weight[x]
        ar = lora_A.T[x]
        lora_out = jnp.einsum('bsr,dr->bsd', ar, lora_B)
        return base_out + lora_out

    def _L0_attn_ref(x, W_dq, W_uq, q_ln_g, q_ln_b, W_dkv, W_ukv, kv_ln_g, kv_ln_b, W_o):
        import jax, jax.numpy as jnp
        import numpy as np
        import math
        D_MODEL = 512
        N_HEADS = 16
        Q_PROJ = D_MODEL // 4
        KV_PROJ = D_MODEL // 4
        DH = D_MODEL // N_HEADS
        LN_EPS = 1e-05

        def _layernorm(x, gamma, beta):
            mu = jnp.mean(x, axis=-1, keepdims=True)
            var = jnp.var(x, axis=-1, keepdims=True)
            return (x - mu) * jax.lax.rsqrt(var + LN_EPS) * gamma + beta
        B, S, D = x.shape
        H, dh = (N_HEADS, DH)
        cq = _layernorm(x @ W_dq, q_ln_g, q_ln_b)
        Q = cq @ W_uq
        ckv = _layernorm(x @ W_dkv, kv_ln_g, kv_ln_b)
        KV = ckv @ W_ukv
        K, V = (KV[..., :D], KV[..., D:])
        q = Q.reshape(B, S, H, dh).transpose(0, 2, 1, 3)
        k = K.reshape(B, S, H, dh).transpose(0, 2, 1, 3)
        v = V.reshape(B, S, H, dh).transpose(0, 2, 1, 3)
        scores = jnp.einsum('bhqd,bhkd->bhqk', q, k) / math.sqrt(float(dh))
        causal = jnp.tril(jnp.ones((S, S), dtype=bool))
        scores = jnp.where(causal, scores, -jnp.inf)
        attn = jax.nn.softmax(scores, axis=-1)
        o = jnp.einsum('bhqk,bhkd->bhqd', attn, v)
        o = o.transpose(0, 2, 1, 3).reshape(B, S, D)
        return o @ W_o.T

    def _L0_ffn_ref(x, sw1, swg, sw2, rw1, rwg, rw2, Wg, Wdown, Wup, biases):
        import jax, jax.numpy as jnp
        import numpy as np
        B, S, EMB = (4, 512, 512)
        LAT, HID = (128, 256)
        E, K = (16, 8)
        SCALE = 2.5

        def _w(key, shape, fan_in):
            return jax.random.normal(key, shape, jnp.float32) * fan_in ** (-0.5)

        def _sqrelu(x):
            return jnp.square(jax.nn.relu(x))
        b, s, d = x.shape
        x2 = x.reshape(-1, d)
        shared = x2 @ sw1.T * _sqrelu(x2 @ swg.T) @ sw2.T
        xl = x2 @ Wdown.T
        probas = jax.nn.sigmoid(x2 @ Wg.T)
        _, idx = jax.lax.top_k(probas + biases, K)
        p = jnp.take_along_axis(probas, idx, axis=-1)
        p = p / p.sum(-1, keepdims=True) * SCALE
        T = x2.shape[0]
        w_dense = jnp.zeros((T, E), x2.dtype).at[jnp.arange(T)[:, None], idx].add(p)
        acc = jnp.zeros_like(xl)
        for e in range(E):
            ye = xl @ rw1[e].T * _sqrelu(xl @ rwg[e].T) @ rw2[e].T
            acc = acc + w_dense[:, e:e + 1] * ye
        out = shared + acc @ Wup.T
        return out.reshape(b, s, d)
    h = _L0_tok_ref(x, L0_tok_base_weight, L0_tok_lora_A, L0_tok_lora_B)
    h = h + _L0_attn_ref(_layernorm(h, axis=-1), L0_attn_W_dq, L0_attn_W_uq, L0_attn_q_ln_g, L0_attn_q_ln_b, L0_attn_W_dkv, L0_attn_W_ukv, L0_attn_kv_ln_g, L0_attn_kv_ln_b, L0_attn_W_o)
    h = h + _L0_ffn_ref(_layernorm(h, axis=-1), L0_ffn_sw1, L0_ffn_swg, L0_ffn_sw2, L0_ffn_rw1, L0_ffn_rwg, L0_ffn_rw2, L0_ffn_Wg, L0_ffn_Wdown, L0_ffn_Wup, L0_ffn_biases)
    return h

_drawn_inputs = setup_inputs


def setup_inputs(seed=0):
    import zlib

    import numpy as np

    out = dict(_drawn_inputs(seed))
    spreads = {'L0_attn_q_ln_g': (1.0, 0.6),
     'L0_attn_q_ln_b': (0.0, 0.8),
     'L0_attn_kv_ln_g': (1.0, 0.2),
     'L0_attn_kv_ln_b': (0.0, 0.1),
     'L0_ffn_biases': (0.0, 0.1)}
    factors = {'L0_attn_W_dq': 3.629, 'L0_attn_W_uq': 3.798}
    for name, (base, spread) in spreads.items():
        noise = np.random.default_rng([zlib.crc32(name.encode()), seed]).standard_normal(out[name].shape)
        drawn = base * np.exp(spread * noise) if base else spread * noise
        out[name] = jnp.asarray(drawn.astype(out[name].dtype))
    for name, factor in factors.items():
        out[name] = (out[name] * factor).astype(out[name].dtype)
    return out
```

```python
import concourse.bass as bass
from concourse import mybir
from contextlib import ExitStack

F32 = mybir.dt.float32
F32R = mybir.dt.float32r
BF16 = mybir.dt.bfloat16
I32 = mybir.dt.int32
ALU = mybir.AluOpType
ACT = mybir.ActivationFunctionType
AX = mybir.AxisListType

P = 128
D = 512
DC = D // P
VOCAB, RANK = 32000, 16
HEADS = 16
DH = D // HEADS
HPC = P // DH
SEQS = 64
TILES = 4
TOK = TILES * P
GROUPS = SEQS // TILES
EPS = 1e-5
RSQRT_MAGIC = 0x5F3759DF
NEWTON_OPS = 13
MASKED = -1e30

W_DQKV = 0
W_UQ = W_DQKV + DC * 256
W_UK = W_UQ + D
W_UV = W_UK + D
W_O = W_UV + D
W_ATTN = W_O + DC * D


def at_least(engine, semaphore, value):
    if not (isinstance(value, int) and value <= 0):
        engine.wait_ge(semaphore, value)


def wait_alone(engine, semaphore, value, passed):
    if not (isinstance(value, int) and value <= 0):
        engine.wait_ge(semaphore, value)
        engine.sem_inc(passed, 1)


def rsqrt(dve, step, base, var, v, nhalf, bits, t, y):
    dve.tensor_scalar(v, var, EPS, None, ALU.add).then_inc(step, 1)
    dve.tensor_scalar(nhalf, var, EPS, -0.5, ALU.add, ALU.mult).then_inc(step, 1)
    dve.wait_ge(step, base + 1)
    dve.tensor_scalar(bits, v.bitcast(I32), 1, None, ALU.logical_shift_right).then_inc(step, 1)
    dve.wait_ge(step, base + 3)
    dve.tensor_scalar(y.bitcast(I32), bits, -1, RSQRT_MAGIC, ALU.mult, ALU.add).then_inc(step, 1)
    for k in range(3):
        dve.wait_ge(step, base + 4 + 3 * k)
        dve.tensor_tensor(t, nhalf, y, ALU.mult).then_inc(step, 1)
        dve.wait_ge(step, base + 5 + 3 * k)
        dve.tensor_tensor(t, t, y, ALU.mult).then_inc(step, 1)
        dve.wait_ge(step, base + 6 + 3 * k)
        dve.scalar_tensor_tensor(out=y, in0=t, scalar=1.5, in1=y, op0=ALU.add,
                                 op1=ALU.mult).then_inc(step, 1)


U_ART, U_H, U_XT, U_WD, U_CT, U_Q, U_K, U_V, FRONT_USES = 0, 2, 6, 10, 12, 14, 18, 22, 26
GROUP_USES = FRONT_USES + TILES

AT_ART, AT_H, AT_STATS, AT_RSTD, AT_XN, AT_XT, AT_WD, AT_C, AT_CT = 2, 3, 5, 6, 7, 8, (11, 12), 13, 15
SLOTS = TILES * DC
STEPS = SLOTS + 3
NORM_LAG, T_LAG, PV_LAG = 1, 2, 3


def attention_phase(nc, table, tok, lora_b, w_attn, ln, h2):
    with ExitStack() as ctx:
        def sb(name, shape, dt):
            return ctx.enter_context(nc.sbuf_tensor(name, shape, dt))

        def pb(name, shape, dt):
            return ctx.enter_context(nc.psum_tensor(name, shape, dt))

        def sem(name):
            return ctx.enter_context(nc.semaphore(name))

        ident = sb("ident", [P, P], F32)
        ident_r = sb("ident_r", [P, P], F32R)
        ident_b = sb("ident_b", [P, P], BF16)
        mask = sb("mask", [P, HPC, P], BF16)
        gains = sb("gains", [P, 4], F32)
        w_hi = sb("w_hi", [P, W_ATTN], F32R)
        w_lo = sb("w_lo", [P, W_ATTN], F32R)
        lora_raw = sb("lora_raw", [3 * RANK, D], F32)
        lora_hi = sb("lora_hi", [3 * RANK, D], F32R)
        lora_lo = sb("lora_lo", [3 * RANK, D], F32R)
        tok_raw = sb("tok_raw", [P, SEQS], I32)
        tok_neg = sb("tok_neg", [P, SEQS], I32)
        tok_fix = sb("tok_fix", [P, SEQS], I32)
        tok_now = sb("tok_now", [P, TILES], I32)
        gath = sb("gath", [P, TILES, D + RANK], F32)
        ar = sb("ar", [P, TILES, P], F32R)
        arT = sb("arT", [3 * RANK, TOK], F32R)
        h = sb("h", [P, TILES, D], F32)
        res = sb("res", [P, TILES, D], F32)
        stats = sb("stats", [P, TILES, 6], F32)
        moments = sb("moments", [P, TILES, 2], F32)
        cstats = sb("cstats", [P, 2 * TILES, 6], F32)
        cmoments = sb("cmoments", [P, 2 * TILES, 2], F32)
        nw = sb("nw", [P, 5, 2 * TILES], F32)
        xn = sb("xn", [P, TILES, D], F32)
        xT_hi = sb("xT_hi", [P, DC, TOK], F32R)
        xT_lo = sb("xT_lo", [P, DC, TOK], F32R)
        c = sb("c", [P, TILES, 256], F32)
        cT = sb("cT", [P, 2, TOK], F32)
        cT_hi = sb("cT_hi", [P, 2, TOK], F32R)
        cT_lo = sb("cT_lo", [P, 2, TOK], F32R)
        qT = sb("qT", [P, DC, TOK], F32)
        k_diag = sb("k_diag", [P, DC, TILES, HPC, P], F32)
        raw = k_diag[:, :, :, :, :].rearrange("p a b c d -> p (a b c d)")[:, 0:W_ATTN]
        v = sb("v", [P, TILES, D], F32)
        probs = sb("probs", [P, 4, HPC, P], F32)
        nmax = sb("nmax", [P, 4, HPC], F32)
        total = sb("total", [P, 4, HPC], F32)
        inv = sb("inv", [P, 4, HPC], F32)
        pT = sb("pT", [P, 2, HPC * P], F32)
        oT_hi = sb("oT_hi", [P, DC, TOK], F32R)
        oT_lo = sb("oT_lo", [P, DC, TOK], F32R)

        ps_s = pb("ps_s", [P, 2, HPC, P], F32)
        ps_t = pb("ps_t", [P, 2, HPC * P], F32)
        ps_o = pb("ps_o", [P, 2, TOK], F32)
        work = pb("work", [P, 2, 512], F32)

        loaded = sem("loaded")
        lora_loaded = sem("lora_loaded")
        tok_loaded = sem("tok_loaded")
        consts = sem("consts")
        ident_done = sem("ident_done")
        ident_conv = sem("ident_conv")
        w_hi_done = sem("w_hi_done")
        w_lo_done = sem("w_lo_done")
        k_zeroed = sem("k_zeroed")
        lora_split = sem("lora_split")
        lora_placed = sem("lora_placed")
        tok_step = sem("tok_step")
        tok_picked = sem("tok_picked")
        gathered = [sem(f"gathered{t}") for t in range(TILES)]
        ar_zeroed = sem("ar_zeroed")
        ar_split = sem("ar_split")
        work_full = [sem(f"work_full{b}") for b in range(2)]
        work_free = [sem(f"work_free{b}") for b in range(2)]
        h_stats = sem("h_stats")
        h_moments = sem("h_moments")
        newton = sem("newton")
        xn_done = sem("xn_done")
        xT_hi_done = sem("xT_hi_done")
        c_stats = sem("c_stats")
        c_moments = sem("c_moments")
        cT_hi_done = sem("cT_hi_done")
        cT_lo_done = sem("cT_lo_done")
        scores_full = sem("scores_full")
        max_done = sem("max_done")
        exp_done = sem("exp_done")
        inv_done = sem("inv_done")
        probs_done = sem("probs_done")
        pT_full = sem("pT_full")
        pT_done = sem("pT_done")
        o_full = sem("o_full")
        oT_hi_done = sem("oT_hi_done")
        oT_lo_done = sem("oT_lo_done")
        res_loaded = sem("res_loaded")
        stored = sem("stored")
        dve_passed = sem("dve_passed")
        pool_passed = sem("pool_passed")
        sp_passed = sem("sp_passed")

        block = ctx.enter_context(nc.Block())

        def full(engine, half, k):
            engine.wait_ge(work_full[k % 2], half + k // 2 + 1)

        def empty(engine, half, k):
            at_least(engine, work_free[k % 2], half + k // 2)

        def drained(engine, half, k):
            engine.wait_ge(work_free[k % 2], half + k // 2 + 1)

        def front_half(g):
            return 0 if isinstance(g, int) and g == 0 else (GROUP_USES // 2) * g - TILES // 2

        def out_half(g):
            last = isinstance(g, int) and g == GROUPS - 1
            return (GROUP_USES // 2) * g + (FRONT_USES // 2) + (0 if last else FRONT_USES // 2)

        @block.sync
        def _(sp):
            sp.dma_start(tok_raw[:, :], tok).then_inc(tok_loaded, 16)
            for r in range(3):
                sp.dma_start(lora_raw[r * RANK:(r + 1) * RANK, :], lora_b).then_inc(lora_loaded, 16)
            sp.dma_start(gains[:, :], ln).then_inc(loaded, 16)
            sp.dma_start(raw, w_attn).then_inc(loaded, 16)
            sp.wait_ge(lora_split, 2)
            sp.dma_start(lora_hi[RANK:2 * RANK, :].bitcast(F32),
                         lora_lo[RANK:2 * RANK, :].bitcast(F32)).then_inc(lora_placed, 16)

            def group(g):
                for k in (U_H + 2, U_H + 3):
                    wait_alone(sp, work_free[k % 2], front_half(g) + k // 2 + 1, sp_passed)
                wait_alone(sp, stored, 16 * TILES * g, sp_passed)
                sp.dma_start(res[:, :, :], h[:, :, :]).then_inc(res_loaded, 16)
                for t in range(TILES):
                    row = g * TOK + t * P
                    wait_alone(sp, work_free[t % 2], out_half(g) + t // 2 + 1, sp_passed)
                    sp.dma_start(h2[bass.ds(row, P), :], res[:, t, :]).then_inc(stored, 16)

            group(0)
            with sp.Fori(1, GROUPS - 1) as g:
                group(g)
            group(GROUPS - 1)
            sp.wait_ge(stored, 16 * TILES * GROUPS)

        @block.gpsimd
        def _(pool):
            pool.memset(ident[:, :], 0.0).then_inc(consts, 1)
            pool.memset(mask[:, :, :], 0.0).then_inc(consts, 1)
            pool.wait_ge(consts, 2)
            pool.affine_select(out=ident[:, :], in_=ident[:, :], compare_op=ALU.not_equal, fill=1.0,
                               base=0, pattern=[[-1, P]], channel_multiplier=1).then_inc(ident_done, 1)
            pool.affine_select(out=mask[:, :, :], in_=mask[:, :, :], compare_op=ALU.is_ge, fill=MASKED,
                               base=0, pattern=[[0, HPC], [-1, P]],
                               channel_multiplier=1).then_inc(ident_done, 1)
            pool.wait_ge(tok_step, 4)

            def gather(g):
                pool.tensor_copy(tok_now[:, :], tok_fix[:, bass.ds(g * TILES, TILES)]).then_inc(tok_picked, 1)
                wait_alone(pool, tok_picked, g + 1, pool_passed)
                for t in range(TILES):
                    pool.indirect_dma_start(
                        out=gath[:, t, :], out_offset=None, in_=table,
                        in_offset=bass.IndirectOffsetOnAxis(ap=tok_now[:, t:t + 1], axis=0),
                    ).then_inc(gathered[t], 16)

            def wait_gathered(g):
                for t in range(TILES):
                    pool.wait_ge(gathered[t], 16 * (g + 1))

            gather(0)
            wait_gathered(0)
            drained(pool, front_half(0), U_H + 3)
            gather(1)
            with pool.Fori(2, GROUPS) as g:
                wait_gathered(g - 1)
                drained(pool, front_half(g - 1), U_H + 3)
                gather(g)

        @block.tensor
        def _(pe):
            def split_matmul(out, lhs, rhs, first, last):
                (a_hi, a_lo), (b_hi, b_lo) = lhs, rhs
                pe.matmul(out, a_hi, b_hi, start=first, stop=False)
                pe.matmul(out, a_hi, b_lo, start=False, stop=False)
                return pe.matmul(out, a_lo, b_hi, start=False, stop=last)

            def wts(col, n):
                return w_hi[:, col:col + n], w_lo[:, col:col + n]

            def pair(hi, lo, i, lo_, hi_):
                return hi[:, i, lo_:hi_], lo[:, i, lo_:hi_]

            def ar_turn(g, half, j):
                if j == 0:
                    pe.wait_ge(ar_split, 3 * (g + 1))
                empty(pe, half, U_ART + j)
                for t in (2 * j, 2 * j + 1):
                    mm = pe.transpose(work[:, j, (t % 2) * P:(t % 2 + 1) * P].bitcast(F32R),
                                      ar[:, t, :], ident_r[:, :])
                mm.then_inc(work_full[(U_ART + j) % 2], 1)

            def embed(g, half, t):
                if t % 2 == 0:
                    drained(pe, half, U_ART + t // 2)
                empty(pe, half, U_H + t)
                pe.matmul(work[:, t % 2, :], arT[:, t * P:(t + 1) * P], lora_hi[:, :],
                          start=True, stop=True).then_inc(work_full[t % 2], 1)

            def x_turn(g, half, t):
                pe.wait_ge(xn_done, TILES * g + t + 1)
                empty(pe, half, U_XT + t)
                for m in range(DC):
                    mm = pe.transpose(work[:, t % 2, m * P:(m + 1) * P], xn[:, t, m * P:(m + 1) * P],
                                      ident[:, :])
                mm.then_inc(work_full[t % 2], 1)

            def down(g, half, j):
                drained(pe, half, U_XT + 2 * j)
                drained(pe, half, U_XT + 2 * j + 1)
                empty(pe, half, U_WD + j)
                for t in (2 * j, 2 * j + 1):
                    for m in range(DC):
                        mm = split_matmul(work[:, j, (t % 2) * 256:(t % 2 + 1) * 256],
                                          pair(xT_hi, xT_lo, m, t * P, (t + 1) * P),
                                          wts(W_DQKV + m * 256, 256), m == 0, m == DC - 1)
                mm.then_inc(work_full[j], 1)

            def c_turn(g, half, j):
                drained(pe, half, U_WD)
                drained(pe, half, U_WD + 1)
                for t in range(TILES):
                    mm = pe.transpose(work[:, j, t * P:(t + 1) * P], c[:, t, j * P:(j + 1) * P],
                                      ident[:, :])
                mm.then_inc(work_full[j], 1)

            def up(g, half, use, i):
                if use == U_Q and i == 0:
                    pe.wait_ge(cT_lo_done, 2 * g + 1)
                if use == U_K and i == 0:
                    pe.wait_ge(cT_lo_done, 2 * g + 2)
                empty(pe, half, use + i)
                if use == U_V:
                    a, b = pair(cT_hi, cT_lo, 1, i * P, (i + 1) * P), wts(W_UV, D)
                else:
                    a = wts((W_UQ if use == U_Q else W_UK) + i * P, P)
                    b = pair(cT_hi, cT_lo, int(use == U_K), 0, TOK)
                split_matmul(work[:, i % 2, :], a, b, True, True).then_inc(work_full[i % 2], 1)

            def out_proj(g, half, t):
                if t == 0:
                    pe.wait_ge(oT_lo_done, DC * (g + 1))
                empty(pe, half, t)
                for m in range(DC):
                    mm = split_matmul(work[:, t % 2, :], pair(oT_hi, oT_lo, m, t * P, (t + 1) * P),
                                      wts(W_O + m * D, D), m == 0, m == DC - 1)
                mm.then_inc(work_full[t % 2], 1)

            def scores(g, s):
                m, t = divmod(s, TILES)
                if s == 0:
                    drained(pe, front_half(g), U_K + 2)
                    drained(pe, front_half(g), U_K + 3)
                at_least(pe, exp_done, SLOTS * g + s - 1)
                pe.matmul(ps_s[:, s % 2, :, :], ident_b[:, :], mask[:, :, :], start=True, stop=False,
                          skip_group_check=True)
                pe.matmul(ps_s[:, s % 2, :, :], qT[:, m, t * P:(t + 1) * P], k_diag[:, m, t, :, :],
                          start=False, stop=True, skip_group_check=True).then_inc(scores_full, 1)

            def probs_turn(g, s):
                pe.wait_ge(probs_done, SLOTS * g + s + 1)
                at_least(pe, pT_done, SLOTS * g + s - 1)
                for j in range(HPC):
                    mm = pe.transpose(ps_t[:, s % 2, j * P:(j + 1) * P], probs[:, s % 4, j, :], ident[:, :])
                mm.then_inc(pT_full, 1)

            def heads_out(g, s):
                m, t = divmod(s, TILES)
                if s == 0:
                    drained(pe, front_half(g), U_V + 2)
                    drained(pe, front_half(g), U_V + 3)
                if t == 0:
                    at_least(pe, oT_lo_done, DC * g + m - 1)
                pe.wait_ge(pT_done, SLOTS * g + s + 1)
                for j in range(HPC):
                    mm = pe.matmul(ps_o[j * DH:(j + 1) * DH, m % 2, t * P:(t + 1) * P],
                                   v[:, t, m * P + j * DH:m * P + (j + 1) * DH],
                                   pT[:, s % 2, j * P:(j + 1) * P], start=True, stop=True)
                mm.then_inc(o_full, 1)

            def front(g, half, step):
                if step == AT_ART:
                    ar_turn(g, half, 0)
                    ar_turn(g, half, 1)
                if step in (AT_H, AT_H + 1):
                    embed(g, half, 2 * (step - AT_H))
                    embed(g, half, 2 * (step - AT_H) + 1)
                if AT_XT <= step < AT_XT + TILES:
                    x_turn(g, half, step - AT_XT)
                if step in AT_WD:
                    down(g, half, AT_WD.index(step))
                if step == AT_CT:
                    c_turn(g, half, 0)
                    c_turn(g, half, 1)

            def ups(g, half, step):
                part = {SLOTS: range(0, 3), SLOTS + 1: range(3, 6), SLOTS + 2: range(6, 8),
                        SLOTS + 3: range(8, 12)}.get(step, ())
                for n in part:
                    up(g, half, U_Q + n - n % 4, n % 4)

            def group(g, more):
                for step in range(STEPS):
                    if step < SLOTS:
                        scores(g, step)
                    if more:
                        front(g + 1, front_half(g + 1), step)
                    if 0 <= step - T_LAG < SLOTS:
                        probs_turn(g, step - T_LAG)
                    if 0 <= step - PV_LAG < SLOTS:
                        heads_out(g, step - PV_LAG)
                    if more:
                        ups(g + 1, front_half(g + 1), step)
                if more:
                    ups(g + 1, front_half(g + 1), STEPS)
                for t in range(TILES):
                    out_proj(g, out_half(g), t)

            pe.wait_ge(ident_conv, 2)
            pe.wait_ge(lora_placed, 16)
            pe.wait_ge(w_lo_done, 1)
            for step in range(STEPS + 1):
                front(0, 0, step)
                ups(0, 0, step)
            group(0, True)
            with pe.Fori(1, GROUPS - 1) as g:
                group(g, True)
            group(GROUPS - 1, False)

        @block.scalar
        def _(act):
            def ar_copy(g, half, j):
                full(act, half, U_ART + j)
                act.activation(arT[:, 2 * j * P:(2 * j + 2) * P], work[0:3 * RANK, j, 0:2 * P],
                               ACT.Copy).then_inc(work_free[j], 1)

            def x_hi(g, half, t):
                full(act, half, U_XT + t)
                act.activation(xT_hi[:, :, t * P:(t + 1) * P],
                               work[:, t % 2, :].rearrange("p (m k) -> p m k", m=DC),
                               ACT.Copy).then_inc(xT_hi_done, 1)

            def c_hi(g, half, j):
                drained(act, half, U_CT + j)
                act.activation(cT_hi[:, j, :], cT[:, j, :], ACT.Copy).then_inc(cT_hi_done, 1)

            def qk_copy(g, half, use, i):
                full(act, half, use + i)
                if use == U_Q:
                    act.activation(qT[:, i, :], work[:, i % 2, :], ACT.Copy,
                                   scale=DH ** -0.5).then_inc(work_free[i % 2], 1)
                    return
                for j in range(HPC):
                    op = act.activation(k_diag[j * DH:(j + 1) * DH, i, :, j, :],
                                        work[j * DH:(j + 1) * DH, i % 2, :].rearrange("p (t k) -> p t k", t=TILES),
                                        ACT.Copy)
                op.then_inc(work_free[i % 2], 1)

            def exps(g, s):
                act.wait_ge(max_done, SLOTS * g + s + 1)
                at_least(act, pT_full, SLOTS * g + s - 3)
                for j in range(HPC):
                    e = act.activation(probs[:, s % 4, j, :], ps_s[:, s % 2, j, :], ACT.Exp,
                                       bias=nmax[:, s % 4, j:j + 1], accum_out=total[:, s % 4, j:j + 1])
                e.then_inc(exp_done, 1)

            def pT_copy(g, s):
                act.wait_ge(pT_full, SLOTS * g + s + 1)
                at_least(act, o_full, SLOTS * g + s - 1)
                act.activation(pT[:, s % 2, :], ps_t[:, s % 2, :], ACT.Copy).then_inc(pT_done, 1)

            def o_hi(g, m):
                act.wait_ge(o_full, SLOTS * g + TILES * (m + 1))
                act.activation(oT_hi[:, m, :], ps_o[:, m % 2, :], ACT.Copy).then_inc(oT_hi_done, 1)

            def front(g, half, step):
                if step == AT_ART:
                    ar_copy(g, half, 0)
                    ar_copy(g, half, 1)
                if AT_XT <= step < AT_XT + TILES:
                    x_hi(g, half, step - AT_XT)
                if step == AT_CT:
                    c_hi(g, half, 0)
                    c_hi(g, half, 1)

            def ups(g, half, step):
                part = {SLOTS: range(0, 3), SLOTS + 1: range(3, 6), SLOTS + 2: range(6, 8)}.get(step, ())
                for n in part:
                    qk_copy(g, half, U_Q + n - n % 4, n % 4)

            def group(g, more):
                for step in range(STEPS):
                    if step < SLOTS:
                        exps(g, step)
                    if 0 <= step - T_LAG < SLOTS:
                        pT_copy(g, step - T_LAG)
                    if step in (7, 11, 15):
                        o_hi(g, (step - 7) // 4)
                    if more:
                        front(g + 1, front_half(g + 1), step)
                        ups(g + 1, front_half(g + 1), step)
                o_hi(g, DC - 1)

            act.wait_ge(loaded, 32)
            act.activation(w_hi[:, :], raw, ACT.Copy).then_inc(w_hi_done, 1)
            act.wait_ge(k_zeroed, 1)
            for step in range(STEPS):
                front(0, 0, step)
                ups(0, 0, step)
            group(0, True)
            with act.Fori(1, GROUPS - 1) as g:
                group(g, True)
            group(GROUPS - 1, False)

        @block.vector
        def _(dve):
            def split_ar(g):
                for t in range(TILES):
                    dve.wait_ge(gathered[t], 16 * (g + 1))
                dve.tensor_copy(ar[:, :, 0:RANK], gath[:, :, D:D + RANK]).then_inc(ar_split, 1)
                dve.tensor_copy(ar[:, :, RANK:2 * RANK], gath[:, :, D:D + RANK]).then_inc(ar_split, 1)
                dve.wait_ge(ar_split, 3 * g + 1)
                dve.tensor_tensor(ar[:, :, 2 * RANK:3 * RANK], gath[:, :, D:D + RANK],
                                  ar[:, :, 0:RANK].bitcast(F32), ALU.subtract).then_inc(ar_split, 1)

            def h_add(g, half, t):
                full(dve, half, U_H + t)
                if t == 0:
                    at_least(dve, res_loaded, 16 * g)
                dve.tensor_tensor(h[:, t, :], gath[:, t, 0:D], work[:, t % 2, :],
                                  ALU.add).then_inc(work_free[t % 2], 1)

            def h_moment(g, half):
                for t in range(TILES):
                    if t % 2 == 0:
                        drained(dve, half, U_H + t)
                    else:
                        drained(dve, half, U_H + t)
                    dve.bn_stats(stats[:, t, :], h[:, t, :]).then_inc(h_stats, 1)
                for t in range(TILES):
                    wait_alone(dve, h_stats, TILES * g + t + 1, dve_passed)
                    dve.bn_aggr(moments[:, t, :], stats[:, t, :]).then_inc(h_moments, 1)

            def newton_of(base, var, n):
                rsqrt(dve, newton, base, var, nw[:, 0, 0:n], nw[:, 1, 0:n], nw[:, 2, 0:n].bitcast(I32),
                      nw[:, 3, 0:n], nw[:, 4, 0:n])

            def h_rstd(g):
                dve.wait_ge(h_moments, TILES * (g + 1))
                newton_of(2 * NEWTON_OPS * g, moments[:, :, 1], TILES)

            def normalise(g):
                dve.wait_ge(newton, 2 * NEWTON_OPS * g + NEWTON_OPS)
                for t in range(TILES):
                    dve.tensor_scalar(xn[:, t, :], h[:, t, :], moments[:, t, 0:1], nw[:, 4, t:t + 1],
                                      ALU.subtract, ALU.mult).then_inc(xn_done, 1)

            def x_lo(g, half, t):
                dve.wait_ge(xT_hi_done, TILES * g + t + 1)
                dve.tensor_tensor(xT_lo[:, :, t * P:(t + 1) * P],
                                  work[:, t % 2, :].rearrange("p (m k) -> p m k", m=DC),
                                  xT_hi[:, :, t * P:(t + 1) * P].bitcast(F32),
                                  ALU.subtract).then_inc(work_free[t % 2], 1)

            def c_moment(g, half, j):
                full(dve, half, U_WD + j)
                for i in range(4):
                    dve.bn_stats(cstats[:, 4 * j + i, :], work[:, j, i * P:(i + 1) * P]).then_inc(c_stats, 1)
                for i in range(4):
                    wait_alone(dve, c_stats, 8 * g + 4 * j + i + 1, dve_passed)
                    dve.bn_aggr(cmoments[:, 4 * j + i, :], cstats[:, 4 * j + i, :]).then_inc(c_moments, 1)

            def c_rstd(g):
                dve.wait_ge(c_moments, 8 * (g + 1))
                newton_of(2 * NEWTON_OPS * g + NEWTON_OPS, cmoments[:, :, 1], 2 * TILES)

            def c_norm(g):
                dve.wait_ge(newton, 2 * NEWTON_OPS * (g + 1))
                for n in range(2 * TILES):
                    j, i = divmod(n, 4)
                    op = dve.tensor_scalar(c[:, n // 2, (n % 2) * P:(n % 2 + 1) * P],
                                           work[:, j, i * P:(i + 1) * P], cmoments[:, n, 0:1],
                                           nw[:, 4, n:n + 1], ALU.subtract, ALU.mult)
                    if i == 3:
                        op.then_inc(work_free[j], 1)

            def c_gain(g, half, j):
                full(dve, half, U_CT + j)
                dve.tensor_scalar(cT[:, j, :], work[:, j, :], gains[:, 2 * j:2 * j + 1],
                                  gains[:, 2 * j + 1:2 * j + 2], ALU.mult,
                                  ALU.add).then_inc(work_free[j], 1)

            def c_lo(g, j):
                dve.wait_ge(cT_hi_done, 2 * g + j + 1)
                dve.tensor_tensor(cT_lo[:, j, :], cT[:, j, :], cT_hi[:, j, :].bitcast(F32),
                                  ALU.subtract).then_inc(cT_lo_done, 1)

            def v_copy(g, half, t):
                full(dve, half, U_V + t)
                dve.tensor_copy(v[:, t, :], work[:, t % 2, :]).then_inc(work_free[t % 2], 1)

            def add_out(g, half, t):
                full(dve, half, t)
                if t == 0:
                    dve.wait_ge(res_loaded, 16 * (g + 1))
                dve.tensor_tensor(res[:, t, :], res[:, t, :], work[:, t % 2, :],
                                  ALU.add).then_inc(work_free[t % 2], 1)

            def row_max(g, s):
                dve.wait_ge(scores_full, SLOTS * g + s + 1)
                dve.tensor_reduce(nmax[:, s % 4, :], ps_s[:, s % 2, :, :], AX.X, ALU.max,
                                  negate=True).then_inc(max_done, 1)

            def normalise_probs(g, s):
                dve.wait_ge(exp_done, SLOTS * g + s + 1)
                dve.reciprocal(inv[:, s % 4, :], total[:, s % 4, :]).then_inc(inv_done, 1)
                dve.wait_ge(inv_done, SLOTS * g + s + 1)
                dve.tensor_tensor(probs[:, s % 4, :, :], probs[:, s % 4, :, :],
                                  inv[:, s % 4, :].rearrange("p (h o) -> p h o", o=1).to_broadcast([P, HPC, P]),
                                  ALU.mult).then_inc(probs_done, 1)

            def o_lo(g, m):
                dve.wait_ge(oT_hi_done, DC * g + m + 1)
                dve.tensor_tensor(oT_lo[:, m, :], ps_o[:, m % 2, :], oT_hi[:, m, :].bitcast(F32),
                                  ALU.subtract).then_inc(oT_lo_done, 1)

            def front(g, half, step):
                if step == AT_ART - 1:
                    split_ar(g)
                if step in (AT_H, AT_H + 1):
                    h_add(g, half, 2 * (step - AT_H))
                    h_add(g, half, 2 * (step - AT_H) + 1)
                if step == AT_STATS:
                    h_moment(g, half)
                if step == AT_RSTD:
                    h_rstd(g)
                if step == AT_XN:
                    normalise(g)
                if AT_XT <= step < AT_XT + TILES:
                    x_lo(g, half, step - AT_XT)
                if step in AT_WD:
                    c_moment(g, half, AT_WD.index(step))
                if step == AT_C:
                    c_rstd(g)
                if step == AT_C + 1:
                    c_norm(g)
                if step == AT_CT:
                    c_gain(g, half, 0)
                    c_gain(g, half, 1)
                    c_lo(g, 0)
                    c_lo(g, 1)

            def group(g, more):
                for step in range(STEPS):
                    if step < SLOTS:
                        row_max(g, step)
                    if 0 <= step - NORM_LAG < SLOTS:
                        normalise_probs(g, step - NORM_LAG)
                    if step in (7, 11, 15):
                        o_lo(g, (step - 7) // 4)
                    if more:
                        front(g + 1, front_half(g + 1), step)
                o_lo(g, DC - 1)
                if more:
                    for t in range(TILES):
                        v_copy(g + 1, front_half(g + 1), t)
                for t in range(TILES):
                    add_out(g, out_half(g), t)

            dve.memset(ar[:, :, :].bitcast(F32), 0.0).then_inc(ar_zeroed, 1)
            dve.wait_ge(tok_loaded, 16)
            dve.tensor_scalar(tok_neg[:, :], tok_raw[:, :], 0, VOCAB, ALU.is_lt, ALU.mult).then_inc(tok_step, 1)
            dve.wait_ge(tok_step, 1)
            dve.tensor_tensor(tok_fix[:, :], tok_raw[:, :], tok_neg[:, :], ALU.add).then_inc(tok_step, 1)
            dve.wait_ge(tok_step, 2)
            dve.tensor_scalar(tok_fix[:, :], tok_fix[:, :], 0, VOCAB - 1, ALU.max, ALU.min).then_inc(tok_step, 2)
            dve.wait_ge(ar_zeroed, 1)
            dve.wait_ge(lora_loaded, 48)
            dve.tensor_copy(lora_hi[:, :], lora_raw[:, :]).then_inc(lora_split, 1)
            dve.wait_ge(lora_split, 1)
            dve.tensor_tensor(lora_lo[:, :], lora_raw[:, :], lora_hi[:, :].bitcast(F32),
                              ALU.subtract).then_inc(lora_split, 1)
            dve.wait_ge(ident_done, 2)
            dve.tensor_copy(ident_r[:, :], ident[:, :]).then_inc(ident_conv, 1)
            dve.tensor_copy(ident_b[:, :], ident[:, :]).then_inc(ident_conv, 1)
            dve.wait_ge(w_hi_done, 1)
            dve.tensor_tensor(w_lo[:, :], raw, w_hi[:, :].bitcast(F32),
                              ALU.subtract).then_inc(w_lo_done, 1)
            dve.wait_ge(w_lo_done, 1)
            dve.memset(k_diag[:, :, :, :, :], 0.0).then_inc(k_zeroed, 1)
            for step in range(STEPS):
                front(0, 0, step)
            for t in range(TILES):
                v_copy(0, 0, t)
            group(0, True)
            with dve.Fori(1, GROUPS - 1) as g:
                group(g, True)
            group(GROUPS - 1, False)


LAT, HID, EXPERTS, TOP = 128, 256, 16, 8
HC = HID // P
ROUTE_SCALE = 2.5
TAKEN = -1e30

F_DOWN = 0
F_S1 = F_DOWN + DC * LAT
F_SG = F_S1 + DC * HID
F_S2 = F_SG + DC * HID
F_UP = F_S2 + HC * D
F_EXP = F_UP + D
E_COLS = 2 * HID + HC * LAT
W_FFN = F_EXP + EXPERTS * E_COLS
PIECE = 2048

V_XT, V_LOGITS, V_XL, V_LT, V_OUT, V_WT = 0, 4, 5, 6, 7, 11
TURN_USES = 12
FIRST_USES = 8
UNITS = 2 * EXPERTS
ALL_UNITS = UNITS + HC
Y_LAG = 2

F_STATS, F_MOMENTS, F_RSTD, F_XN, F_XT = (1, 2), 4, 6, (8, 9), (11, 15, 19, 23)


def ffn_phase(nc, h2, w_ffn, w_gate, biases, out):
    with ExitStack() as ctx:
        def sb(name, shape, dt):
            return ctx.enter_context(nc.sbuf_tensor(name, shape, dt))

        def pb(name, shape, dt):
            return ctx.enter_context(nc.psum_tensor(name, shape, dt))

        def sem(name):
            return ctx.enter_context(nc.semaphore(name))

        f_hi = sb("f_hi", [P, W_FFN], F32R)
        f_lo = sb("f_lo", [P, W_FFN], F32R)
        fident = sb("fident", [P, P], F32)
        pick = sb("pick", [2 * EXPERTS, EXPERTS], F32R)
        gate_raw = sb("gate_raw", [P, DC, EXPERTS], F32)
        gate = sb("gate", [P, DC, P], F32R)
        bias = sb("bias", [P, EXPERTS], F32)
        x = sb("x", [P, TILES, D], F32)
        res = sb("fres", [P, TILES, D], F32)
        stats = sb("fstats", [P, TILES, 6], F32)
        moments = sb("fmoments", [P, TILES, 2], F32)
        nw = sb("fnw", [P, 5, TILES], F32)
        xT_hi = sb("fxT_hi", [P, DC, TOK], F32R)
        xT_lo = sb("fxT_lo", [P, DC, TOK], F32R)
        xl_hi = sb("xl_hi", [P, TOK], F32R)
        xl_lo = sb("xl_lo", [P, TOK], F32R)
        sh_hi = sb("sh_hi", [P, HC, TOK], F32R)
        sh_lo = sb("sh_lo", [P, HC, TOK], F32R)
        acc_hi = sb("acc_hi", [P, TOK], F32R)
        acc_lo = sb("acc_lo", [P, TOK], F32R)
        square = sb("square", [P, 2, TOK], F32)
        t = sb("t", [P, 2, TOK], F32)
        t_hi = sb("t_hi", [P, 2, TOK], F32R)
        t_lo = sb("t_lo", [P, 2, TOK], F32R)
        logits = sb("logits", [2 * EXPERTS, TOK], F32)
        route = sb("route", [P, 7, TILES, EXPERTS], F32)
        top = sb("top", [P, TILES, TOP], F32)
        wsum = sb("wsum", [P, 2, TILES], F32)
        w_parts = sb("w_parts", [P, TILES, 2 * EXPERTS], F32)
        wT = sb("wT", [2 * EXPERTS, TOK], F32R)

        ps_g = pb("ps_g", [P, 2, TOK], F32)
        ps_u = pb("ps_u", [P, 2, TOK], F32)
        ps_y = pb("ps_y", [P, TOK], F32)
        ps_w = pb("ps_w", [P, TOK], F32)
        work = pb("fwork", [P, 2, 512], F32)

        s_piece = [sem(f"piece{i}") for i in range(2)]
        piece_hi = sem("piece_hi")
        piece_lo = sem("piece_lo")
        small_loaded = sem("small_loaded")
        f_zeroed = sem("f_zeroed")
        f_ident = sem("f_ident")
        small_step = sem("small_step")
        x_loaded = sem("x_loaded")
        fres_loaded = sem("fres_loaded")
        work_full = [sem(f"fwork_full{b}") for b in range(2)]
        work_free = [sem(f"fwork_free{b}") for b in range(2)]
        x_stats = sem("x_stats")
        x_moments = sem("x_moments")
        newton = sem("fnewton")
        x_done = sem("x_done")
        xT_hi_done = sem("fxT_hi_done")
        xl_hi_done = sem("xl_hi_done")
        lt_done = sem("lt_done")
        sig_done = sem("sig_done")
        route_step = sem("route_step")
        g_full = sem("g_full")
        u_full = sem("u_full")
        relu_done = sem("relu_done")
        square_done = sem("square_done")
        t1_done = sem("t1_done")
        t_done = sem("t_done")
        t_hi_done = sem("t_hi_done")
        t_lo_done = sem("t_lo_done")
        w_full = sem("w_full")
        y_done = sem("y_done")
        acc_hi_done = sem("acc_hi_done")
        acc_lo_done = sem("acc_lo_done")
        out_stored = sem("out_stored")
        dve_passed = sem("fdve_passed")
        sp_passed = sem("fsp_passed")
        pe_passed = sem("fpe_passed")

        ROUTE_OPS = 5 + 4 + 4 + 8

        block = ctx.enter_context(nc.Block())

        def full(engine, half, k):
            engine.wait_ge(work_full[k % 2], half + k // 2 + 1)

        def empty(engine, half, k):
            at_least(engine, work_free[k % 2], half + k // 2)

        def drained(engine, half, k):
            engine.wait_ge(work_free[k % 2], half + k // 2 + 1)

        def front_half(g):
            if isinstance(g, int) and g == 0:
                return 0
            return (TURN_USES // 2) * (g - 1) + FIRST_USES // 2

        def last_use(g):
            return FIRST_USES - 1 if isinstance(g, int) and g == 0 else V_WT

        def out_half(g):
            return (TURN_USES // 2) * g + FIRST_USES // 2

        def out_use(g):
            return 0 if isinstance(g, int) and g == GROUPS - 1 else V_OUT

        @block.sync
        def _(sp):
            sp.dma_start(gate_raw[:, :, :], w_gate).then_inc(small_loaded, 16)
            sp.dma_start(bias[:, :], biases).then_inc(small_loaded, 16)
            for i in range(W_FFN // PIECE):
                at_least(sp, piece_lo, i - 1)
                sp.dma_start((x if i % 2 else res)[:, :, :].rearrange("p t d -> p (t d)"),
                             w_ffn[:, i * PIECE:(i + 1) * PIECE]).then_inc(s_piece[i % 2], 16)
            sp.wait_ge(piece_lo, W_FFN // PIECE)

            def wait_drained(half, k):
                wait_alone(sp, work_free[k % 2], half + k // 2 + 1, sp_passed)

            def load_x(g, before):
                if before is not None:
                    wait_drained(front_half(before), V_XT + 2)
                    wait_drained(front_half(before), V_XT + 3)
                sp.dma_start(x[:, :, :], h2[bass.ds(g * TOK, TOK), :].rearrange(
                    "(t p) d -> p t d", p=P)).then_inc(x_loaded, 16)

            def load_res(g):
                wait_alone(sp, out_stored, 16 * TILES * g, sp_passed)
                sp.dma_start(res[:, :, :], h2[bass.ds(g * TOK, TOK), :].rearrange(
                    "(t p) d -> p t d", p=P)).then_inc(fres_loaded, 16)

            def store(g):
                for i in range(TILES):
                    wait_drained(out_half(g), out_use(g) + i)
                    sp.dma_start(out[bass.ds(g * TOK + i * P, P), :], res[:, i, :]).then_inc(out_stored, 16)

            load_x(0, None)
            load_res(0)
            load_x(1, 0)
            store(0)
            with sp.Fori(1, GROUPS - 1) as g:
                load_res(g)
                load_x(g + 1, g)
                store(g)
            load_res(GROUPS - 1)
            store(GROUPS - 1)
            sp.wait_ge(out_stored, 16 * TILES * GROUPS)

        @block.gpsimd
        def _(pool):
            pool.memset(fident[:, :], 0.0).then_inc(f_ident, 1)
            pool.wait_ge(f_ident, 1)
            pool.affine_select(out=fident[:, :], in_=fident[:, :], compare_op=ALU.not_equal, fill=1.0,
                               base=0, pattern=[[-1, P]], channel_multiplier=1).then_inc(f_ident, 1)

        @block.tensor
        def _(pe):
            def split_matmul(o, lhs, rhs, first, last):
                (a_hi, a_lo), (b_hi, b_lo) = lhs, rhs
                pe.matmul(o, a_hi, b_hi, start=first, stop=False)
                pe.matmul(o, a_hi, b_lo, start=False, stop=False)
                return pe.matmul(o, a_lo, b_hi, start=False, stop=last)

            def wts(col, n):
                return f_hi[:, col:col + n], f_lo[:, col:col + n]

            def xs(m):
                return xT_hi[:, m, :], xT_lo[:, m, :]

            def x_turn(g, half, i):
                pe.wait_ge(x_done, TILES * g + i + 1)
                empty(pe, half, V_XT + i)
                for m in range(DC):
                    mm = pe.transpose(work[:, i % 2, m * P:(m + 1) * P], x[:, i, m * P:(m + 1) * P],
                                      fident[:, :])
                mm.then_inc(work_full[i % 2], 1)

            def route_logits(g, half):
                drained(pe, half, V_XT + 2)
                drained(pe, half, V_XT + 3)
                empty(pe, half, V_LOGITS)
                for m in range(DC):
                    for part in (xT_hi, xT_lo):
                        mm = pe.matmul(work[:, V_LOGITS % 2, :], gate[:, m, :], part[:, m, :],
                                       start=(m == 0 and part is xT_hi), stop=(m == DC - 1 and part is xT_lo))
                mm.then_inc(work_full[V_LOGITS % 2], 1)

            def to_latent(g, half):
                empty(pe, half, V_XL)
                for m in range(DC):
                    mm = split_matmul(work[:, V_XL % 2, :], wts(F_DOWN + m * LAT, LAT), xs(m),
                                      m == 0, m == DC - 1)
                mm.then_inc(work_full[V_XL % 2], 1)

            def logits_turn(g, half):
                empty(pe, half, V_LT)
                wait_alone(pe, work_free[V_LOGITS % 2], half + V_LOGITS // 2 + 1, pe_passed)
                for i in range(TILES):
                    mm = pe.transpose(work[:, V_LT % 2, i * 2 * EXPERTS:(i + 1) * 2 * EXPERTS],
                                      logits[:, i * P:(i + 1) * P], fident[0:2 * EXPERTS, 0:2 * EXPERTS])
                mm.then_inc(work_full[V_LT % 2], 1)

            def weights_turn(g, half):
                k = last_use(g)
                pe.wait_ge(route_step, ROUTE_OPS * (g + 1))
                empty(pe, half, k)
                for i in range(TILES):
                    mm = pe.transpose(work[0:2 * EXPERTS, k % 2, i * P:(i + 1) * P], w_parts[:, i, :],
                                      fident[:, :])
                mm.then_inc(work_full[k % 2], 1)

            def shared(g, j):
                n = ALL_UNITS * g + j
                for bank, col, sem_free, sem_full in ((ps_g, F_SG, relu_done, g_full),
                                                      (ps_u, F_S1, t1_done, u_full)):
                    at_least(pe, sem_free, n - 1)
                    for m in range(DC):
                        mm = split_matmul(bank[:, j % 2, :], wts(col + m * HID + j * P, P), xs(m),
                                          m == 0, m == DC - 1)
                    mm.then_inc(sem_full, 1)

            def first_products(g, n):
                e, j = divmod(n, HC)
                b = (HC + n) % 2
                for bank, col, sem_free, sem_full in ((ps_g, HID, relu_done, g_full),
                                                      (ps_u, 0, t1_done, u_full)):
                    pe.wait_ge(sem_free, ALL_UNITS * g + HC + n - 1)
                    split_matmul(bank[:, b, :], wts(F_EXP + e * E_COLS + col + j * P, P),
                                 (xl_hi[:, :], xl_lo[:, :]), True, True).then_inc(sem_full, 1)

            def spread_weights(g, e):
                at_least(pe, t_done, UNITS * g + HC * e)
                pe.matmul(ps_w[:, :], pick[:, e:e + 1].to_broadcast([2 * EXPERTS, P]), wT[:, :],
                          start=True, stop=True).then_inc(w_full, 1)

            def second_product(g, n):
                e, j = divmod(n, HC)
                if n == 0:
                    at_least(pe, acc_lo_done, g)
                pe.wait_ge(t_lo_done, ALL_UNITS * g + HC + n + 1)
                b = n % 2
                split_matmul(ps_y[:, :], wts(F_EXP + e * E_COLS + 2 * HID + j * LAT, LAT),
                             (t_hi[:, b, :], t_lo[:, b, :]), n == 0, n == UNITS - 1).then_inc(y_done, 1)

            def output(g, half, i):
                k = out_use(g) + i
                empty(pe, half, k)
                if i == 0:
                    pe.wait_ge(acc_lo_done, g + 1)
                for j in range(HC):
                    split_matmul(work[:, k % 2, :],
                                 (sh_hi[:, j, i * P:(i + 1) * P], sh_lo[:, j, i * P:(i + 1) * P]),
                                 wts(F_S2 + j * D, D), j == 0, False)
                split_matmul(work[:, k % 2, :], (acc_hi[:, i * P:(i + 1) * P], acc_lo[:, i * P:(i + 1) * P]),
                             wts(F_UP, D), False, True).then_inc(work_full[k % 2], 1)

            def front_end(g, half):
                pass

            def group(g, more):
                half = front_half(g + 1)
                for n in range(UNITS + Y_LAG):
                    if n < UNITS:
                        if n == 0:
                            drained(pe, front_half(g), V_XL)
                        if isinstance(g, int) and g == 0:
                            pe.wait_ge(piece_lo, piece_of(F_EXP + (n // HC + 1) * E_COLS))
                        first_products(g, n)
                    if n == 0:
                        drained(pe, front_half(g), last_use(g))
                        spread_weights(g, 0)
                    if more:
                        if n in F_XT:
                            x_turn(g + 1, half, F_XT.index(n))
                        if n == UNITS:
                            route_logits(g + 1, half)
                        if n == UNITS + 1:
                            to_latent(g + 1, half)
                    if n >= Y_LAG:
                        second_product(g, n - Y_LAG)
                    if n % HC == 0 and 0 < n < UNITS:
                        spread_weights(g, n // HC)
                if more:
                    logits_turn(g + 1, half)
                for i in range(TILES):
                    output(g, out_half(g), i)
                if more:
                    shared(g + 1, 0)
                    weights_turn(g + 1, half)
                    shared(g + 1, 1)

            def piece_of(col):
                return min(-(-col // PIECE), W_FFN // PIECE)

            pe.wait_ge(f_ident, 2)
            for i in range(TILES):
                x_turn(0, 0, i)
            pe.wait_ge(small_step, 4)
            route_logits(0, 0)
            to_latent(0, 0)
            logits_turn(0, 0)
            shared(0, 0)
            weights_turn(0, 0)
            shared(0, 1)
            group(0, True)
            with pe.Fori(1, GROUPS - 1) as g:
                group(g, True)
            group(GROUPS - 1, False)

        @block.scalar
        def _(act):
            def x_hi(g, half, i):
                full(act, half, V_XT + i)
                act.activation(xT_hi[:, :, i * P:(i + 1) * P],
                               work[:, i % 2, :].rearrange("p (m k) -> p m k", m=DC),
                               ACT.Copy).then_inc(xT_hi_done, 1)

            def logits_copy(g, half):
                full(act, half, V_LOGITS)
                act.activation(logits[:, :], work[0:2 * EXPERTS, V_LOGITS % 2, :],
                               ACT.Copy).then_inc(work_free[V_LOGITS % 2], 1)

            def latent_hi(g, half):
                full(act, half, V_XL)
                act.activation(xl_hi[:, :], work[:, V_XL % 2, :], ACT.Copy).then_inc(xl_hi_done, 1)

            def logits_back(g, half):
                full(act, half, V_LT)
                act.activation(w_parts[:, :, :],
                               work[:, V_LT % 2, 0:TILES * 2 * EXPERTS].rearrange("p (t e) -> p t e", t=TILES),
                               ACT.Copy).then_inc(work_free[V_LT % 2], 1)

            def sigmoid(g):
                act.wait_ge(route_step, ROUTE_OPS * g + 1)
                act.activation(route[:, 1, :, :], route[:, 0, :, :], ACT.Sigmoid).then_inc(sig_done, 1)

            def weights_copy(g, half):
                k = last_use(g)
                full(act, half, k)
                act.activation(wT[:, :], work[0:2 * EXPERTS, k % 2, :], ACT.Copy).then_inc(work_free[k % 2], 1)

            def squares(g, j):
                n = ALL_UNITS * g + j
                act.wait_ge(g_full, n + 1)
                at_least(act, t1_done, n - 1)
                act.activation(square[:, j % 2, :], ps_g[:, j % 2, :], ACT.Relu).then_inc(relu_done, 1)

            def squares_end(g, j):
                act.wait_ge(relu_done, ALL_UNITS * g + j + 1)
                act.activation(square[:, j % 2, :], square[:, j % 2, :], ACT.Square).then_inc(square_done, 1)

            def hidden_hi(g, j):
                n = ALL_UNITS * g + j
                if j < HC:
                    act.wait_ge(t1_done, n + 1)
                    dst = sh_hi[:, j, :]
                else:
                    act.wait_ge(t_done, UNITS * g + j - HC + 1)
                    at_least(act, y_done, UNITS * g + j - HC - 1)
                    dst = t_hi[:, j % 2, :]
                act.activation(dst, t[:, j % 2, :], ACT.Copy).then_inc(t_hi_done, 1)

            def sum_hi(g):
                act.wait_ge(y_done, UNITS * (g + 1))
                act.activation(acc_hi[:, :], ps_y[:, :], ACT.Copy).then_inc(acc_hi_done, 1)

            def shared(g):
                squares(g, 0)
                squares_end(g, 0)
                squares(g, 1)
                hidden_hi(g, 0)
                squares_end(g, 1)

            def group(g, more):
                half = front_half(g + 1)
                for n in range(UNITS):
                    squares(g, HC + n)
                    squares_end(g, HC + n)
                    hidden_hi(g, HC + n - 1)
                    if more and n in F_XT:
                        x_hi(g + 1, half, F_XT.index(n))
                hidden_hi(g, HC + UNITS - 1)
                if more:
                    logits_copy(g + 1, half)
                    latent_hi(g + 1, half)
                sum_hi(g)
                if more:
                    logits_back(g + 1, half)
                    sigmoid(g + 1)
                    squares(g + 1, 0)
                    squares_end(g + 1, 0)
                    weights_copy(g + 1, half)
                    squares(g + 1, 1)
                    hidden_hi(g + 1, 0)
                    squares_end(g + 1, 1)

            for i in range(W_FFN // PIECE):
                act.wait_ge(s_piece[i % 2], 16 * (i // 2 + 1))
                raw = (x if i % 2 else res)[:, :, :].rearrange("p t d -> p (t d)")
                act.activation(f_hi[:, i * PIECE:(i + 1) * PIECE], raw, ACT.Copy).then_inc(piece_hi, 1)
            for i in range(TILES):
                x_hi(0, 0, i)
            logits_copy(0, 0)
            latent_hi(0, 0)
            logits_back(0, 0)
            sigmoid(0)
            squares(0, 0)
            squares_end(0, 0)
            weights_copy(0, 0)
            squares(0, 1)
            hidden_hi(0, 0)
            squares_end(0, 1)
            group(0, True)
            with act.Fori(1, GROUPS - 1) as g:
                group(g, True)
            group(GROUPS - 1, False)

        @block.vector
        def _(dve):
            def x_moments_of(g, part):
                if part in (0, 1):
                    for i in (2 * part, 2 * part + 1):
                        dve.wait_ge(x_loaded, 16 * (g + 1))
                        dve.bn_stats(stats[:, i, :], x[:, i, :]).then_inc(x_stats, 1)
                else:
                    for i in range(TILES):
                        wait_alone(dve, x_stats, TILES * g + i + 1, dve_passed)
                        dve.bn_aggr(moments[:, i, :], stats[:, i, :]).then_inc(x_moments, 1)

            def x_rstd(g):
                dve.wait_ge(x_moments, TILES * (g + 1))
                rsqrt(dve, newton, NEWTON_OPS * g, moments[:, :, 1], nw[:, 0, :], nw[:, 1, :],
                      nw[:, 2, :].bitcast(I32), nw[:, 3, :], nw[:, 4, :])

            def normalise(g, part):
                dve.wait_ge(newton, NEWTON_OPS * (g + 1))
                for i in (2 * part, 2 * part + 1):
                    dve.tensor_scalar(x[:, i, :], x[:, i, :], moments[:, i, 0:1], nw[:, 4, i:i + 1],
                                      ALU.subtract, ALU.mult).then_inc(x_done, 1)

            def x_lo(g, half, i):
                dve.wait_ge(xT_hi_done, TILES * g + i + 1)
                dve.tensor_tensor(xT_lo[:, :, i * P:(i + 1) * P],
                                  work[:, i % 2, :].rearrange("p (m k) -> p m k", m=DC),
                                  xT_hi[:, :, i * P:(i + 1) * P].bitcast(F32),
                                  ALU.subtract).then_inc(work_free[i % 2], 1)

            def latent_lo(g, half):
                dve.wait_ge(xl_hi_done, g + 1)
                dve.tensor_tensor(xl_lo[:, :], work[:, V_XL % 2, :], xl_hi[:, :].bitcast(F32),
                                  ALU.subtract).then_inc(work_free[V_XL % 2], 1)

            def routing(g, half):
                base = ROUTE_OPS * g
                count = [0]

                def did(op):
                    op.then_inc(route_step, 1)
                    count[0] += 1

                def done(n):
                    dve.wait_ge(route_step, base + n)

                r = [route[:, i, :, :] for i in range(7)]
                drained(dve, half, V_LT)
                did(dve.tensor_tensor(r[0], w_parts[:, :, 0:EXPERTS], w_parts[:, :, EXPERTS:], ALU.add))
                dve.wait_ge(sig_done, g + 1)
                did(dve.tensor_tensor(r[2], r[1], bias[:, :].rearrange("p (o e) -> p o e", o=1)
                                      .to_broadcast([P, TILES, EXPERTS]), ALU.add))
                for i in range(TILES):
                    wait_alone(dve, route_step, base + 2, dve_passed)
                    did(dve.max(top[:, i, :], route[:, 2, i, :]))
                for i in range(TILES):
                    wait_alone(dve, route_step, base + 3 + i, dve_passed)
                    did(dve.match_replace(route[:, 3, i, :], top[:, i, :], route[:, 2, i, :], TAKEN))
                done(10)
                did(dve.tensor_tensor(r[4], r[3], r[2], ALU.not_equal))
                done(11)
                did(dve.tensor_tensor(r[5], r[4], r[1], ALU.mult))
                done(12)
                did(dve.tensor_reduce(wsum[:, 0, :], r[5], AX.X, ALU.add))
                done(13)
                did(dve.reciprocal(wsum[:, 1, :], wsum[:, 0, :]))
                done(14)
                did(dve.scalar_tensor_tensor(out=r[6], in0=r[5], scalar=ROUTE_SCALE,
                                             in1=wsum[:, 1, :].rearrange("p (t o) -> p t o", o=1)
                                             .to_broadcast([P, TILES, EXPERTS]),
                                             op0=ALU.mult, op1=ALU.mult))
                done(15)
                did(dve.tensor_copy(r[4].bitcast(F32R), r[6]))
                done(16)
                did(dve.tensor_copy(w_parts[:, :, 0:EXPERTS], r[4]))
                dve.tensor_tensor(w_parts[:, :, EXPERTS:], r[6], r[4],
                                  ALU.subtract).then_inc(route_step, ROUTE_OPS - count[0])

            def linear(g, j):
                n = ALL_UNITS * g + j
                dve.wait_ge(square_done, n + 1)
                dve.wait_ge(u_full, n + 1)
                at_least(dve, t_lo_done, n - 1)
                dve.tensor_tensor(t[:, j % 2, :], ps_u[:, j % 2, :], square[:, j % 2, :],
                                  ALU.mult).then_inc(t1_done, 1)

            def weigh(g, j):
                dve.wait_ge(t1_done, ALL_UNITS * g + j + 1)
                dve.wait_ge(w_full, EXPERTS * g + (j - HC) // HC + 1)
                dve.tensor_tensor(t[:, j % 2, :], t[:, j % 2, :], ps_w[:, :], ALU.mult).then_inc(t_done, 1)

            def hidden_lo(g, j):
                dve.wait_ge(t_hi_done, ALL_UNITS * g + j + 1)
                lo, hi = (sh_lo[:, j, :], sh_hi[:, j, :]) if j < HC else (t_lo[:, j % 2, :], t_hi[:, j % 2, :])
                dve.tensor_tensor(lo, t[:, j % 2, :], hi.bitcast(F32), ALU.subtract).then_inc(t_lo_done, 1)

            def sum_lo(g):
                dve.wait_ge(acc_hi_done, g + 1)
                dve.tensor_tensor(acc_lo[:, :], ps_y[:, :], acc_hi[:, :].bitcast(F32),
                                  ALU.subtract).then_inc(acc_lo_done, 1)

            def add_out(g, i):
                k = out_use(g) + i
                full(dve, out_half(g), k)
                if i == 0:
                    dve.wait_ge(fres_loaded, 16 * (g + 1))
                dve.tensor_tensor(res[:, i, :], res[:, i, :], work[:, k % 2, :],
                                  ALU.add).then_inc(work_free[k % 2], 1)

            def group(g, more):
                half = front_half(g + 1)
                for n in range(UNITS):
                    linear(g, HC + n)
                    hidden_lo(g, HC + n - 1)
                    weigh(g, HC + n)
                    if more:
                        if n in F_STATS:
                            x_moments_of(g + 1, F_STATS.index(n))
                        if n == F_MOMENTS:
                            x_moments_of(g + 1, 2)
                        if n == F_RSTD:
                            x_rstd(g + 1)
                        if n in F_XN:
                            normalise(g + 1, F_XN.index(n))
                        if n in F_XT:
                            x_lo(g + 1, half, F_XT.index(n))
                hidden_lo(g, HC + UNITS - 1)
                if more:
                    latent_lo(g + 1, half)
                sum_lo(g)
                if more:
                    routing(g + 1, half)
                for i in range(TILES):
                    add_out(g, i)
                if more:
                    linear(g + 1, 0)
                    linear(g + 1, 1)
                    hidden_lo(g + 1, 0)

            dve.memset(gate[:, :, :].bitcast(F32), 0.0).then_inc(f_zeroed, 1)
            dve.wait_ge(f_zeroed, 1)
            dve.wait_ge(small_loaded, 32)
            dve.tensor_copy(gate[:, :, 0:EXPERTS], gate_raw[:, :, :]).then_inc(small_step, 1)
            dve.wait_ge(small_step, 1)
            dve.tensor_tensor(gate[:, :, EXPERTS:2 * EXPERTS], gate_raw[:, :, :],
                              gate[:, :, 0:EXPERTS].bitcast(F32), ALU.subtract).then_inc(small_step, 1)
            dve.wait_ge(f_ident, 2)
            dve.tensor_tensor(pick[:, :], fident[0:2 * EXPERTS, 0:EXPERTS],
                              fident[0:2 * EXPERTS, EXPERTS:2 * EXPERTS], ALU.add).then_inc(small_step, 2)
            for i in range(W_FFN // PIECE):
                dve.wait_ge(piece_hi, i + 1)
                raw = (x if i % 2 else res)[:, :, :].rearrange("p t d -> p (t d)")
                cols = slice(i * PIECE, (i + 1) * PIECE)
                dve.tensor_tensor(f_lo[:, cols], raw, f_hi[:, cols].bitcast(F32),
                                  ALU.subtract).then_inc(piece_lo, 1)
            for part in range(3):
                x_moments_of(0, part)
            x_rstd(0)
            normalise(0, 0)
            normalise(0, 1)
            for i in range(TILES):
                x_lo(0, 0, i)
            latent_lo(0, 0)
            routing(0, 0)
            linear(0, 0)
            linear(0, 1)
            hidden_lo(0, 0)
            group(0, True)
            with dve.Fori(1, GROUPS - 1) as g:
                group(g, True)
            group(GROUPS - 1, False)


_F = "L0_ffn_"
_A = "L0_attn_"


def _chunks(w):
    return w.reshape(w.shape[0] // P, P, w.shape[1]).transpose(1, 0, 2).reshape(P, -1)


def build(nc, table, tok, lora_b, w_attn, ln, w_ffn, w_gate, biases, out):
    h2 = nc.dram_tensor("h2", [GROUPS * TOK, D], F32, kind="Internal").ap()
    attention_phase(nc, table, tok, lora_b, w_attn, ln, h2)
    ffn_phase(nc, h2, w_ffn, w_gate, biases, out)


def kernel(**inputs):
    import numpy as np
    import concourse.bacc as bacc
    from concourse.bass_utils import run_bass_kernel_spmd

    a = {k: np.asarray(v) for k, v in inputs.items()}
    expert = []
    for e in range(EXPERTS):
        expert += [a[_F + "rw1"][e].T, a[_F + "rwg"][e].T, _chunks(a[_F + "rw2"][e].T)]
    laid_out = {
        "table": np.concatenate([a["L0_tok_base_weight"], a["L0_tok_lora_A"].T], 1),
        "tok": a["x"].T,
        "lora_b": a["L0_tok_lora_B"].T,
        "w_attn": np.concatenate([
            _chunks(np.concatenate([a[_A + "W_dq"], a[_A + "W_dkv"]], 1)),
            a[_A + "W_uq"], a[_A + "W_ukv"], _chunks(a[_A + "W_o"].T)], 1),
        "ln": np.stack([a[_A + "q_ln_g"], a[_A + "q_ln_b"], a[_A + "kv_ln_g"], a[_A + "kv_ln_b"]], 1),
        "w_ffn": np.concatenate([
            _chunks(a[_F + "Wdown"].T), _chunks(a[_F + "sw1"].T), _chunks(a[_F + "swg"].T),
            _chunks(a[_F + "sw2"].T), a[_F + "Wup"].T] + expert, 1),
        "w_gate": _chunks(a[_F + "Wg"].T).reshape(P, DC, EXPERTS),
        "biases": np.broadcast_to(a[_F + "biases"], (P, EXPERTS)),
    }
    nc = bacc.Bacc("TRN2", target_bir_lowering=False, num_devices=1)
    arrays, args = {}, []
    for name, array in laid_out.items():
        array = np.ascontiguousarray(array)
        arrays["in_" + name] = array
        args.append(nc.dram_tensor("in_" + name, array.shape, mybir.dt.from_np(array.dtype),
                                   kind="ExternalInput").ap())
    out = nc.dram_tensor("out_0", (SEQS * P, D), F32, kind="ExternalOutput").ap()
    build(nc, *args, out)
    r = run_bass_kernel_spmd(nc, [arrays], core_ids=[0])
    return r.results[0]["out_0"].reshape(SEQS, P, D)
```

```python
import concourse.bass as bass
from concourse import mybir
from contextlib import ExitStack

F32 = mybir.dt.float32
F32R = mybir.dt.float32r
BF16 = mybir.dt.bfloat16
I32 = mybir.dt.int32
ALU = mybir.AluOpType
ACT = mybir.ActivationFunctionType
AX = mybir.AxisListType

P = 128
D = 512
DC = D // P
VOCAB, RANK = 32000, 16
HEADS = 16
DH = D // HEADS
HPC = P // DH
SEQS = 64
TILES = 4
TOK = TILES * P
GROUPS = SEQS // TILES
EPS = 1e-5
RSQRT_MAGIC = 0x5F3759DF
NEWTON_OPS = 4 + 3 * 4
MASKED = -1e30

W_DQKV = 0
W_UQ = W_DQKV + DC * 256
W_UK = W_UQ + D
W_UV = W_UK + D
W_O = W_UV + D
W_ATTN = W_O + DC * D


def at_least(engine, semaphore, value):
    if not (isinstance(value, int) and value <= 0):
        engine.wait_ge(semaphore, value)


def wait_alone(engine, semaphore, value, passed):
    if not (isinstance(value, int) and value <= 0):
        engine.wait_ge(semaphore, value)
        engine.sem_inc(passed, 1)


def rsqrt_seed(dve, step, base, var, v, nhalf, bits, y):
    dve.tensor_scalar(v, var, EPS, None, ALU.add).then_inc(step, 1)
    dve.tensor_scalar(nhalf, var, EPS, -0.5, ALU.add, ALU.mult).then_inc(step, 1)
    dve.wait_ge(step, base + 1)
    dve.tensor_scalar(bits, v.bitcast(I32), 1, None, ALU.logical_shift_right).then_inc(step, 1)
    dve.wait_ge(step, base + 3)
    dve.tensor_scalar(y.bitcast(I32), bits, -1, RSQRT_MAGIC, ALU.mult, ALU.add).then_inc(step, 1)


def rsqrt_steps(pool, step, base, nhalf, t, y, passed):
    for k in range(3):
        pool.wait_ge(step, base + 4 + 4 * k)
        pool.tensor_tensor(t, nhalf, y, ALU.mult).then_inc(step, 1)
        pool.wait_ge(step, base + 5 + 4 * k)
        pool.tensor_tensor(t, t, y, ALU.mult).then_inc(step, 1)
        wait_alone(pool, step, base + 6 + 4 * k, passed)
        pool.tensor_scalar(t, t, 1.5, None, ALU.add).then_inc(step, 1)
        pool.wait_ge(step, base + 7 + 4 * k)
        pool.tensor_tensor(y, y, t, ALU.mult).then_inc(step, 1)


def shift_of(pool, done, count, mean, y, t, shift, passed):
    pool.tensor_tensor(t, mean, y, ALU.mult).then_inc(done, 1)
    wait_alone(pool, done, 2 * count + 1, passed)
    pool.tensor_scalar(shift, t, -1.0, None, ALU.mult).then_inc(done, 1)


SLOTS = TILES * DC
NORM_LAG, T_LAG, PV_LAG = 1, 3, 4

MIDWAY = {3: (("h", 0), ("h", 1)), 4: (("h", 2), ("h", 3))}
END = {0: (("q", 1), ("k", 1)), 1: (("v", 0), ("v", 1)), 2: (("art", 0), ("art", 1)),
       3: (("q", 2), ("k", 2)), 4: (("v", 2), ("v", 3)), 5: (("q", 3), ("k", 3)),
       6: (("out", 0),), 7: (("out", 1), ("xt", 0)), 8: (("out", 2), ("xt", 1)),
       9: (("out", 3), ("xt", 2)), 10: (("xt", 3), ("wd", 0)), 11: (("wd", 1),),
       13: (("ct", 0), ("ct", 1)), 15: (("q", 0), ("k", 0))}
FRONT = ("art", "h", "xt", "wd", "ct")
STATS_AT, NORM_AT, C_NORM_AT = (4, 5), 6, 13
O_HI_AT = {9: 0, 12: 1, 0: 2, 4: 3}
O_LO_AT = {10: 0, 15: 1, 1: 2, 4: 3}
NORM_FIRST = range(7, 13)
V_ON_DVE = ()
SOON, LATER = ("k", "out", "h", "ct", "v"), ("xt", "wd")
DRAINS = 2


def is_turn(n, which):
    return isinstance(n, int) and n == which


def has_part(n, part, i):
    if part == "out":
        return not (is_turn(n, -1) or is_turn(n, 0))
    if part in FRONT or (part in "qk" and i == 0):
        return not (is_turn(n, GROUPS - 1) or is_turn(n, GROUPS))
    return not (is_turn(n, -1) or is_turn(n, GROUPS))


def uses_of(n):
    return [use for step in range(SLOTS) for use in MIDWAY.get(step, ()) + END.get(step, ())
            if has_part(n, *use)]


def place(n, part, i):
    k = uses_of(n).index((part, i))
    start, first = len(uses_of(-1)), len(uses_of(0))
    each = len(uses_of(1))
    if is_turn(n, -1):
        before = 0
    elif is_turn(n, 0):
        before = start // 2
    elif is_turn(n, GROUPS):
        before = (start + first + each * (GROUPS - 2) + len(uses_of(GROUPS - 1))) // 2
    else:
        before = (each // 2) * n + (start + first - each) // 2
    return k % 2, before + k // 2


def attention_phase(nc, table, tok, lora_b, w_attn, ln, h2):
    with ExitStack() as ctx:
        def sb(name, shape, dt):
            return ctx.enter_context(nc.sbuf_tensor(name, shape, dt))

        def pb(name, shape, dt):
            return ctx.enter_context(nc.psum_tensor(name, shape, dt))

        def sem(name):
            return ctx.enter_context(nc.semaphore(name))

        ident = sb("ident", [P, P], F32)
        ident_r = sb("ident_r", [P, P], F32R)
        ident_b = sb("ident_b", [P, P], BF16)
        mask = sb("mask", [P, HPC, P], BF16)
        gains = sb("gains", [P, 4], F32)
        w_hi = sb("w_hi", [P, W_ATTN], F32R)
        w_lo = sb("w_lo", [P, W_ATTN], F32R)
        lora_raw = sb("lora_raw", [3 * RANK, D], F32)
        lora_hi = sb("lora_hi", [3 * RANK, D], F32R)
        lora_lo = sb("lora_lo", [3 * RANK, D], F32R)
        tok_raw = sb("tok_raw", [P, SEQS], I32)
        tok_neg = sb("tok_neg", [P, SEQS], I32)
        tok_fix = sb("tok_fix", [P, SEQS], I32)
        tok_now = sb("tok_now", [P, TILES], I32)
        gath = sb("gath", [P, TILES, D + RANK], F32)
        ar = sb("ar", [P, TILES, P], F32R)
        arT = sb("arT", [3 * RANK, TOK], F32R)
        h = sb("h", [P, TILES, D], F32)
        res_next = sb("res_next", [P, TILES, D], F32)
        res = sb("res", [P, TILES, D], F32)
        stats = sb("stats", [P, TILES, 6], F32)
        moments = sb("moments", [P, TILES, 2], F32)
        cstats = sb("cstats", [P, 2 * TILES, 6], F32)
        cmoments = sb("cmoments", [P, 2 * TILES, 2], F32)
        nw = sb("nw", [P, 5, 2 * TILES], F32)
        c_shift = sb("c_shift", [P, 2 * TILES], F32)
        xn = sb("xn", [P, TILES, D], F32)
        xT_hi = sb("xT_hi", [P, DC, TOK], F32R)
        xT_lo = sb("xT_lo", [P, DC, TOK], F32R)
        c = sb("c", [P, TILES, 256], F32)
        cT = sb("cT", [P, 2, TOK], F32)
        cT_hi = sb("cT_hi", [P, 2, TOK], F32R)
        cT_lo = sb("cT_lo", [P, 2, TOK], F32R)
        qT = sb("qT", [P, DC, TOK], F32)
        k_diag = sb("k_diag", [P, DC, TILES, HPC, P], F32)
        raw = k_diag[:, :, :, :, :].rearrange("p a b c d -> p (a b c d)")[:, 0:W_ATTN]
        v = sb("v", [P, TILES, D], F32)
        probs = sb("probs", [P, 4, HPC, P], F32)
        nmax = sb("nmax", [P, 4, HPC], F32)
        total = sb("total", [P, 4, HPC], F32)
        inv = sb("inv", [P, 4, HPC], F32)
        pT = sb("pT", [P, 2, HPC * P], F32)
        oT_hi = sb("oT_hi", [P, DC, TOK], F32R)
        oT_lo = sb("oT_lo", [P, DC, TOK], F32R)

        ps_s = pb("ps_s", [P, 2, HPC, P], F32)
        ps_t = pb("ps_t", [P, 2, HPC * P], F32)
        ps_o = pb("ps_o", [P, 2, TOK], F32)
        work = pb("work", [P, 2, 512], F32)

        loaded = sem("loaded")
        lora_loaded = sem("lora_loaded")
        tok_loaded = sem("tok_loaded")
        consts = sem("consts")
        ident_done = sem("ident_done")
        ident_conv = sem("ident_conv")
        w_hi_done = sem("w_hi_done")
        w_lo_done = sem("w_lo_done")
        k_zeroed = sem("k_zeroed")
        lora_split = sem("lora_split")
        lora_placed = sem("lora_placed")
        tok_step = sem("tok_step")
        tok_picked = sem("tok_picked")
        gathered = [sem(f"gathered{t}") for t in range(TILES)]
        ar_zeroed = sem("ar_zeroed")
        ar_split = sem("ar_split")
        work_full = [sem(f"work_full{b}") for b in range(2)]
        work_free = [sem(f"work_free{b}") for b in range(2)]
        h_stats = sem("h_stats")
        h_moments = sem("h_moments")
        newton = sem("newton")
        xn_done = sem("xn_done")
        xT_hi_done = sem("xT_hi_done")
        c_stats = sem("c_stats")
        c_moments = sem("c_moments")
        cT_hi_done = sem("cT_hi_done")
        c_shift_done = sem("c_shift_done")
        cT_done = sem("cT_done")
        scores_full = sem("scores_full")
        max_done = sem("max_done")
        exp_done = sem("exp_done")
        inv_done = sem("inv_done")
        probs_done = sem("probs_done")
        pT_full = sem("pT_full")
        pT_done = sem("pT_done")
        o_full = sem("o_full")
        oT_hi_done = sem("oT_hi_done")
        oT_lo_done = sem("oT_lo_done")
        res_kept = [sem(f"res_kept{t}") for t in range(TILES)]
        res_loaded = [sem(f"res_loaded{t}") for t in range(TILES)]
        stored = [sem(f"stored{t}") for t in range(TILES)]
        dve_passed = sem("dve_passed")
        pool_passed = sem("pool_passed")
        sp_passed = sem("sp_passed")

        block = ctx.enter_context(nc.Block())

        def full(engine, n, part, i):
            bank, before = place(n, part, i)
            engine.wait_ge(work_full[bank], before + 1)

        def empty(engine, n, part, i):
            bank, before = place(n, part, i)
            at_least(engine, work_free[bank], DRAINS * before)

        def drained(engine, n, part, i):
            bank, before = place(n, part, i)
            engine.wait_ge(work_free[bank], DRAINS * (before + 1))

        def bank_of(n, part, i):
            return work[:, place(n, part, i)[0], :]

        def was_read(instruction, n, part, i, drains=DRAINS):
            instruction.then_inc(work_free[place(n, part, i)[0]], drains)

        def slots_of(n):
            return range(0 if is_turn(n, -1) or is_turn(n, GROUPS) else SLOTS)

        def has_slot(n, slot):
            if slot < 0:
                return not (is_turn(n, -1) or is_turn(n, 0))
            return slot in slots_of(n)

        @block.sync
        def _(sp):
            sp.dma_start(tok_raw[:, :], tok).then_inc(tok_loaded, 16)
            for r in range(3):
                sp.dma_start(lora_raw[r * RANK:(r + 1) * RANK, :], lora_b).then_inc(lora_loaded, 16)
            sp.dma_start(gains[:, :], ln).then_inc(loaded, 16)
            sp.dma_start(raw, w_attn).then_inc(loaded, 16)
            sp.wait_ge(lora_split, 2)
            sp.dma_start(lora_hi[RANK:2 * RANK, :].bitcast(F32),
                         lora_lo[RANK:2 * RANK, :].bitcast(F32)).then_inc(lora_placed, 16)

            def turn(n):
                if has_part(n, "out", 0):
                    for t in range(TILES):
                        bank, before = place(n, "out", t)
                        wait_alone(sp, work_free[bank], DRAINS * (before + 1), sp_passed)
                        sp.dma_start(h2[bass.ds((n - 1) * TOK + t * P, P), :],
                                     res[:, t, :]).then_inc(stored[t], 16)
                if slots_of(n):
                    for t in range(TILES):
                        wait_alone(sp, stored[t], 16 * n, sp_passed)
                        wait_alone(sp, res_kept[t], 16 * (n + 1), sp_passed)
                        sp.dma_start(res[:, t, :], res_next[:, t, :]).then_inc(res_loaded[t], 16)
                if has_part(n, "h", 0):
                    for t in range(TILES):
                        bank, before = place(n, "h", t)
                        wait_alone(sp, work_free[bank], DRAINS * (before + 1), sp_passed)
                        wait_alone(sp, res_loaded[t], 16 * (n + 1), sp_passed)
                        sp.dma_start(res_next[:, t, :], h[:, t, :]).then_inc(res_kept[t], 16)

            turn(-1)
            turn(0)
            with sp.Fori(1, GROUPS - 1) as n:
                turn(n)
            turn(GROUPS - 1)
            turn(GROUPS)
            for t in range(TILES):
                sp.wait_ge(stored[t], 16 * GROUPS)

        @block.gpsimd
        def _(pool):
            pool.memset(ident[:, :], 0.0).then_inc(consts, 1)
            pool.memset(mask[:, :, :], 0.0).then_inc(consts, 1)
            pool.wait_ge(consts, 2)
            pool.affine_select(out=ident[:, :], in_=ident[:, :], compare_op=ALU.not_equal, fill=1.0,
                               base=0, pattern=[[-1, P]], channel_multiplier=1).then_inc(ident_done, 1)
            pool.affine_select(out=mask[:, :, :], in_=mask[:, :, :], compare_op=ALU.is_ge, fill=MASKED,
                               base=0, pattern=[[0, HPC], [-1, P]],
                               channel_multiplier=1).then_inc(ident_done, 1)
            pool.wait_ge(tok_step, 4)

            def gather(g):
                pool.tensor_copy(tok_now[:, :], tok_fix[:, bass.ds(g * TILES, TILES)]).then_inc(tok_picked, 1)
                wait_alone(pool, tok_picked, g + 1, pool_passed)
                for t in range(TILES):
                    pool.indirect_dma_start(
                        out=gath[:, t, :], out_offset=None, in_=table,
                        in_offset=bass.IndirectOffsetOnAxis(ap=tok_now[:, t:t + 1], axis=0),
                    ).then_inc(gathered[t], 16)

            def wait_gathered(g):
                for t in range(TILES):
                    pool.wait_ge(gathered[t], 16 * (g + 1))

            def newton_of(base, n):
                rsqrt_steps(pool, newton, base, nw[:, 1, 0:n], nw[:, 3, 0:n], nw[:, 4, 0:n],
                            pool_passed)

            def turn(n, more=True):
                if more:
                    wait_gathered(n + 1)
                    drained(pool, n, "h", TILES - 1)
                    gather(n + 2)
                newton_of(2 * NEWTON_OPS * (n + 1), TILES)
                newton_of(2 * NEWTON_OPS * (n + 1) + NEWTON_OPS, 2 * TILES)
                pool.wait_ge(newton, 2 * NEWTON_OPS * (n + 2))
                shift_of(pool, c_shift_done, n + 1, cmoments[:, :, 0], nw[:, 4, 0:2 * TILES],
                         nw[:, 3, 0:2 * TILES], c_shift[:, :], pool_passed)

            gather(0)
            turn(-1)
            turn(0)
            with pool.Fori(1, GROUPS - 2) as n:
                turn(n)
            turn(GROUPS - 2, more=False)

        @block.tensor
        def _(pe):
            def split_matmul(out, lhs, rhs, first, last):
                (a_hi, a_lo), (b_hi, b_lo) = lhs, rhs
                pe.matmul(out, a_hi, b_hi, start=first, stop=False)
                pe.matmul(out, a_hi, b_lo, start=False, stop=False)
                return pe.matmul(out, a_lo, b_hi, start=False, stop=last)

            def wts(col, n):
                return w_hi[:, col:col + n], w_lo[:, col:col + n]

            def pair(hi, lo, i, lo_, hi_):
                return hi[:, i, lo_:hi_], lo[:, i, lo_:hi_]

            def ar_turn(n, j):
                if j == 0:
                    pe.wait_ge(ar_split, 3 * (n + 2))
                bank = bank_of(n, "art", j)
                for t in (2 * j, 2 * j + 1):
                    mm = pe.transpose(bank[:, (t % 2) * P:(t % 2 + 1) * P].bitcast(F32R),
                                      ar[:, t, :], ident_r[:, :])
                return mm

            def embed(n, t):
                if t % 2 == 0:
                    drained(pe, n, "art", t // 2)
                return pe.matmul(bank_of(n, "h", t), arT[:, t * P:(t + 1) * P], lora_hi[:, :],
                                 start=True, stop=True)

            def x_turn(n, t):
                pe.wait_ge(xn_done, TILES * (n + 1) + t + 1)
                bank = bank_of(n, "xt", t)
                for m in range(DC):
                    mm = pe.transpose(bank[:, m * P:(m + 1) * P], xn[:, t, m * P:(m + 1) * P],
                                      ident[:, :])
                return mm

            def down(n, j):
                bank = bank_of(n, "wd", j)
                for t in (2 * j, 2 * j + 1):
                    drained(pe, n, "xt", t)
                    for m in range(DC):
                        mm = split_matmul(bank[:, (t % 2) * 256:(t % 2 + 1) * 256],
                                          pair(xT_hi, xT_lo, m, t * P, (t + 1) * P),
                                          wts(W_DQKV + m * 256, 256), m == 0, m == DC - 1)
                return mm

            def c_turn(n, j):
                drained(pe, n, "wd", 0)
                drained(pe, n, "wd", 1)
                bank = bank_of(n, "ct", j)
                for t in range(TILES):
                    mm = pe.transpose(bank[:, t * P:(t + 1) * P], c[:, t, j * P:(j + 1) * P],
                                      ident[:, :])
                return mm

            def up(n, part, i):
                if i == 0 and part != "v":
                    drained(pe, n, "ct", int(part == "k"))
                if part == "v":
                    a, b = pair(cT_hi, cT_lo, 1, i * P, (i + 1) * P), wts(W_UV, D)
                else:
                    a = wts((W_UQ if part == "q" else W_UK) + i * P, P)
                    b = pair(cT_hi, cT_lo, int(part == "k"), 0, TOK)
                return split_matmul(bank_of(n, part, i), a, b, True, True)

            def out_proj(n, t):
                pe.wait_ge(oT_lo_done, DC * n)
                for m in range(DC):
                    mm = split_matmul(bank_of(n, "out", t), pair(oT_hi, oT_lo, m, t * P, (t + 1) * P),
                                      wts(W_O + m * D, D), m == 0, m == DC - 1)
                return mm

            def scores(n, s):
                m, t = divmod(s, TILES)
                if t == 0:
                    drained(pe, n - (m == 0), "q", m)
                    drained(pe, n - (m == 0), "k", m)
                at_least(pe, exp_done, SLOTS * n + s - 1)
                pe.matmul(ps_s[:, s % 2, :, :], ident_b[:, :], mask[:, :, :], start=True, stop=False,
                          skip_group_check=True)
                pe.matmul(ps_s[:, s % 2, :, :], qT[:, m, t * P:(t + 1) * P], k_diag[:, m, t, :, :],
                          start=False, stop=True, skip_group_check=True).then_inc(scores_full, 1)

            def probs_turn(n, s):
                pe.wait_ge(probs_done, SLOTS * n + s + 1)
                at_least(pe, pT_done, SLOTS * n + s - 1)
                for j in range(HPC):
                    mm = pe.transpose(ps_t[:, s % 2, j * P:(j + 1) * P], probs[:, s % 4, j, :], ident[:, :])
                mm.then_inc(pT_full, 1)

            def heads_out(n, s):
                m, t = divmod(s, TILES)
                if m == 0:
                    drained(pe, n, "v", t)
                if t == 0:
                    at_least(pe, oT_lo_done, DC * n + m - 1)
                pe.wait_ge(pT_done, SLOTS * n + s + 1)
                for j in range(HPC):
                    f = (m % DC) * P + j * DH
                    mm = pe.matmul(ps_o[j * DH:(j + 1) * DH, m % 2, t * P:(t + 1) * P],
                                   v[:, t, f:f + DH], pT[:, s % 2, j * P:(j + 1) * P],
                                   start=True, stop=True)
                mm.then_inc(o_full, 1)

            def work_on(n, uses):
                for part, i in uses:
                    if has_part(n, part, i):
                        empty(pe, n, part, i)
                        if part == "art":
                            mm = ar_turn(n, i)
                        elif part == "h":
                            mm = embed(n, i)
                        elif part == "xt":
                            mm = x_turn(n, i)
                        elif part == "wd":
                            mm = down(n, i)
                        elif part == "ct":
                            mm = c_turn(n, i)
                        elif part == "out":
                            mm = out_proj(n, i)
                        else:
                            mm = up(n, part, i)
                        mm.then_inc(work_full[place(n, part, i)[0]], 1)

            def turn(n):
                for step in range(SLOTS):
                    if step > 0 and has_slot(n, step):
                        scores(n, step)
                    work_on(n, MIDWAY.get(step, ()))
                    if has_slot(n, step - T_LAG):
                        probs_turn(n, step - T_LAG)
                    if has_slot(n, step - PV_LAG):
                        heads_out(n, step - PV_LAG)
                    if step == 0 and has_slot(n, 0):
                        scores(n, 0)
                    work_on(n, END.get(step, ()))

            pe.wait_ge(ident_conv, 2)
            pe.wait_ge(lora_placed, 16)
            pe.wait_ge(w_lo_done, 1)
            turn(-1)
            turn(0)
            with pe.Fori(1, GROUPS - 1) as n:
                turn(n)
            turn(GROUPS - 1)
            turn(GROUPS)

        @block.scalar
        def _(act):
            def ar_copy(n, j):
                was_read(act.activation(arT[:, 2 * j * P:(2 * j + 2) * P],
                                        bank_of(n, "art", j)[0:3 * RANK, 0:2 * P], ACT.Copy), n, "art", j)

            def x_hi(n, t):
                act.activation(xT_hi[:, :, t * P:(t + 1) * P],
                               bank_of(n, "xt", t).rearrange("p (m k) -> p m k", m=DC),
                               ACT.Copy).then_inc(xT_hi_done, 1)

            def c_hi(n, j):
                if j == 0:
                    full(act, n, "ct", j)
                else:
                    act.wait_ge(cT_done, 2 * (n + 1) + 1)
                act.activation(cT_hi[:, j, :], bank_of(n, "ct", j), ACT.Identity,
                               scale=gains[:, 2 * j:2 * j + 1],
                               bias=gains[:, 2 * j + 1:2 * j + 2]).then_inc(cT_hi_done, 1)

            def c_norm(n):
                act.wait_ge(c_shift_done, 2 * (n + 2))
                for a in range(TILES, 2 * TILES):
                    i = a - TILES
                    op = act.activation(c[:, a // 2, (a % 2) * P:(a % 2 + 1) * P],
                                        bank_of(n, "wd", 1)[:, i * P:(i + 1) * P], ACT.Identity,
                                        scale=nw[:, 4, a:a + 1], bias=c_shift[:, a:a + 1])
                was_read(op, n, "wd", 1)

            def q_copy(n, i):
                was_read(act.activation(qT[:, i, :], bank_of(n, "q", i), ACT.Copy, scale=DH ** -0.5),
                         n, "q", i)

            def k_copy(n, i):
                for j in (2, 3):
                    op = act.activation(k_diag[j * DH:(j + 1) * DH, i, :, j, :],
                                        bank_of(n, "k", i)[j * DH:(j + 1) * DH, :].rearrange("p (t k) -> p t k", t=TILES),
                                        ACT.Copy)
                was_read(op, n, "k", i, 1)

            def v_copy(n, t):
                was_read(act.activation(v[:, t, :], bank_of(n, "v", t), ACT.Copy), n, "v", t)

            def exps(n, s):
                act.wait_ge(max_done, SLOTS * n + s + 1)
                at_least(act, pT_full, SLOTS * n + s - 3)
                for j in range(HPC):
                    e = act.activation(probs[:, s % 4, j, :], ps_s[:, s % 2, j, :], ACT.Exp,
                                       bias=nmax[:, s % 4, j:j + 1], accum_out=total[:, s % 4, j:j + 1])
                e.then_inc(exp_done, 1)

            def pT_copy(n, s):
                act.wait_ge(pT_full, SLOTS * n + s + 1)
                at_least(act, o_full, SLOTS * n + s - 1)
                act.activation(pT[:, s % 2, :], ps_t[:, s % 2, :], ACT.Copy).then_inc(pT_done, 1)

            def o_hi(n, m):
                if m == 0 and has_part(n, "out", TILES - 1):
                    full(act, n, "out", TILES - 1)
                act.wait_ge(o_full, SLOTS * (n - (m >= 2)) + TILES * (m + 1))
                act.activation(oT_hi[:, m, :], ps_o[:, m % 2, :], ACT.Copy).then_inc(oT_hi_done, 1)

            def read_work(n, uses):
                for part, i in uses:
                    if part == "ct" and has_part(n, part, i):
                        c_hi(n, i)
                    elif (has_part(n, part, i) and part in ("art", "xt", "q", "k", "v")
                          and not (part == "v" and i in V_ON_DVE)):
                        full(act, n, part, i)
                        if part == "art":
                            ar_copy(n, i)
                        elif part == "xt":
                            x_hi(n, i)
                        elif part == "q":
                            q_copy(n, i)
                        elif part == "k":
                            k_copy(n, i)
                        else:
                            v_copy(n, i)

            def turn(n):
                if not is_turn(n, -1):
                    read_work(n - 1, END[SLOTS - 1])
                for step in range(SLOTS):
                    if step > 0:
                        read_work(n, END.get(step - 1, ()))
                    if step in O_HI_AT and has_slot(n, 0 if O_HI_AT[step] < 2 else -1):
                        o_hi(n, O_HI_AT[step])
                    if has_slot(n, step):
                        exps(n, step)
                    read_work(n, MIDWAY.get(step, ()))
                    if step == C_NORM_AT and has_part(n, "wd", 1):
                        c_norm(n)
                    if has_slot(n, step - T_LAG):
                        pT_copy(n, step - T_LAG)

            act.wait_ge(loaded, 32)
            act.activation(w_hi[:, :], raw, ACT.Copy).then_inc(w_hi_done, 1)
            act.wait_ge(k_zeroed, 1)
            turn(-1)
            turn(0)
            with act.Fori(1, GROUPS - 1) as n:
                turn(n)
            turn(GROUPS - 1)
            turn(GROUPS)

        @block.vector
        def _(dve):
            def split_ar(g):
                for t in range(TILES):
                    dve.wait_ge(gathered[t], 16 * (g + 1))
                dve.tensor_copy(ar[:, :, 0:RANK], gath[:, :, D:D + RANK]).then_inc(ar_split, 1)
                dve.tensor_copy(ar[:, :, RANK:2 * RANK], gath[:, :, D:D + RANK]).then_inc(ar_split, 1)
                dve.wait_ge(ar_split, 3 * g + 1)
                dve.tensor_tensor(ar[:, :, 2 * RANK:3 * RANK], gath[:, :, D:D + RANK],
                                  ar[:, :, 0:RANK].bitcast(F32), ALU.subtract).then_inc(ar_split, 1)

            def h_add(n, t):
                full(dve, n, "h", t)
                at_least(dve, res_kept[t], 16 * (n + 1))
                was_read(dve.tensor_tensor(h[:, t, :], gath[:, t, 0:D], bank_of(n, "h", t), ALU.add),
                         n, "h", t)

            def h_stat(n, t):
                drained(dve, n, "h", t)
                dve.bn_stats(stats[:, t, :], h[:, t, :]).then_inc(h_stats, 1)

            def h_moment(g):
                for t in range(TILES):
                    wait_alone(dve, h_stats, TILES * g + t + 1, dve_passed)
                    dve.bn_aggr(moments[:, t, :], stats[:, t, :]).then_inc(h_moments, 1)

            def seed_of(base, var, n):
                rsqrt_seed(dve, newton, base, var, nw[:, 0, 0:n], nw[:, 1, 0:n],
                           nw[:, 2, 0:n].bitcast(I32), nw[:, 4, 0:n])

            def h_seed(g):
                dve.wait_ge(h_moments, TILES * (g + 1))
                seed_of(2 * NEWTON_OPS * g, moments[:, :, 1], TILES)

            def c_seed(g):
                dve.wait_ge(c_moments, 2 * TILES * (g + 1))
                seed_of(2 * NEWTON_OPS * g + NEWTON_OPS, cmoments[:, :, 1], 2 * TILES)

            def normalise(g):
                dve.wait_ge(newton, 2 * NEWTON_OPS * g + NEWTON_OPS)
                for t in range(TILES):
                    dve.tensor_scalar(xn[:, t, :], h[:, t, :], moments[:, t, 0:1], nw[:, 4, t:t + 1],
                                      ALU.subtract, ALU.mult).then_inc(xn_done, 1)

            def x_lo(n, t):
                dve.wait_ge(xT_hi_done, TILES * (n + 1) + t + 1)
                was_read(dve.tensor_tensor(xT_lo[:, :, t * P:(t + 1) * P],
                                           bank_of(n, "xt", t).rearrange("p (m k) -> p m k", m=DC),
                                           xT_hi[:, :, t * P:(t + 1) * P].bitcast(F32),
                                           ALU.subtract), n, "xt", t)

            def c_moment(n, j):
                full(dve, n, "wd", j)
                for i in range(4):
                    dve.bn_stats(cstats[:, 4 * j + i, :],
                                 bank_of(n, "wd", j)[:, i * P:(i + 1) * P]).then_inc(c_stats, 1)
                for i in range(4):
                    wait_alone(dve, c_stats, 8 * (n + 1) + 4 * j + i + 1, dve_passed)
                    dve.bn_aggr(cmoments[:, 4 * j + i, :], cstats[:, 4 * j + i, :]).then_inc(c_moments, 1)

            def c_norm(n):
                dve.wait_ge(newton, 2 * NEWTON_OPS * (n + 2))
                for a in range(TILES):
                    op = dve.tensor_scalar(c[:, a // 2, (a % 2) * P:(a % 2 + 1) * P],
                                           bank_of(n, "wd", 0)[:, a * P:(a + 1) * P], cmoments[:, a, 0:1],
                                           nw[:, 4, a:a + 1], ALU.subtract, ALU.mult)
                was_read(op, n, "wd", 0)

            def c_gain(n, j):
                if j == 1:
                    full(dve, n, "ct", j)
                else:
                    dve.wait_ge(cT_hi_done, 2 * (n + 1) + 1)
                dve.tensor_scalar(cT[:, j, :], bank_of(n, "ct", j), gains[:, 2 * j:2 * j + 1],
                                  gains[:, 2 * j + 1:2 * j + 2], ALU.mult, ALU.add).then_inc(cT_done, 1)

            def c_lo(n, j):
                dve.wait_ge(cT_done, 2 * (n + 1) + 2)
                dve.wait_ge(cT_hi_done, 2 * (n + 1) + j + 1)
                was_read(dve.tensor_tensor(cT_lo[:, j, :], cT[:, j, :], cT_hi[:, j, :].bitcast(F32),
                                           ALU.subtract), n, "ct", j)

            def v_copy(n, t):
                full(dve, n, "v", t)
                was_read(dve.tensor_copy(v[:, t, :], bank_of(n, "v", t)), n, "v", t)

            def k_copy(n, i):
                full(dve, n, "k", i)
                for j in (0, 1):
                    op = dve.tensor_copy(k_diag[j * DH:(j + 1) * DH, i, :, j, :],
                                         bank_of(n, "k", i)[j * DH:(j + 1) * DH, :].rearrange("p (t k) -> p t k", t=TILES))
                was_read(op, n, "k", i, 1)

            def add_out(n, t):
                dve.wait_ge(res_loaded[t], 16 * n)
                full(dve, n, "out", t)
                was_read(dve.tensor_tensor(res[:, t, :], res[:, t, :], bank_of(n, "out", t), ALU.add),
                         n, "out", t)

            def row_max(g, s):
                dve.wait_ge(scores_full, SLOTS * g + s + 1)
                dve.tensor_reduce(nmax[:, s % 4, :], ps_s[:, s % 2, :, :], AX.X, ALU.max,
                                  negate=True).then_inc(max_done, 1)

            def normalise_probs(g, s):
                dve.wait_ge(exp_done, SLOTS * g + s + 1)
                dve.reciprocal(inv[:, s % 4, :], total[:, s % 4, :]).then_inc(inv_done, 1)
                dve.wait_ge(inv_done, SLOTS * g + s + 1)
                dve.tensor_tensor(probs[:, s % 4, :, :], probs[:, s % 4, :, :],
                                  inv[:, s % 4, :].rearrange("p (h o) -> p h o", o=1).to_broadcast([P, HPC, P]),
                                  ALU.mult).then_inc(probs_done, 1)

            def o_lo(n, m):
                dve.wait_ge(oT_hi_done, DC * (n - (m >= 2)) + m + 1)
                dve.tensor_tensor(oT_lo[:, m, :], ps_o[:, m % 2, :], oT_hi[:, m, :].bitcast(F32),
                                  ALU.subtract).then_inc(oT_lo_done, 1)

            def read_work(n, uses, parts):
                for part, i in uses:
                    if has_part(n, part, i) and part in parts:
                        if part == "k":
                            k_copy(n, i)
                        elif part == "out":
                            add_out(n, i)
                        elif part == "h":
                            h_add(n, i)
                        elif part == "v" and i in V_ON_DVE:
                            v_copy(n, i)
                        elif part == "xt":
                            x_lo(n, i)
                        elif part == "wd":
                            c_moment(n, i)
                            if i == 1:
                                c_seed(n + 1)
                        elif part == "ct":
                            c_gain(n, 1 - i)

            def turn(n):
                ahead = has_part(n, "h", 0)
                for step in range(SLOTS):
                    if step in NORM_FIRST and has_slot(n, step - NORM_LAG):
                        normalise_probs(n, step - NORM_LAG)
                    if step > 0:
                        read_work(n, END.get(step - 1, ()), SOON)
                    elif not is_turn(n, -1):
                        read_work(n - 1, END[SLOTS - 1], SOON + LATER)
                    if has_slot(n, step):
                        row_max(n, step)
                    read_work(n, MIDWAY.get(step, ()), SOON + LATER)
                    read_work(n, END.get(step - 1, ()), LATER)
                    if ahead and step == C_NORM_AT:
                        c_norm(n)
                    if step not in NORM_FIRST and has_slot(n, step - NORM_LAG):
                        normalise_probs(n, step - NORM_LAG)
                    if step in O_LO_AT and has_slot(n, 0 if O_LO_AT[step] < 2 else -1):
                        o_lo(n, O_LO_AT[step])
                    if ahead:
                        if step == 0:
                            split_ar(n + 1)
                        if step in STATS_AT:
                            h_stat(n, 2 * STATS_AT.index(step))
                            h_stat(n, 2 * STATS_AT.index(step) + 1)
                        if step == STATS_AT[1]:
                            h_moment(n + 1)
                            h_seed(n + 1)
                        if step == NORM_AT:
                            normalise(n + 1)
                        if ("ct", 0) in END.get(step - 1, ()):
                            c_lo(n, 0)
                            c_lo(n, 1)

            dve.memset(ar[:, :, :].bitcast(F32), 0.0).then_inc(ar_zeroed, 1)
            dve.wait_ge(tok_loaded, 16)
            dve.tensor_scalar(tok_neg[:, :], tok_raw[:, :], 0, VOCAB, ALU.is_lt, ALU.mult).then_inc(tok_step, 1)
            dve.wait_ge(tok_step, 1)
            dve.tensor_tensor(tok_fix[:, :], tok_raw[:, :], tok_neg[:, :], ALU.add).then_inc(tok_step, 1)
            dve.wait_ge(tok_step, 2)
            dve.tensor_scalar(tok_fix[:, :], tok_fix[:, :], 0, VOCAB - 1, ALU.max, ALU.min).then_inc(tok_step, 2)
            dve.wait_ge(ar_zeroed, 1)
            dve.wait_ge(lora_loaded, 48)
            dve.tensor_copy(lora_hi[:, :], lora_raw[:, :]).then_inc(lora_split, 1)
            dve.wait_ge(lora_split, 1)
            dve.tensor_tensor(lora_lo[:, :], lora_raw[:, :], lora_hi[:, :].bitcast(F32),
                              ALU.subtract).then_inc(lora_split, 1)
            dve.wait_ge(ident_done, 2)
            dve.tensor_copy(ident_r[:, :], ident[:, :]).then_inc(ident_conv, 1)
            dve.tensor_copy(ident_b[:, :], ident[:, :]).then_inc(ident_conv, 1)
            dve.wait_ge(w_hi_done, 1)
            dve.tensor_tensor(w_lo[:, :], raw, w_hi[:, :].bitcast(F32),
                              ALU.subtract).then_inc(w_lo_done, 1)
            dve.wait_ge(w_lo_done, 1)
            dve.memset(k_diag[:, :, :, :, :], 0.0).then_inc(k_zeroed, 1)
            dve.wait_ge(k_zeroed, 1)
            turn(-1)
            turn(0)
            with dve.Fori(1, GROUPS - 1) as n:
                turn(n)
            turn(GROUPS - 1)
            turn(GROUPS)


LAT, HID, EXPERTS, TOP = 128, 256, 16, 8
HC = HID // P
ROUTE_SCALE = 2.5
TAKEN = -1e30

F_DOWN = 0
F_S1 = F_DOWN + DC * LAT
F_SG = F_S1 + DC * HID
F_S2 = F_SG + DC * HID
F_UP = F_S2 + HC * D
F_EXP = F_UP + D
E_COLS = 2 * HID + HC * LAT
W_FFN = F_EXP + EXPERTS * E_COLS
PIECE = 2048

V_XT, V_LOGITS, V_XL, V_LT, V_WT, V_OUT = 0, 4, 5, 6, 7, 8
TURN_USES = 12
FIRST_USES = 8
UNITS = 2 * EXPERTS
ALL_UNITS = UNITS + HC
Y_LAG = 2

F_STATS, F_MOMENTS, F_RSTD, F_XN, F_XT = (3, 6, 9, 12), 14, 15, (18, 19, 20, 21), (20, 23, 26, 29)


def ffn_phase(nc, h2, w_ffn, w_gate, biases, out):
    with ExitStack() as ctx:
        def sb(name, shape, dt):
            return ctx.enter_context(nc.sbuf_tensor(name, shape, dt))

        def pb(name, shape, dt):
            return ctx.enter_context(nc.psum_tensor(name, shape, dt))

        def sem(name):
            return ctx.enter_context(nc.semaphore(name))

        f_hi = sb("f_hi", [P, W_FFN], F32R)
        f_lo = sb("f_lo", [P, W_FFN], F32R)
        fident = sb("fident", [P, P], F32)
        pick = sb("pick", [2 * EXPERTS, EXPERTS], F32R)
        gate_raw = sb("gate_raw", [P, DC, EXPERTS], F32)
        gate = sb("gate", [P, DC, P], F32R)
        bias = sb("bias", [P, EXPERTS], F32)
        x = sb("x", [P, TILES, D], F32)
        res = sb("fres", [P, TILES, D], F32)
        stats = sb("fstats", [P, TILES, 6], F32)
        moments = sb("fmoments", [P, TILES, 2], F32)
        nw = sb("fnw", [P, 5, TILES], F32)
        shift = sb("shift", [P, TILES], F32)
        xT_hi = sb("fxT_hi", [P, DC, TOK], F32R)
        xT_lo = sb("fxT_lo", [P, DC, TOK], F32R)
        xl_hi = sb("xl_hi", [P, TOK], F32R)
        xl_lo = sb("xl_lo", [P, TOK], F32R)
        sh_hi = sb("sh_hi", [P, HC, TOK], F32R)
        sh_lo = sb("sh_lo", [P, HC, TOK], F32R)
        acc_hi = sb("acc_hi", [P, TOK], F32R)
        acc_lo = sb("acc_lo", [P, TOK], F32R)
        square = sb("square", [P, 2, TOK], F32)
        t = sb("t", [P, 2, TOK], F32)
        t_hi = sb("t_hi", [P, 2, TOK], F32R)
        t_lo = sb("t_lo", [P, 2, TOK], F32R)
        logits = sb("logits", [2 * EXPERTS, TOK], F32)
        route = sb("route", [P, 7, TILES, EXPERTS], F32)
        top = sb("top", [P, TILES, TOP], F32)
        wsum = sb("wsum", [P, 2, TILES], F32)
        w_parts = sb("w_parts", [P, TILES, 2 * EXPERTS], F32)
        wT = sb("wT", [2 * EXPERTS, TOK], F32R)

        ps_g = pb("ps_g", [P, 2, TOK], F32)
        ps_u = pb("ps_u", [P, 2, TOK], F32)
        ps_y = pb("ps_y", [P, TOK], F32)
        ps_w = pb("ps_w", [P, TOK], F32)
        work = pb("fwork", [P, 2, 512], F32)

        s_piece = [sem(f"piece{i}") for i in range(2)]
        piece_hi = sem("piece_hi")
        piece_lo = sem("piece_lo")
        small_loaded = sem("small_loaded")
        f_zeroed = sem("f_zeroed")
        f_ident = sem("f_ident")
        small_step = sem("small_step")
        x_loaded = sem("x_loaded")
        fres_loaded = sem("fres_loaded")
        work_full = [sem(f"fwork_full{b}") for b in range(2)]
        work_free = [sem(f"fwork_free{b}") for b in range(2)]
        x_stats = sem("x_stats")
        x_moments = sem("x_moments")
        newton = sem("fnewton")
        pool_passed = sem("fpool_passed")
        shift_done = sem("shift_done")
        x_done = sem("x_done")
        xT_hi_done = sem("fxT_hi_done")
        xl_hi_done = sem("xl_hi_done")
        lt_done = sem("lt_done")
        sig_done = sem("sig_done")
        route_step = sem("route_step")
        g_full = sem("g_full")
        u_full = sem("u_full")
        relu_done = sem("relu_done")
        square_done = sem("square_done")
        t1_done = sem("t1_done")
        t_done = sem("t_done")
        t_hi_done = sem("t_hi_done")
        t_lo_done = sem("t_lo_done")
        w_full = sem("w_full")
        y_done = sem("y_done")
        acc_hi_done = sem("acc_hi_done")
        acc_lo_done = sem("acc_lo_done")
        out_stored = sem("out_stored")
        dve_passed = sem("fdve_passed")
        sp_passed = sem("fsp_passed")
        pe_passed = sem("fpe_passed")

        ROUTE_OPS = 5 + 4 + 4 + 8

        block = ctx.enter_context(nc.Block())

        def full(engine, half, k):
            engine.wait_ge(work_full[k % 2], half + k // 2 + 1)

        def empty(engine, half, k):
            at_least(engine, work_free[k % 2], half + k // 2)

        def drained(engine, half, k):
            engine.wait_ge(work_free[k % 2], half + k // 2 + 1)

        def front_half(g):
            if isinstance(g, int) and g == 0:
                return 0
            return (TURN_USES // 2) * (g - 1) + FIRST_USES // 2

        def out_half(g):
            return (TURN_USES // 2) * g + FIRST_USES // 2

        def out_use(g):
            return 0 if isinstance(g, int) and g == GROUPS - 1 else V_OUT

        @block.sync
        def _(sp):
            sp.dma_start(gate_raw[:, :, :], w_gate).then_inc(small_loaded, 16)
            sp.dma_start(bias[:, :], biases).then_inc(small_loaded, 16)
            for i in range(W_FFN // PIECE):
                at_least(sp, piece_lo, i - 1)
                sp.dma_start((x if i % 2 else res)[:, :, :].rearrange("p t d -> p (t d)"),
                             w_ffn[:, i * PIECE:(i + 1) * PIECE]).then_inc(s_piece[i % 2], 16)
            sp.wait_ge(piece_lo, W_FFN // PIECE)

            def wait_drained(half, k):
                wait_alone(sp, work_free[k % 2], half + k // 2 + 1, sp_passed)

            def load_x(g, before):
                if before is not None:
                    wait_drained(front_half(before), V_XT + 2)
                    wait_drained(front_half(before), V_XT + 3)
                sp.dma_start(x[:, :, :], h2[bass.ds(g * TOK, TOK), :].rearrange(
                    "(t p) d -> p t d", p=P)).then_inc(x_loaded, 16)

            def load_res(g):
                wait_alone(sp, out_stored, 16 * TILES * g, sp_passed)
                sp.dma_start(res[:, :, :], h2[bass.ds(g * TOK, TOK), :].rearrange(
                    "(t p) d -> p t d", p=P)).then_inc(fres_loaded, 16)

            def store(g):
                for i in range(TILES):
                    wait_drained(out_half(g), out_use(g) + i)
                    sp.dma_start(out[bass.ds(g * TOK + i * P, P), :], res[:, i, :]).then_inc(out_stored, 16)

            load_x(0, None)
            load_res(0)
            load_x(1, 0)
            store(0)
            with sp.Fori(1, GROUPS - 1) as g:
                load_x(g + 1, g)
                load_res(g)
                store(g)
            load_res(GROUPS - 1)
            store(GROUPS - 1)
            sp.wait_ge(out_stored, 16 * TILES * GROUPS)

        @block.gpsimd
        def _(pool):
            pool.memset(fident[:, :], 0.0).then_inc(f_ident, 1)
            pool.wait_ge(f_ident, 1)
            pool.affine_select(out=fident[:, :], in_=fident[:, :], compare_op=ALU.not_equal, fill=1.0,
                               base=0, pattern=[[-1, P]], channel_multiplier=1).then_inc(f_ident, 1)

            def x_rstd(g):
                rsqrt_steps(pool, newton, NEWTON_OPS * g, nw[:, 1, :], nw[:, 3, :], nw[:, 4, :],
                            pool_passed)
                pool.wait_ge(newton, NEWTON_OPS * (g + 1))
                at_least(pool, x_done, TILES * g)
                shift_of(pool, shift_done, g, moments[:, :, 0], nw[:, 4, :], nw[:, 3, :], shift[:, :],
                         pool_passed)

            x_rstd(0)
            with pool.Fori(1, GROUPS) as g:
                x_rstd(g)

        @block.tensor
        def _(pe):
            def split_matmul(o, lhs, rhs, first, last):
                (a_hi, a_lo), (b_hi, b_lo) = lhs, rhs
                pe.matmul(o, a_hi, b_hi, start=first, stop=False)
                pe.matmul(o, a_hi, b_lo, start=False, stop=False)
                return pe.matmul(o, a_lo, b_hi, start=False, stop=last)

            def wts(col, n):
                return f_hi[:, col:col + n], f_lo[:, col:col + n]

            def xs(m):
                return xT_hi[:, m, :], xT_lo[:, m, :]

            def x_turn(g, half, i):
                pe.wait_ge(x_done, TILES * g + i + 1)
                empty(pe, half, V_XT + i)
                for m in range(DC):
                    mm = pe.transpose(work[:, i % 2, m * P:(m + 1) * P], x[:, i, m * P:(m + 1) * P],
                                      fident[:, :])
                mm.then_inc(work_full[i % 2], 1)

            def route_logits(g, half):
                drained(pe, half, V_XT + 2)
                drained(pe, half, V_XT + 3)
                empty(pe, half, V_LOGITS)
                for m in range(DC):
                    for part in (xT_hi, xT_lo):
                        mm = pe.matmul(work[:, V_LOGITS % 2, :], gate[:, m, :], part[:, m, :],
                                       start=(m == 0 and part is xT_hi), stop=(m == DC - 1 and part is xT_lo))
                mm.then_inc(work_full[V_LOGITS % 2], 1)

            def to_latent(g, half):
                empty(pe, half, V_XL)
                for m in range(DC):
                    mm = split_matmul(work[:, V_XL % 2, :], wts(F_DOWN + m * LAT, LAT), xs(m),
                                      m == 0, m == DC - 1)
                mm.then_inc(work_full[V_XL % 2], 1)

            def logits_turn(g, half):
                empty(pe, half, V_LT)
                wait_alone(pe, work_free[V_LOGITS % 2], half + V_LOGITS // 2 + 1, pe_passed)
                for i in range(TILES):
                    mm = pe.transpose(work[:, V_LT % 2, i * 2 * EXPERTS:(i + 1) * 2 * EXPERTS],
                                      logits[:, i * P:(i + 1) * P], fident[0:2 * EXPERTS, 0:2 * EXPERTS])
                mm.then_inc(work_full[V_LT % 2], 1)

            def weights_turn(g, half):
                k = V_WT
                pe.wait_ge(route_step, ROUTE_OPS * (g + 1))
                empty(pe, half, k)
                for i in range(TILES):
                    mm = pe.transpose(work[0:2 * EXPERTS, k % 2, i * P:(i + 1) * P], w_parts[:, i, :],
                                      fident[:, :])
                mm.then_inc(work_full[k % 2], 1)

            def shared(g, j):
                n = ALL_UNITS * g + j
                for bank, col, sem_free, sem_full in ((ps_g, F_SG, relu_done, g_full),
                                                      (ps_u, F_S1, t1_done, u_full)):
                    at_least(pe, sem_free, n - 1)
                    for m in range(DC):
                        mm = split_matmul(bank[:, j % 2, :], wts(col + m * HID + j * P, P), xs(m),
                                          m == 0, m == DC - 1)
                    mm.then_inc(sem_full, 1)

            def first_products(g, n):
                e, j = divmod(n, HC)
                b = (HC + n) % 2
                for bank, col, sem_free, sem_full in ((ps_g, HID, relu_done, g_full),
                                                      (ps_u, 0, t1_done, u_full)):
                    pe.wait_ge(sem_free, ALL_UNITS * g + HC + n - 1)
                    split_matmul(bank[:, b, :], wts(F_EXP + e * E_COLS + col + j * P, P),
                                 (xl_hi[:, :], xl_lo[:, :]), True, True).then_inc(sem_full, 1)

            def spread_weights(g, e):
                at_least(pe, t_done, UNITS * g + HC * e)
                pe.matmul(ps_w[:, :], pick[:, e:e + 1].to_broadcast([2 * EXPERTS, P]), wT[:, :],
                          start=True, stop=True).then_inc(w_full, 1)

            def second_product(g, n):
                e, j = divmod(n, HC)
                if n == 0:
                    at_least(pe, acc_lo_done, g)
                pe.wait_ge(t_lo_done, ALL_UNITS * g + HC + n + 1)
                b = n % 2
                split_matmul(ps_y[:, :], wts(F_EXP + e * E_COLS + 2 * HID + j * LAT, LAT),
                             (t_hi[:, b, :], t_lo[:, b, :]), n == 0, n == UNITS - 1).then_inc(y_done, 1)

            def output(g, half, i):
                k = out_use(g) + i
                empty(pe, half, k)
                if i == 0:
                    pe.wait_ge(acc_lo_done, g + 1)
                for j in range(HC):
                    split_matmul(work[:, k % 2, :],
                                 (sh_hi[:, j, i * P:(i + 1) * P], sh_lo[:, j, i * P:(i + 1) * P]),
                                 wts(F_S2 + j * D, D), j == 0, False)
                split_matmul(work[:, k % 2, :], (acc_hi[:, i * P:(i + 1) * P], acc_lo[:, i * P:(i + 1) * P]),
                             wts(F_UP, D), False, True).then_inc(work_full[k % 2], 1)

            def group(g, more):
                half = front_half(g + 1)
                for n in range(UNITS + Y_LAG):
                    if n < UNITS:
                        if n == 0:
                            drained(pe, front_half(g), V_XL)
                        if isinstance(g, int) and g == 0:
                            pe.wait_ge(piece_lo, piece_of(F_EXP + (n // HC + 1) * E_COLS))
                        first_products(g, n)
                    if n == 0:
                        drained(pe, front_half(g), V_WT)
                        spread_weights(g, 0)
                    if more:
                        if n in F_XT:
                            x_turn(g + 1, half, F_XT.index(n))
                        if n == UNITS:
                            route_logits(g + 1, half)
                        if n == UNITS + 1:
                            to_latent(g + 1, half)
                    if n >= Y_LAG:
                        second_product(g, n - Y_LAG)
                    if n % HC == 0 and 0 < n < UNITS:
                        spread_weights(g, n // HC)
                if more:
                    logits_turn(g + 1, half)
                    shared(g + 1, 0)
                    shared(g + 1, 1)
                    weights_turn(g + 1, half)
                for i in range(TILES):
                    output(g, out_half(g), i)

            def piece_of(col):
                return min(-(-col // PIECE), W_FFN // PIECE)

            pe.wait_ge(f_ident, 2)
            for i in range(TILES):
                x_turn(0, 0, i)
            pe.wait_ge(small_step, 4)
            route_logits(0, 0)
            to_latent(0, 0)
            logits_turn(0, 0)
            shared(0, 0)
            shared(0, 1)
            weights_turn(0, 0)
            group(0, True)
            with pe.Fori(1, GROUPS - 1) as g:
                group(g, True)
            group(GROUPS - 1, False)

        @block.scalar
        def _(act):
            def normalise(g, i):
                act.wait_ge(shift_done, 2 * (g + 1))
                act.activation(x[:, i, :], x[:, i, :], ACT.Identity, scale=nw[:, 4, i:i + 1],
                               bias=shift[:, i:i + 1]).then_inc(x_done, 1)

            def x_hi(g, half, i):
                full(act, half, V_XT + i)
                act.activation(xT_hi[:, :, i * P:(i + 1) * P],
                               work[:, i % 2, :].rearrange("p (m k) -> p m k", m=DC),
                               ACT.Copy).then_inc(xT_hi_done, 1)

            def logits_copy(g, half):
                full(act, half, V_LOGITS)
                act.activation(logits[:, :], work[0:2 * EXPERTS, V_LOGITS % 2, :],
                               ACT.Copy).then_inc(work_free[V_LOGITS % 2], 1)

            def latent_hi(g, half):
                full(act, half, V_XL)
                act.activation(xl_hi[:, :], work[:, V_XL % 2, :], ACT.Copy).then_inc(xl_hi_done, 1)

            def logits_back(g, half):
                full(act, half, V_LT)
                act.activation(w_parts[:, :, :],
                               work[:, V_LT % 2, 0:TILES * 2 * EXPERTS].rearrange("p (t e) -> p t e", t=TILES),
                               ACT.Copy).then_inc(work_free[V_LT % 2], 1)

            def sigmoid(g):
                act.wait_ge(route_step, ROUTE_OPS * g + 1)
                act.activation(route[:, 1, :, :], route[:, 0, :, :], ACT.Sigmoid).then_inc(sig_done, 1)

            def weights_copy(g, half):
                k = V_WT
                full(act, half, k)
                act.activation(wT[:, :], work[0:2 * EXPERTS, k % 2, :], ACT.Copy).then_inc(work_free[k % 2], 1)

            def squares(g, j):
                n = ALL_UNITS * g + j
                act.wait_ge(g_full, n + 1)
                at_least(act, t1_done, n - 1)
                act.activation(square[:, j % 2, :], ps_g[:, j % 2, :], ACT.Relu).then_inc(relu_done, 1)

            def squares_end(g, j):
                act.wait_ge(relu_done, ALL_UNITS * g + j + 1)
                act.activation(square[:, j % 2, :], square[:, j % 2, :], ACT.Square).then_inc(square_done, 1)

            def hidden_hi(g, j):
                n = ALL_UNITS * g + j
                if j < HC:
                    if not (isinstance(g, int) and g == 0):
                        full(act, out_half(g - 1), out_use(g - 1) + TILES - 1)
                    act.wait_ge(t1_done, n + 1)
                    dst = sh_hi[:, j, :]
                else:
                    act.wait_ge(t_done, UNITS * g + j - HC + 1)
                    at_least(act, y_done, UNITS * g + j - HC - 1)
                    dst = t_hi[:, j % 2, :]
                act.activation(dst, t[:, j % 2, :], ACT.Copy).then_inc(t_hi_done, 1)

            def sum_hi(g):
                act.wait_ge(y_done, UNITS * (g + 1))
                act.activation(acc_hi[:, :], ps_y[:, :], ACT.Copy).then_inc(acc_hi_done, 1)

            def group(g, more):
                half = front_half(g + 1)
                for n in range(UNITS):
                    squares(g, HC + n)
                    squares_end(g, HC + n)
                    hidden_hi(g, HC + n - 1)
                    if more and n in F_XN:
                        normalise(g + 1, F_XN.index(n))
                    if more and n in F_XT:
                        x_hi(g + 1, half, F_XT.index(n))
                hidden_hi(g, HC + UNITS - 1)
                if more:
                    logits_copy(g + 1, half)
                    latent_hi(g + 1, half)
                sum_hi(g)
                if more:
                    logits_back(g + 1, half)
                    sigmoid(g + 1)
                    squares(g + 1, 0)
                    squares_end(g + 1, 0)
                    squares(g + 1, 1)
                    squares_end(g + 1, 1)
                    weights_copy(g + 1, half)
                    hidden_hi(g + 1, 0)

            for i in range(W_FFN // PIECE):
                act.wait_ge(s_piece[i % 2], 16 * (i // 2 + 1))
                raw = (x if i % 2 else res)[:, :, :].rearrange("p t d -> p (t d)")
                act.activation(f_hi[:, i * PIECE:(i + 1) * PIECE], raw, ACT.Copy).then_inc(piece_hi, 1)
            for i in range(TILES):
                normalise(0, i)
            for i in range(TILES):
                x_hi(0, 0, i)
            logits_copy(0, 0)
            latent_hi(0, 0)
            logits_back(0, 0)
            sigmoid(0)
            squares(0, 0)
            squares_end(0, 0)
            squares(0, 1)
            squares_end(0, 1)
            weights_copy(0, 0)
            hidden_hi(0, 0)
            group(0, True)
            with act.Fori(1, GROUPS - 1) as g:
                group(g, True)
            group(GROUPS - 1, False)

        @block.vector
        def _(dve):
            def x_moments_of(g, part):
                if part < TILES:
                    dve.wait_ge(x_loaded, 16 * (g + 1))
                    dve.bn_stats(stats[:, part, :], x[:, part, :]).then_inc(x_stats, 1)
                else:
                    for i in range(TILES):
                        wait_alone(dve, x_stats, TILES * g + i + 1, dve_passed)
                        dve.bn_aggr(moments[:, i, :], stats[:, i, :]).then_inc(x_moments, 1)

            def x_rstd(g):
                dve.wait_ge(x_moments, TILES * (g + 1))
                at_least(dve, newton, NEWTON_OPS * g)
                rsqrt_seed(dve, newton, NEWTON_OPS * g, moments[:, :, 1], nw[:, 0, :], nw[:, 1, :],
                           nw[:, 2, :].bitcast(I32), nw[:, 4, :])

            def x_lo(g, half, i):
                dve.wait_ge(xT_hi_done, TILES * g + i + 1)
                dve.tensor_tensor(xT_lo[:, :, i * P:(i + 1) * P],
                                  work[:, i % 2, :].rearrange("p (m k) -> p m k", m=DC),
                                  xT_hi[:, :, i * P:(i + 1) * P].bitcast(F32),
                                  ALU.subtract).then_inc(work_free[i % 2], 1)

            def latent_lo(g, half):
                dve.wait_ge(xl_hi_done, g + 1)
                dve.tensor_tensor(xl_lo[:, :], work[:, V_XL % 2, :], xl_hi[:, :].bitcast(F32),
                                  ALU.subtract).then_inc(work_free[V_XL % 2], 1)

            def routing(g, half):
                base = ROUTE_OPS * g
                count = [0]

                def did(op):
                    op.then_inc(route_step, 1)
                    count[0] += 1

                def done(n):
                    dve.wait_ge(route_step, base + n)

                r = [route[:, i, :, :] for i in range(7)]
                drained(dve, half, V_LT)
                did(dve.tensor_tensor(r[0], w_parts[:, :, 0:EXPERTS], w_parts[:, :, EXPERTS:], ALU.add))
                dve.wait_ge(sig_done, g + 1)
                did(dve.tensor_tensor(r[2], r[1], bias[:, :].rearrange("p (o e) -> p o e", o=1)
                                      .to_broadcast([P, TILES, EXPERTS]), ALU.add))
                for i in range(TILES):
                    wait_alone(dve, route_step, base + 2, dve_passed)
                    did(dve.max(top[:, i, :], route[:, 2, i, :]))
                for i in range(TILES):
                    wait_alone(dve, route_step, base + 3 + i, dve_passed)
                    did(dve.match_replace(route[:, 3, i, :], top[:, i, :], route[:, 2, i, :], TAKEN))
                done(10)
                did(dve.tensor_tensor(r[4], r[3], r[2], ALU.not_equal))
                done(11)
                did(dve.tensor_tensor(r[5], r[4], r[1], ALU.mult))
                done(12)
                did(dve.tensor_reduce(wsum[:, 0, :], r[5], AX.X, ALU.add))
                done(13)
                did(dve.reciprocal(wsum[:, 1, :], wsum[:, 0, :]))
                done(14)
                did(dve.scalar_tensor_tensor(out=r[6], in0=r[5], scalar=ROUTE_SCALE,
                                             in1=wsum[:, 1, :].rearrange("p (t o) -> p t o", o=1)
                                             .to_broadcast([P, TILES, EXPERTS]),
                                             op0=ALU.mult, op1=ALU.mult))
                done(15)
                did(dve.tensor_copy(r[4].bitcast(F32R), r[6]))
                done(16)
                did(dve.tensor_copy(w_parts[:, :, 0:EXPERTS], r[4]))
                dve.tensor_tensor(w_parts[:, :, EXPERTS:], r[6], r[4],
                                  ALU.subtract).then_inc(route_step, ROUTE_OPS - count[0])

            def linear(g, j):
                n = ALL_UNITS * g + j
                dve.wait_ge(square_done, n + 1)
                dve.wait_ge(u_full, n + 1)
                at_least(dve, t_lo_done, n - 1)
                dve.tensor_tensor(t[:, j % 2, :], ps_u[:, j % 2, :], square[:, j % 2, :],
                                  ALU.mult).then_inc(t1_done, 1)

            def weigh(g, j):
                dve.wait_ge(t1_done, ALL_UNITS * g + j + 1)
                dve.wait_ge(w_full, EXPERTS * g + (j - HC) // HC + 1)
                dve.tensor_tensor(t[:, j % 2, :], t[:, j % 2, :], ps_w[:, :], ALU.mult).then_inc(t_done, 1)

            def hidden_lo(g, j):
                dve.wait_ge(t_hi_done, ALL_UNITS * g + j + 1)
                lo, hi = (sh_lo[:, j, :], sh_hi[:, j, :]) if j < HC else (t_lo[:, j % 2, :], t_hi[:, j % 2, :])
                dve.tensor_tensor(lo, t[:, j % 2, :], hi.bitcast(F32), ALU.subtract).then_inc(t_lo_done, 1)

            def sum_lo(g):
                dve.wait_ge(acc_hi_done, g + 1)
                dve.tensor_tensor(acc_lo[:, :], ps_y[:, :], acc_hi[:, :].bitcast(F32),
                                  ALU.subtract).then_inc(acc_lo_done, 1)

            def add_out(g, i):
                k = out_use(g) + i
                full(dve, out_half(g), k)
                if i == 0:
                    dve.wait_ge(fres_loaded, 16 * (g + 1))
                dve.tensor_tensor(res[:, i, :], res[:, i, :], work[:, k % 2, :],
                                  ALU.add).then_inc(work_free[k % 2], 1)

            def group(g, more):
                half = front_half(g + 1)
                for n in range(UNITS):
                    linear(g, HC + n)
                    hidden_lo(g, HC + n - 1)
                    weigh(g, HC + n)
                    if more:
                        if n in F_STATS:
                            x_moments_of(g + 1, F_STATS.index(n))
                        if n == F_MOMENTS:
                            x_moments_of(g + 1, TILES)
                        if n == F_RSTD:
                            x_rstd(g + 1)
                        if n in F_XT:
                            x_lo(g + 1, half, F_XT.index(n))
                hidden_lo(g, HC + UNITS - 1)
                if more:
                    latent_lo(g + 1, half)
                sum_lo(g)
                if more:
                    routing(g + 1, half)
                    linear(g + 1, 0)
                    linear(g + 1, 1)
                for i in range(TILES):
                    add_out(g, i)
                if more:
                    hidden_lo(g + 1, 0)

            dve.memset(gate[:, :, :].bitcast(F32), 0.0).then_inc(f_zeroed, 1)
            dve.wait_ge(f_zeroed, 1)
            dve.wait_ge(small_loaded, 32)
            dve.tensor_copy(gate[:, :, 0:EXPERTS], gate_raw[:, :, :]).then_inc(small_step, 1)
            dve.wait_ge(small_step, 1)
            dve.tensor_tensor(gate[:, :, EXPERTS:2 * EXPERTS], gate_raw[:, :, :],
                              gate[:, :, 0:EXPERTS].bitcast(F32), ALU.subtract).then_inc(small_step, 1)
            dve.wait_ge(f_ident, 2)
            dve.tensor_tensor(pick[:, :], fident[0:2 * EXPERTS, 0:EXPERTS],
                              fident[0:2 * EXPERTS, EXPERTS:2 * EXPERTS], ALU.add).then_inc(small_step, 2)
            for i in range(W_FFN // PIECE):
                dve.wait_ge(piece_hi, i + 1)
                raw = (x if i % 2 else res)[:, :, :].rearrange("p t d -> p (t d)")
                cols = slice(i * PIECE, (i + 1) * PIECE)
                dve.tensor_tensor(f_lo[:, cols], raw, f_hi[:, cols].bitcast(F32),
                                  ALU.subtract).then_inc(piece_lo, 1)
            for part in range(TILES + 1):
                x_moments_of(0, part)
            x_rstd(0)
            for i in range(TILES):
                x_lo(0, 0, i)
            latent_lo(0, 0)
            routing(0, 0)
            linear(0, 0)
            linear(0, 1)
            hidden_lo(0, 0)
            group(0, True)
            with dve.Fori(1, GROUPS - 1) as g:
                group(g, True)
            group(GROUPS - 1, False)


_F = "L0_ffn_"
_A = "L0_attn_"


def _chunks(w):
    return w.reshape(w.shape[0] // P, P, w.shape[1]).transpose(1, 0, 2).reshape(P, -1)


def build(nc, table, tok, lora_b, w_attn, ln, w_ffn, w_gate, biases, out):
    h2 = nc.dram_tensor("h2", [GROUPS * TOK, D], F32, kind="Internal").ap()
    attention_phase(nc, table, tok, lora_b, w_attn, ln, h2)
    ffn_phase(nc, h2, w_ffn, w_gate, biases, out)


def kernel(**inputs):
    import numpy as np
    import concourse.bacc as bacc
    from concourse.bass_utils import run_bass_kernel_spmd

    a = {k: np.asarray(v) for k, v in inputs.items()}
    expert = []
    for e in range(EXPERTS):
        expert += [a[_F + "rw1"][e].T, a[_F + "rwg"][e].T, _chunks(a[_F + "rw2"][e].T)]
    laid_out = {
        "table": np.concatenate([a["L0_tok_base_weight"], a["L0_tok_lora_A"].T], 1),
        "tok": a["x"].T,
        "lora_b": a["L0_tok_lora_B"].T,
        "w_attn": np.concatenate([
            _chunks(np.concatenate([a[_A + "W_dq"], a[_A + "W_dkv"]], 1)),
            a[_A + "W_uq"], a[_A + "W_ukv"], _chunks(a[_A + "W_o"].T)], 1),
        "ln": np.stack([a[_A + "q_ln_g"], a[_A + "q_ln_b"], a[_A + "kv_ln_g"], a[_A + "kv_ln_b"]], 1),
        "w_ffn": np.concatenate([
            _chunks(a[_F + "Wdown"].T), _chunks(a[_F + "sw1"].T), _chunks(a[_F + "swg"].T),
            _chunks(a[_F + "sw2"].T), a[_F + "Wup"].T] + expert, 1),
        "w_gate": _chunks(a[_F + "Wg"].T).reshape(P, DC, EXPERTS),
        "biases": np.broadcast_to(a[_F + "biases"], (P, EXPERTS)),
    }
    nc = bacc.Bacc("TRN2", target_bir_lowering=False, num_devices=1)
    arrays, args = {}, []
    for name, array in laid_out.items():
        array = np.ascontiguousarray(array)
        arrays["in_" + name] = array
        args.append(nc.dram_tensor("in_" + name, array.shape, mybir.dt.from_np(array.dtype),
                                   kind="ExternalInput").ap())
    out = nc.dram_tensor("out_0", (SEQS * P, D), F32, kind="ExternalOutput").ap()
    build(nc, *args, out)
    r = run_bass_kernel_spmd(nc, [arrays], core_ids=[0])
    return r.results[0]["out_0"].reshape(SEQS, P, D)
```

```python
import concourse.bass as bass
from concourse import mybir
from contextlib import ExitStack

F32 = mybir.dt.float32
F32R = mybir.dt.float32r
BF16 = mybir.dt.bfloat16
I32 = mybir.dt.int32
ALU = mybir.AluOpType
ACT = mybir.ActivationFunctionType
AX = mybir.AxisListType

P = 128
D = 512
DC = D // P
VOCAB, RANK = 32000, 16
HEADS = 16
DH = D // HEADS
HPC = P // DH
SEQS = 64
TILES = 4
TOK = TILES * P
GROUPS = SEQS // TILES
EPS = 1e-5
RSQRT_MAGIC = 0x5F3759DF
NEWTON_OPS = 4 + 3 * 4
MASKED = -1e30

W_DQKV = 0
W_UQ = W_DQKV + DC * 256
W_UK = W_UQ + D
W_UV = W_UK + D
W_O = W_UV + D
W_ATTN = W_O + DC * D
W_PIECES = (slice(0, W_UQ), slice(W_UQ, W_O), slice(W_O, W_ATTN))


def at_least(engine, semaphore, value):
    if not (isinstance(value, int) and value <= 0):
        engine.wait_ge(semaphore, value)


def wait_alone(engine, semaphore, value, passed):
    if not (isinstance(value, int) and value <= 0):
        engine.wait_ge(semaphore, value)
        engine.sem_inc(passed, 1)


def rsqrt_seed(dve, step, base, var, v, nhalf, bits, y):
    dve.tensor_scalar(v, var, EPS, None, ALU.add).then_inc(step, 1)
    dve.tensor_scalar(nhalf, var, EPS, -0.5, ALU.add, ALU.mult).then_inc(step, 1)
    dve.wait_ge(step, base + 1)
    dve.tensor_scalar(bits, v.bitcast(I32), 1, None, ALU.logical_shift_right).then_inc(step, 1)
    dve.wait_ge(step, base + 3)
    dve.tensor_scalar(y.bitcast(I32), bits, -1, RSQRT_MAGIC, ALU.mult, ALU.add).then_inc(step, 1)


def rsqrt_steps(pool, step, base, nhalf, t, y, passed, steps=range(3)):
    for k in steps:
        pool.wait_ge(step, base + 4 + 4 * k)
        pool.tensor_tensor(t, nhalf, y, ALU.mult).then_inc(step, 1)
        pool.wait_ge(step, base + 5 + 4 * k)
        pool.tensor_tensor(t, t, y, ALU.mult).then_inc(step, 1)
        wait_alone(pool, step, base + 6 + 4 * k, passed)
        pool.tensor_scalar(t, t, 1.5, None, ALU.add).then_inc(step, 1)
        pool.wait_ge(step, base + 7 + 4 * k)
        pool.tensor_tensor(y, y, t, ALU.mult).then_inc(step, 1)


def shift_of(pool, done, count, mean, y, t, shift, passed):
    pool.tensor_tensor(t, mean, y, ALU.mult).then_inc(done, 1)
    wait_alone(pool, done, 2 * count + 1, passed)
    pool.tensor_scalar(shift, t, -1.0, None, ALU.mult).then_inc(done, 1)


SLOTS = TILES * DC
INV_LAG, NORM_LAG, T_LAG, PV_LAG = 1, 1, 2, 4

MIDWAY = {1: (("art", 1), ("h", 0), ("h", 1)), 2: (("h", 2), ("v", 0)), 3: (("h", 3), ("q", 2)),
          4: (("v", 2),), 5: (("v", 3),), 7: (("out", 0), ("xt", 3)), 8: (("out", 1),),
          9: (("out", 2),), 14: (("k", 0),)}
END = {0: (("k", 1), ("art", 0)), 1: (("q", 1),), 2: (("v", 1),), 3: (("k", 2),),
       5: (("xt", 0), ("xt", 1)), 6: (("xt", 2),), 7: (("wd", 0), ("wd", 1)),
       9: (("q", 3), ("k", 3)), 10: (("out", 3),), 11: (("ct", 0), ("ct", 1)), 15: (("q", 0),)}
FRONT = ("art", "h", "xt", "wd", "ct")
STATS_AT, NORM_AT, C_NORM_AT = (2, 3), 5, 10
O_HI_AT = {11: 0, 14: 1, 0: 2, 4: 3}
O_LO_AT = {11: 0, 15: 1, 1: 2, 4: 3}
GATHER_AT, RSTD_AT, C_RSTD_AT = 5, 4, 9
INVERT_FIRST = (2, 4, 5, 7, 8, 9, 10, 11, 12, 14, 15)
ON_DVE = (("art", 1), ("q", 0), ("v", 1), ("v", 3))
K_ON_DVE = (2, 3, 1, 2)
SOON, LATER = ("k", "h", "ct", "v", "q", "art", "xt", "wd"), ("out",)
DRAINS = 2


def is_turn(n, which):
    return isinstance(n, int) and n == which


def has_part(n, part, i):
    if part == "out":
        return not (is_turn(n, -1) or is_turn(n, 0))
    if part in FRONT or (part in "qk" and i == 0):
        return not (is_turn(n, GROUPS - 1) or is_turn(n, GROUPS))
    return not (is_turn(n, -1) or is_turn(n, GROUPS))


def uses_of(n):
    return [use for step in range(SLOTS) for use in MIDWAY.get(step, ()) + END.get(step, ())
            if has_part(n, *use)]


def place(n, part, i):
    k = uses_of(n).index((part, i))
    start, first = len(uses_of(-1)), len(uses_of(0))
    each = len(uses_of(1))
    if is_turn(n, -1):
        before = 0
    elif is_turn(n, 0):
        before = start // 2
    elif is_turn(n, GROUPS):
        before = (start + first + each * (GROUPS - 2) + len(uses_of(GROUPS - 1))) // 2
    else:
        before = (each // 2) * n + (start + first - each) // 2
    return k % 2, before + k // 2


def attention_phase(nc, table, tok, lora_b, w_attn, ln, h2):
    with ExitStack() as ctx:
        def sb(name, shape, dt):
            return ctx.enter_context(nc.sbuf_tensor(name, shape, dt))

        def pb(name, shape, dt):
            return ctx.enter_context(nc.psum_tensor(name, shape, dt))

        def sem(name):
            return ctx.enter_context(nc.semaphore(name))

        ident = sb("ident", [P, P], F32)
        ident_r = sb("ident_r", [P, P], F32R)
        ident_b = sb("ident_b", [P, P], BF16)
        mask = sb("mask", [P, HPC, P], BF16)
        gains = sb("gains", [P, 4], F32)
        w_hi = sb("w_hi", [P, W_ATTN], F32R)
        w_lo = sb("w_lo", [P, W_ATTN], F32R)
        lora_raw = sb("lora_raw", [3 * RANK, D], F32)
        lora_hi = sb("lora_hi", [3 * RANK, D], F32R)
        lora_lo = sb("lora_lo", [3 * RANK, D], F32R)
        tok_raw = sb("tok_raw", [P, SEQS], I32)
        tok_neg = sb("tok_neg", [P, SEQS], I32)
        tok_fix = sb("tok_fix", [P, SEQS], I32)
        tok_now = sb("tok_now", [P, TILES], I32)
        gath = sb("gath", [P, TILES, D + RANK], F32)
        ar = sb("ar", [P, TILES, P], F32R)
        arT = sb("arT", [3 * RANK, TOK], F32R)
        h = sb("h", [P, TILES, D], F32)
        res_next = sb("res_next", [P, TILES, D], F32)
        res = sb("res", [P, TILES, D], F32)
        stats = sb("stats", [P, TILES, 6], F32)
        moments = sb("moments", [P, TILES, 2], F32)
        cstats = sb("cstats", [P, 2 * TILES, 6], F32)
        cmoments = sb("cmoments", [P, 2 * TILES, 2], F32)
        nw = sb("nw", [P, 5, 2 * TILES], F32)
        xn = sb("xn", [P, TILES, D], F32)
        xT_hi = sb("xT_hi", [P, DC, TOK], F32R)
        xT_lo = sb("xT_lo", [P, DC, TOK], F32R)
        c = sb("c", [P, TILES, 256], F32)
        cT = sb("cT", [P, 2, TOK], F32)
        cT_hi = sb("cT_hi", [P, 2, TOK], F32R)
        cT_lo = sb("cT_lo", [P, 2, TOK], F32R)
        qT = sb("qT", [P, DC, TOK], F32)
        k_diag = sb("k_diag", [P, DC, TILES, HPC, P], F32)
        raw = k_diag[:, :, :, :, :].rearrange("p a b c d -> p (a b c d)")[:, 0:W_ATTN]
        v = sb("v", [P, TILES, D], F32)
        probs = sb("probs", [P, 4, HPC, P], F32)
        nmax = sb("nmax", [P, 4, HPC], F32)
        total = sb("total", [P, 4, HPC], F32)
        inv = sb("inv", [P, 4, HPC], F32)
        pT = sb("pT", [P, 2, HPC * P], F32)
        oT_hi = sb("oT_hi", [P, DC, TOK], F32R)
        oT_lo = sb("oT_lo", [P, DC, TOK], F32R)

        ps_s = pb("ps_s", [P, 2, HPC, P], F32)
        ps_t = pb("ps_t", [P, 2, HPC * P], F32)
        ps_o = pb("ps_o", [P, 2, TOK], F32)
        work = pb("work", [P, 2, 512], F32)

        loaded = sem("loaded")
        w_loaded = [sem(f"w_loaded{i}") for i in range(len(W_PIECES))]
        lora_loaded = sem("lora_loaded")
        tok_loaded = sem("tok_loaded")
        consts = sem("consts")
        ident_done = sem("ident_done")
        ident_conv = sem("ident_conv")
        w_hi_done = sem("w_hi_done")
        w_lo_done = sem("w_lo_done")
        k_zeroed = sem("k_zeroed")
        lora_split = sem("lora_split")
        lora_placed = sem("lora_placed")
        tok_step = sem("tok_step")
        tok_picked = sem("tok_picked")
        gathered = [sem(f"gathered{t}") for t in range(TILES)]
        ar_zeroed = sem("ar_zeroed")
        ar_split = sem("ar_split")
        work_full = [sem(f"work_full{b}") for b in range(2)]
        work_free = [sem(f"work_free{b}") for b in range(2)]
        h_stats = sem("h_stats")
        h_moments = sem("h_moments")
        newton = sem("newton")
        xn_done = sem("xn_done")
        xT_hi_done = sem("xT_hi_done")
        c_stats = sem("c_stats")
        c_moments = sem("c_moments")
        cT_hi_done = sem("cT_hi_done")
        c_done = sem("c_done")
        cT_done = sem("cT_done")
        scores_full = sem("scores_full")
        max_done = sem("max_done")
        exp_done = sem("exp_done")
        inv_done = sem("inv_done")
        probs_done = sem("probs_done")
        pT_full = sem("pT_full")
        pT_done = sem("pT_done")
        o_full = sem("o_full")
        oT_hi_done = sem("oT_hi_done")
        oT_lo_done = sem("oT_lo_done")
        res_kept = [sem(f"res_kept{t}") for t in range(TILES)]
        res_loaded = [sem(f"res_loaded{t}") for t in range(TILES)]
        stored = [sem(f"stored{t}") for t in range(TILES)]
        dve_passed = sem("dve_passed")
        pool_passed = sem("pool_passed")
        sp_passed = sem("sp_passed")

        block = ctx.enter_context(nc.Block())

        def full(engine, n, part, i):
            bank, before = place(n, part, i)
            engine.wait_ge(work_full[bank], before + 1)

        def empty(engine, n, part, i):
            bank, before = place(n, part, i)
            at_least(engine, work_free[bank], DRAINS * before)

        def drained(engine, n, part, i):
            bank, before = place(n, part, i)
            engine.wait_ge(work_free[bank], DRAINS * (before + 1))

        def bank_of(n, part, i):
            return work[:, place(n, part, i)[0], :]

        def was_read(instruction, n, part, i, drains=DRAINS):
            instruction.then_inc(work_free[place(n, part, i)[0]], drains)

        def slots_of(n):
            return range(0 if is_turn(n, -1) or is_turn(n, GROUPS) else SLOTS)

        def has_slot(n, slot):
            if slot < 0:
                return not (is_turn(n, -1) or is_turn(n, 0))
            return slot in slots_of(n)

        @block.sync
        def _(sp):
            sp.dma_start(tok_raw[:, :], tok).then_inc(tok_loaded, 16)
            for r in range(3):
                sp.dma_start(lora_raw[r * RANK:(r + 1) * RANK, :], lora_b).then_inc(lora_loaded, 16)
            sp.dma_start(gains[:, :], ln).then_inc(loaded, 16)
            for i, cols in enumerate(W_PIECES):
                sp.dma_start(raw[:, cols], w_attn[:, cols]).then_inc(w_loaded[i], 16)
            sp.wait_ge(lora_split, 2)
            sp.dma_start(lora_hi[RANK:2 * RANK, :].bitcast(F32),
                         lora_lo[RANK:2 * RANK, :].bitcast(F32)).then_inc(lora_placed, 16)

            def turn(n):
                if has_part(n, "out", 0):
                    for t in range(TILES):
                        bank, before = place(n, "out", t)
                        wait_alone(sp, work_free[bank], DRAINS * (before + 1), sp_passed)
                        sp.dma_start(h2[bass.ds((n - 1) * TOK + t * P, P), :],
                                     res[:, t, :]).then_inc(stored[t], 16)
                if slots_of(n):
                    for t in range(TILES):
                        wait_alone(sp, stored[t], 16 * n, sp_passed)
                        wait_alone(sp, res_kept[t], 16 * (n + 1), sp_passed)
                        sp.dma_start(res[:, t, :], res_next[:, t, :]).then_inc(res_loaded[t], 16)
                if has_part(n, "h", 0):
                    for t in range(TILES):
                        bank, before = place(n, "h", t)
                        wait_alone(sp, work_free[bank], DRAINS * (before + 1), sp_passed)
                        wait_alone(sp, res_loaded[t], 16 * (n + 1), sp_passed)
                        sp.dma_start(res_next[:, t, :], h[:, t, :]).then_inc(res_kept[t], 16)

            turn(-1)
            turn(0)
            with sp.Fori(1, GROUPS - 1) as n:
                turn(n)
            turn(GROUPS - 1)
            turn(GROUPS)
            for t in range(TILES):
                sp.wait_ge(stored[t], 16 * GROUPS)

        @block.gpsimd
        def _(pool):
            pool.memset(ident[:, :], 0.0).then_inc(consts, 1)
            pool.memset(mask[:, :, :], 0.0).then_inc(consts, 1)
            pool.wait_ge(consts, 2)
            pool.affine_select(out=ident[:, :], in_=ident[:, :], compare_op=ALU.not_equal, fill=1.0,
                               base=0, pattern=[[-1, P]], channel_multiplier=1).then_inc(ident_done, 1)
            pool.affine_select(out=mask[:, :, :], in_=mask[:, :, :], compare_op=ALU.is_ge, fill=MASKED,
                               base=0, pattern=[[0, HPC], [-1, P]],
                               channel_multiplier=1).then_inc(ident_done, 1)
            pool.wait_ge(tok_step, 4)

            def gather(g):
                pool.tensor_copy(tok_now[:, :], tok_fix[:, bass.ds(g * TILES, TILES)]).then_inc(tok_picked, 1)
                wait_alone(pool, tok_picked, g + 1, pool_passed)
                for t in range(TILES):
                    pool.indirect_dma_start(
                        out=gath[:, t, :], out_offset=None, in_=table,
                        in_offset=bass.IndirectOffsetOnAxis(ap=tok_now[:, t:t + 1], axis=0),
                    ).then_inc(gathered[t], 16)

            def wait_gathered(g):
                for t in range(TILES):
                    pool.wait_ge(gathered[t], 16 * (g + 1))

            def newton_of(base, n):
                rsqrt_steps(pool, newton, base, nw[:, 1, 0:n], nw[:, 3, 0:n], nw[:, 4, 0:n],
                            pool_passed)

            def normalise_probs(n, s):
                pool.wait_ge(inv_done, SLOTS * n + s + 1)
                pool.tensor_tensor(probs[:, s % 4, :, :], probs[:, s % 4, :, :],
                                   inv[:, s % 4, :].rearrange("p (h o) -> p h o", o=1).to_broadcast([P, HPC, P]),
                                   ALU.mult).then_inc(probs_done, 1)

            def turn(n):
                ahead = has_part(n, "h", 0)
                for step in range(SLOTS):
                    if has_slot(n, step - NORM_LAG):
                        normalise_probs(n, step - NORM_LAG)
                    if step == GATHER_AT and ahead and not is_turn(n, GROUPS - 2):
                        wait_gathered(n + 1)
                        drained(pool, n, "h", TILES - 1)
                        gather(n + 2)
                        if is_turn(n, -1):
                            pool.wait_ge(w_lo_done, len(W_PIECES))
                            pool.memset(k_diag[:, :, :, :, :], 0.0).then_inc(k_zeroed, 1)
                    if step == RSTD_AT and ahead:
                        newton_of(2 * NEWTON_OPS * (n + 1), TILES)
                    if step == C_RSTD_AT and ahead:
                        newton_of(2 * NEWTON_OPS * (n + 1) + NEWTON_OPS, 2 * TILES)

            gather(0)
            turn(-1)
            turn(0)
            with pool.Fori(1, GROUPS - 2) as n:
                turn(n)
            for n in range(GROUPS - 2, GROUPS + 1):
                turn(n)

        @block.tensor
        def _(pe):
            def split_matmul(out, lhs, rhs, first, last):
                (a_hi, a_lo), (b_hi, b_lo) = lhs, rhs
                pe.matmul(out, a_hi, b_hi, start=first, stop=False)
                pe.matmul(out, a_hi, b_lo, start=False, stop=False)
                return pe.matmul(out, a_lo, b_hi, start=False, stop=last)

            def wts(col, n):
                return w_hi[:, col:col + n], w_lo[:, col:col + n]

            def pair(hi, lo, i, lo_, hi_):
                return hi[:, i, lo_:hi_], lo[:, i, lo_:hi_]

            def ar_turn(n, j):
                if j == 0:
                    pe.wait_ge(ar_split, 3 * (n + 2))
                bank = bank_of(n, "art", j)
                for t in (2 * j, 2 * j + 1):
                    mm = pe.transpose(bank[:, (t % 2) * P:(t % 2 + 1) * P].bitcast(F32R),
                                      ar[:, t, :], ident_r[:, :])
                return mm

            def embed(n, t):
                if t % 2 == 0:
                    drained(pe, n, "art", t // 2)
                return pe.matmul(bank_of(n, "h", t), arT[:, t * P:(t + 1) * P], lora_hi[:, :],
                                 start=True, stop=True)

            def x_turn(n, t):
                pe.wait_ge(xn_done, TILES * (n + 1) + t + 1)
                bank = bank_of(n, "xt", t)
                for m in range(DC):
                    mm = pe.transpose(bank[:, m * P:(m + 1) * P], xn[:, t, m * P:(m + 1) * P],
                                      ident[:, :])
                return mm

            def down(n, j):
                bank = bank_of(n, "wd", j)
                for t in (2 * j, 2 * j + 1):
                    drained(pe, n, "xt", t)
                    for m in range(DC):
                        mm = split_matmul(bank[:, (t % 2) * 256:(t % 2 + 1) * 256],
                                          pair(xT_hi, xT_lo, m, t * P, (t + 1) * P),
                                          wts(W_DQKV + m * 256, 256), m == 0, m == DC - 1)
                return mm

            def c_turn(n, j):
                pe.wait_ge(c_done, n + 2)
                bank = bank_of(n, "ct", j)
                for t in range(TILES):
                    mm = pe.transpose(bank[:, t * P:(t + 1) * P], c[:, t, j * P:(j + 1) * P],
                                      ident[:, :])
                return mm

            def up(n, part, i):
                if i == 0 and part != "v":
                    drained(pe, n, "ct", int(part == "k"))
                if part == "v":
                    a, b = pair(cT_hi, cT_lo, 1, i * P, (i + 1) * P), wts(W_UV, D)
                else:
                    a = wts((W_UQ if part == "q" else W_UK) + i * P, P)
                    b = pair(cT_hi, cT_lo, int(part == "k"), 0, TOK)
                return split_matmul(bank_of(n, part, i), a, b, True, True)

            def out_proj(n, t):
                pe.wait_ge(oT_lo_done, DC * n)
                for m in range(DC):
                    mm = split_matmul(bank_of(n, "out", t), pair(oT_hi, oT_lo, m, t * P, (t + 1) * P),
                                      wts(W_O + m * D, D), m == 0, m == DC - 1)
                return mm

            def scores(n, s):
                m, t = divmod(s, TILES)
                if t == 0:
                    drained(pe, n - (m == 0), "q", m)
                    drained(pe, n - (m == 0), "k", m)
                at_least(pe, exp_done, SLOTS * n + s - 1)
                pe.matmul(ps_s[:, s % 2, :, :], ident_b[:, :], mask[:, :, :], start=True, stop=False,
                          skip_group_check=True)
                pe.matmul(ps_s[:, s % 2, :, :], qT[:, m, t * P:(t + 1) * P], k_diag[:, m, t, :, :],
                          start=False, stop=True, skip_group_check=True).then_inc(scores_full, 1)

            def probs_turn(n, s):
                pe.wait_ge(probs_done, SLOTS * n + s + 1)
                at_least(pe, pT_done, SLOTS * n + s - 1)
                for j in range(HPC):
                    mm = pe.transpose(ps_t[:, s % 2, j * P:(j + 1) * P], probs[:, s % 4, j, :], ident[:, :])
                mm.then_inc(pT_full, 1)

            def heads_out(n, s):
                m, t = divmod(s, TILES)
                if m == 0:
                    drained(pe, n, "v", t)
                if t == 0:
                    at_least(pe, oT_lo_done, DC * n + m - 1)
                pe.wait_ge(pT_done, SLOTS * n + s + 1)
                for j in range(HPC):
                    f = (m % DC) * P + j * DH
                    mm = pe.matmul(ps_o[j * DH:(j + 1) * DH, m % 2, t * P:(t + 1) * P],
                                   v[:, t, f:f + DH], pT[:, s % 2, j * P:(j + 1) * P],
                                   start=True, stop=True)
                mm.then_inc(o_full, 1)

            def work_on(n, uses):
                for part, i in uses:
                    if has_part(n, part, i):
                        empty(pe, n, part, i)
                        if part == "art":
                            mm = ar_turn(n, i)
                        elif part == "h":
                            mm = embed(n, i)
                        elif part == "xt":
                            mm = x_turn(n, i)
                        elif part == "wd":
                            mm = down(n, i)
                        elif part == "ct":
                            mm = c_turn(n, i)
                        elif part == "out":
                            mm = out_proj(n, i)
                        else:
                            mm = up(n, part, i)
                        mm.then_inc(work_full[place(n, part, i)[0]], 1)

            def turn(n):
                for step in range(SLOTS):
                    if step > 0 and has_slot(n, step):
                        scores(n, step)
                    work_on(n, MIDWAY.get(step, ()))
                    if has_slot(n, step - T_LAG):
                        probs_turn(n, step - T_LAG)
                    if has_slot(n, step - PV_LAG):
                        heads_out(n, step - PV_LAG)
                    if step == 0 and has_slot(n, 0):
                        scores(n, 0)
                    work_on(n, END.get(step, ()))

            pe.wait_ge(ident_conv, 2)
            pe.wait_ge(lora_placed, 16)
            pe.wait_ge(w_lo_done, len(W_PIECES))
            turn(-1)
            turn(0)
            with pe.Fori(1, GROUPS - 1) as n:
                turn(n)
            turn(GROUPS - 1)
            turn(GROUPS)

        @block.scalar
        def _(act):
            def ar_copy(n, j):
                was_read(act.activation(arT[:, 2 * j * P:(2 * j + 2) * P],
                                        bank_of(n, "art", j)[0:3 * RANK, 0:2 * P], ACT.Copy), n, "art", j)

            def x_hi(n, t):
                act.activation(xT_hi[:, :, t * P:(t + 1) * P],
                               bank_of(n, "xt", t).rearrange("p (m k) -> p m k", m=DC),
                               ACT.Copy).then_inc(xT_hi_done, 1)

            def c_hi(n, j):
                if j == 0:
                    full(act, n, "ct", j)
                else:
                    act.wait_ge(cT_done, 2 * (n + 1) + 1)
                act.activation(cT_hi[:, j, :], bank_of(n, "ct", j), ACT.Identity,
                               scale=gains[:, 2 * j:2 * j + 1],
                               bias=gains[:, 2 * j + 1:2 * j + 2]).then_inc(cT_hi_done, 1)

            def c_copy(n, j):
                was_read(act.activation(c[:, 2 * j:2 * j + 2, :].rearrange("p t k -> p (t k)"),
                                        bank_of(n, "wd", j), ACT.Copy), n, "wd", j)

            def q_copy(n, i):
                was_read(act.activation(qT[:, i, :], bank_of(n, "q", i), ACT.Copy, scale=DH ** -0.5),
                         n, "q", i)

            def k_copy(n, i):
                if is_turn(n, -1):
                    act.wait_ge(k_zeroed, 1)
                for j in range(K_ON_DVE[i], HPC):
                    op = act.activation(k_diag[j * DH:(j + 1) * DH, i, :, j, :],
                                        bank_of(n, "k", i)[j * DH:(j + 1) * DH, :].rearrange("p (t k) -> p t k", t=TILES),
                                        ACT.Copy)
                was_read(op, n, "k", i, 1)

            def v_copy(n, t):
                was_read(act.activation(v[:, t, :], bank_of(n, "v", t), ACT.Copy), n, "v", t)

            def exps(n, s):
                act.wait_ge(max_done, SLOTS * n + s + 1)
                at_least(act, pT_full, SLOTS * n + s - 3)
                for j in range(HPC):
                    e = act.activation(probs[:, s % 4, j, :], ps_s[:, s % 2, j, :], ACT.Exp,
                                       bias=nmax[:, s % 4, j:j + 1], accum_out=total[:, s % 4, j:j + 1])
                e.then_inc(exp_done, 1)

            def pT_copy(n, s):
                act.wait_ge(pT_full, SLOTS * n + s + 1)
                at_least(act, o_full, SLOTS * n + s - 1)
                act.activation(pT[:, s % 2, :], ps_t[:, s % 2, :], ACT.Copy).then_inc(pT_done, 1)

            def o_hi(n, m):
                if m == 0 and has_part(n, "out", TILES - 1):
                    full(act, n, "out", TILES - 1)
                act.wait_ge(o_full, SLOTS * (n - (m >= 2)) + TILES * (m + 1))
                act.activation(oT_hi[:, m, :], ps_o[:, m % 2, :], ACT.Copy).then_inc(oT_hi_done, 1)

            def read_work(n, uses):
                for part, i in uses:
                    if part == "ct" and has_part(n, part, i):
                        c_hi(n, i)
                    elif (has_part(n, part, i) and part in ("art", "xt", "wd", "q", "k", "v")
                          and (part, i) not in ON_DVE):
                        full(act, n, part, i)
                        if part == "art":
                            ar_copy(n, i)
                        elif part == "xt":
                            x_hi(n, i)
                        elif part == "wd":
                            c_copy(n, i)
                        elif part == "q":
                            q_copy(n, i)
                        elif part == "k":
                            k_copy(n, i)
                        else:
                            v_copy(n, i)

            def turn(n):
                if not is_turn(n, -1):
                    read_work(n - 1, END[SLOTS - 1])
                for step in range(SLOTS):
                    if step > 0:
                        read_work(n, END.get(step - 1, ()))
                    if step in O_HI_AT and has_slot(n, 0 if O_HI_AT[step] < 2 else -1):
                        o_hi(n, O_HI_AT[step])
                    if has_slot(n, step):
                        exps(n, step)
                    read_work(n, MIDWAY.get(step, ()))
                    if has_slot(n, step - T_LAG):
                        pT_copy(n, step - T_LAG)

            for i, cols in enumerate(W_PIECES):
                act.wait_ge(w_loaded[i], 16)
                act.activation(w_hi[:, cols], raw[:, cols], ACT.Copy).then_inc(w_hi_done, 1)
            act.wait_ge(loaded, 16)
            turn(-1)
            turn(0)
            with act.Fori(1, GROUPS - 1) as n:
                turn(n)
            turn(GROUPS - 1)
            turn(GROUPS)

        @block.vector
        def _(dve):
            def split_ar(g):
                for t in range(TILES):
                    dve.wait_ge(gathered[t], 16 * (g + 1))
                dve.tensor_copy(ar[:, :, 0:RANK], gath[:, :, D:D + RANK]).then_inc(ar_split, 1)
                dve.tensor_copy(ar[:, :, RANK:2 * RANK], gath[:, :, D:D + RANK]).then_inc(ar_split, 1)
                dve.wait_ge(ar_split, 3 * g + 1)
                dve.tensor_tensor(ar[:, :, 2 * RANK:3 * RANK], gath[:, :, D:D + RANK],
                                  ar[:, :, 0:RANK].bitcast(F32), ALU.subtract).then_inc(ar_split, 1)

            def h_add(n, t):
                full(dve, n, "h", t)
                at_least(dve, res_kept[t], 16 * (n + 1))
                was_read(dve.tensor_tensor(h[:, t, :], gath[:, t, 0:D], bank_of(n, "h", t), ALU.add),
                         n, "h", t)

            def h_stat(n, t):
                drained(dve, n, "h", t)
                dve.bn_stats(stats[:, t, :], h[:, t, :]).then_inc(h_stats, 1)

            def h_moment(g):
                for t in range(TILES):
                    wait_alone(dve, h_stats, TILES * g + t + 1, dve_passed)
                    dve.bn_aggr(moments[:, t, :], stats[:, t, :]).then_inc(h_moments, 1)

            def seed_of(base, var, n):
                rsqrt_seed(dve, newton, base, var, nw[:, 0, 0:n], nw[:, 1, 0:n],
                           nw[:, 2, 0:n].bitcast(I32), nw[:, 4, 0:n])

            def h_seed(g):
                dve.wait_ge(h_moments, TILES * (g + 1))
                seed_of(2 * NEWTON_OPS * g, moments[:, :, 1], TILES)

            def c_seed(g):
                dve.wait_ge(c_moments, 2 * TILES * (g + 1))
                seed_of(2 * NEWTON_OPS * g + NEWTON_OPS, cmoments[:, :, 1], 2 * TILES)

            def normalise(g):
                dve.wait_ge(newton, 2 * NEWTON_OPS * g + NEWTON_OPS)
                for t in range(TILES):
                    dve.tensor_scalar(xn[:, t, :], h[:, t, :], moments[:, t, 0:1], nw[:, 4, t:t + 1],
                                      ALU.subtract, ALU.mult).then_inc(xn_done, 1)

            def x_lo(n, t):
                dve.wait_ge(xT_hi_done, TILES * (n + 1) + t + 1)
                was_read(dve.tensor_tensor(xT_lo[:, :, t * P:(t + 1) * P],
                                           bank_of(n, "xt", t).rearrange("p (m k) -> p m k", m=DC),
                                           xT_hi[:, :, t * P:(t + 1) * P].bitcast(F32),
                                           ALU.subtract), n, "xt", t)

            def c_moment(n, j):
                drained(dve, n, "wd", j)
                for i in range(4):
                    dve.bn_stats(cstats[:, 4 * j + i, :],
                                 c[:, 2 * j + i // 2, (i % 2) * P:(i % 2 + 1) * P]).then_inc(c_stats, 1)
                for i in range(4):
                    wait_alone(dve, c_stats, 8 * (n + 1) + 4 * j + i + 1, dve_passed)
                    dve.bn_aggr(cmoments[:, 4 * j + i, :], cstats[:, 4 * j + i, :]).then_inc(c_moments, 1)

            def c_norm(n):
                dve.wait_ge(newton, 2 * NEWTON_OPS * (n + 2))
                for a in range(2 * TILES):
                    part = c[:, a // 2, (a % 2) * P:(a % 2 + 1) * P]
                    op = dve.tensor_scalar(part, part, cmoments[:, a, 0:1], nw[:, 4, a:a + 1],
                                           ALU.subtract, ALU.mult)
                op.then_inc(c_done, 1)

            def c_gain(n, j):
                if j == 1:
                    full(dve, n, "ct", j)
                else:
                    dve.wait_ge(cT_hi_done, 2 * (n + 1) + 1)
                dve.tensor_scalar(cT[:, j, :], bank_of(n, "ct", j), gains[:, 2 * j:2 * j + 1],
                                  gains[:, 2 * j + 1:2 * j + 2], ALU.mult, ALU.add).then_inc(cT_done, 1)

            def c_lo(n, j):
                dve.wait_ge(cT_done, 2 * (n + 1) + 2)
                dve.wait_ge(cT_hi_done, 2 * (n + 1) + j + 1)
                was_read(dve.tensor_tensor(cT_lo[:, j, :], cT[:, j, :], cT_hi[:, j, :].bitcast(F32),
                                           ALU.subtract), n, "ct", j)

            def v_copy(n, t):
                was_read(dve.tensor_copy(v[:, t, :], bank_of(n, "v", t)), n, "v", t)

            def q_copy(n, i):
                was_read(dve.tensor_scalar(qT[:, i, :], bank_of(n, "q", i), DH ** -0.5, None, ALU.mult),
                         n, "q", i)

            def ar_copy(n, j):
                was_read(dve.tensor_copy(arT[:, 2 * j * P:(2 * j + 2) * P],
                                         bank_of(n, "art", j)[0:3 * RANK, 0:2 * P]), n, "art", j)

            def k_copy(n, i):
                full(dve, n, "k", i)
                if is_turn(n, -1):
                    dve.wait_ge(k_zeroed, 1)
                for j in range(K_ON_DVE[i]):
                    op = dve.tensor_copy(k_diag[j * DH:(j + 1) * DH, i, :, j, :],
                                         bank_of(n, "k", i)[j * DH:(j + 1) * DH, :].rearrange("p (t k) -> p t k", t=TILES))
                was_read(op, n, "k", i, 1)

            def add_out(n, t):
                dve.wait_ge(res_loaded[t], 16 * n)
                full(dve, n, "out", t)
                was_read(dve.tensor_tensor(res[:, t, :], res[:, t, :], bank_of(n, "out", t), ALU.add),
                         n, "out", t)

            def row_max(g, s):
                dve.wait_ge(scores_full, SLOTS * g + s + 1)
                dve.tensor_reduce(nmax[:, s % 4, :], ps_s[:, s % 2, :, :], AX.X, ALU.max,
                                  negate=True).then_inc(max_done, 1)

            def invert_total(n, s):
                dve.wait_ge(exp_done, SLOTS * n + s + 1)
                dve.reciprocal(inv[:, s % 4, :], total[:, s % 4, :]).then_inc(inv_done, 1)

            def o_lo(n, m):
                dve.wait_ge(oT_hi_done, DC * (n - (m >= 2)) + m + 1)
                dve.tensor_tensor(oT_lo[:, m, :], ps_o[:, m % 2, :], oT_hi[:, m, :].bitcast(F32),
                                  ALU.subtract).then_inc(oT_lo_done, 1)

            def read_work(n, uses, parts):
                for part, i in uses:
                    if has_part(n, part, i) and part in parts:
                        if part == "k":
                            k_copy(n, i)
                        elif part == "out":
                            add_out(n, i)
                        elif part == "h":
                            h_add(n, i)
                        elif (part, i) in ON_DVE:
                            full(dve, n, part, i)
                            if part == "v":
                                v_copy(n, i)
                            elif part == "q":
                                q_copy(n, i)
                            else:
                                ar_copy(n, i)
                        elif part == "xt":
                            x_lo(n, i)
                        elif part == "wd":
                            c_moment(n, i)
                            if i == 1:
                                c_seed(n + 1)
                        elif part == "ct":
                            c_gain(n, 1 - i)

            def turn(n):
                ahead = has_part(n, "h", 0)
                for step in range(SLOTS):
                    if step in INVERT_FIRST and has_slot(n, step - INV_LAG):
                        invert_total(n, step - INV_LAG)
                    if step > 0:
                        read_work(n, END.get(step - 1, ()), SOON)
                    elif not is_turn(n, -1):
                        read_work(n - 1, END[SLOTS - 1], SOON + LATER)
                    if has_slot(n, step):
                        row_max(n, step)
                    read_work(n, MIDWAY.get(step, ()), SOON + LATER)
                    read_work(n, END.get(step - 1, ()), LATER)
                    if ahead and step == C_NORM_AT:
                        c_norm(n)
                    if step not in INVERT_FIRST and has_slot(n, step - INV_LAG):
                        invert_total(n, step - INV_LAG)
                    if step in O_LO_AT and has_slot(n, 0 if O_LO_AT[step] < 2 else -1):
                        o_lo(n, O_LO_AT[step])
                    if ahead:
                        if step == 0:
                            split_ar(n + 1)
                        if step in STATS_AT:
                            h_stat(n, 2 * STATS_AT.index(step))
                            h_stat(n, 2 * STATS_AT.index(step) + 1)
                        if step == STATS_AT[1]:
                            h_moment(n + 1)
                            h_seed(n + 1)
                        if step == NORM_AT:
                            normalise(n + 1)
                        if ("ct", 0) in END.get(step - 1, ()):
                            c_lo(n, 0)
                            c_lo(n, 1)

            dve.memset(ar[:, :, :].bitcast(F32), 0.0).then_inc(ar_zeroed, 1)
            dve.wait_ge(tok_loaded, 16)
            dve.tensor_scalar(tok_neg[:, :], tok_raw[:, :], 0, VOCAB, ALU.is_lt, ALU.mult).then_inc(tok_step, 1)
            dve.wait_ge(tok_step, 1)
            dve.tensor_tensor(tok_fix[:, :], tok_raw[:, :], tok_neg[:, :], ALU.add).then_inc(tok_step, 1)
            dve.wait_ge(tok_step, 2)
            dve.tensor_scalar(tok_fix[:, :], tok_fix[:, :], 0, VOCAB - 1, ALU.max, ALU.min).then_inc(tok_step, 2)
            dve.wait_ge(ar_zeroed, 1)
            dve.wait_ge(lora_loaded, 48)
            dve.tensor_copy(lora_hi[:, :], lora_raw[:, :]).then_inc(lora_split, 1)
            dve.wait_ge(lora_split, 1)
            dve.tensor_tensor(lora_lo[:, :], lora_raw[:, :], lora_hi[:, :].bitcast(F32),
                              ALU.subtract).then_inc(lora_split, 1)
            dve.wait_ge(ident_done, 2)
            dve.tensor_copy(ident_r[:, :], ident[:, :]).then_inc(ident_conv, 1)
            dve.tensor_copy(ident_b[:, :], ident[:, :]).then_inc(ident_conv, 1)
            for i, cols in enumerate(W_PIECES):
                dve.wait_ge(w_hi_done, i + 1)
                dve.tensor_tensor(w_lo[:, cols], raw[:, cols], w_hi[:, cols].bitcast(F32),
                                  ALU.subtract).then_inc(w_lo_done, 1)
            dve.wait_ge(loaded, 16)
            turn(-1)
            turn(0)
            with dve.Fori(1, GROUPS - 1) as n:
                turn(n)
            turn(GROUPS - 1)
            turn(GROUPS)


LAT, HID, EXPERTS, TOP = 128, 256, 16, 8
HC = HID // P
ROUTE_SCALE = 2.5
TAKEN = -1e30

F_DOWN = 0
F_S1 = F_DOWN + DC * LAT
F_SG = F_S1 + DC * HID
F_S2 = F_SG + DC * HID
F_UP = F_S2 + HC * D
F_EXP = F_UP + D
E_COLS = 2 * HID + HC * LAT
W_FFN = F_EXP + EXPERTS * E_COLS
PIECE = 1024
PIECES = W_FFN // PIECE
EARLY_PIECES = PIECES // 2

V_XT, V_LOGITS, V_XL, V_LT, V_WT, V_OUT = 0, 4, 5, 6, 7, 8
TURN_USES = 12
FIRST_USES = 8
UNITS = 2 * EXPERTS
ALL_UNITS = UNITS + HC
Y_LAG = 3

F_STATS, F_MOMENTS, F_SEED, F_RSTD, F_SHIFT, F_XN, F_XT = (
    (3, 5, 7, 9), 10, 11, (12, 13, 14), 15, (17, 18, 19, 20), (20, 23, 26, 29))
F_SPLIT = range(2, 2 + 2 * (PIECES - EARLY_PIECES), 2)


def ffn_phase(nc, h2, w_ffn, w_gate, biases, w_rows, out):
    with ExitStack() as ctx:
        def sb(name, shape, dt):
            return ctx.enter_context(nc.sbuf_tensor(name, shape, dt))

        def pb(name, shape, dt):
            return ctx.enter_context(nc.psum_tensor(name, shape, dt))

        def sem(name):
            return ctx.enter_context(nc.semaphore(name))

        f_hi = sb("f_hi", [P, W_FFN], F32R)
        f_lo = sb("f_lo", [P, W_FFN], F32R)
        fident = sb("fident", [P, P], F32)
        gate_raw = sb("gate_raw", [P, DC, EXPERTS], F32)
        gate = sb("gate", [P, DC, P], F32R)
        bias = sb("bias", [P, EXPERTS], F32)
        x = sb("x", [P, TILES, D], F32)
        res = sb("fres", [P, TILES, D], F32)
        stats = sb("fstats", [P, TILES, 6], F32)
        moments = sb("fmoments", [P, TILES, 2], F32)
        nw = sb("fnw", [P, 5, TILES], F32)
        shift = sb("shift", [P, TILES], F32)
        xT_hi = sb("fxT_hi", [P, DC, TOK], F32R)
        xT_lo = sb("fxT_lo", [P, DC, TOK], F32R)
        xl_hi = sb("xl_hi", [P, TOK], F32R)
        xl_lo = sb("xl_lo", [P, TOK], F32R)
        sh_hi = sb("sh_hi", [P, HC, TOK], F32R)
        sh_lo = sb("sh_lo", [P, HC, TOK], F32R)
        square = sb("square", [P, 2, TOK], F32)
        t = sb("t", [P, 2, TOK], F32)
        t_hi = sb("t_hi", [P, 2, TOK], F32R)
        t_lo = sb("t_lo", [P, 2, TOK], F32R)
        acc_hi, acc_lo = t_hi[:, 0, :], t_lo[:, 0, :]
        logits = sb("logits", [2 * EXPERTS, TOK], F32)
        route = sb("route", [P, 6, TILES, EXPERTS], F32)
        top = sb("top", [P, TILES, TOP], F32)
        wsum = sb("wsum", [P, 2, TILES], F32)
        weights = sb("weights", [P, TILES, 2 * EXPERTS], F32)
        wT = sb("wT", [EXPERTS, TOK], F32)
        w_all = sb("w_all", [P, 2, TOK], F32)

        ps_g = pb("ps_g", [P, 2, TOK], F32)
        ps_u = pb("ps_u", [P, 2, TOK], F32)
        ps_y = pb("ps_y", [P, TOK], F32)
        work = pb("fwork", [P, 2, 512], F32)

        s_piece = [sem(f"piece{i}") for i in range(PIECES)]
        piece_hi = sem("piece_hi")
        piece_lo = sem("piece_lo")
        small_loaded = sem("small_loaded")
        f_zeroed = sem("f_zeroed")
        f_ident = sem("f_ident")
        small_step = sem("small_step")
        x_loaded = sem("x_loaded")
        fres_loaded = sem("fres_loaded")
        work_full = [sem(f"fwork_full{b}") for b in range(2)]
        work_free = [sem(f"fwork_free{b}") for b in range(2)]
        x_stats = sem("x_stats")
        x_moments = sem("x_moments")
        newton = sem("fnewton")
        pool_passed = sem("fpool_passed")
        shift_done = sem("shift_done")
        x_done = sem("x_done")
        xT_hi_done = sem("fxT_hi_done")
        xl_hi_done = sem("xl_hi_done")
        lt_done = sem("lt_done")
        sig_done = sem("sig_done")
        route_step = sem("route_step")
        g_full = sem("g_full")
        u_full = sem("u_full")
        relu_done = sem("relu_done")
        square_done = sem("square_done")
        t1_done = sem("t1_done")
        t_done = sem("t_done")
        t_hi_done = sem("t_hi_done")
        t_lo_done = sem("t_lo_done")
        rows_stored = sem("rows_stored")
        w_spread = [sem(f"w_spread{b}") for b in range(2)]
        y_done = sem("y_done")
        acc_hi_done = sem("acc_hi_done")
        acc_lo_done = sem("acc_lo_done")
        out_stored = sem("out_stored")
        dve_passed = sem("fdve_passed")
        sp_passed = sem("fsp_passed")
        pe_passed = sem("fpe_passed")

        ROUTE_OPS = 2 + 2 * TILES + 5

        block = ctx.enter_context(nc.Block())

        def piece(weights, i):
            return weights[:, i * PIECE:(i + 1) * PIECE]

        def staged(i):
            if i in (2, 3):
                return (square, t)[i - 2][:, :, :].rearrange("p b k -> p (b k)")
            return res[:, :, :].rearrange("p t d -> p (t d)")[:, (i % 2) * PIECE:(i % 2 + 1) * PIECE]

        def full(engine, half, k):
            engine.wait_ge(work_full[k % 2], half + k // 2 + 1)

        def empty(engine, half, k):
            at_least(engine, work_free[k % 2], half + k // 2)

        def drained(engine, half, k):
            engine.wait_ge(work_free[k % 2], half + k // 2 + 1)

        def front_half(g):
            if isinstance(g, int) and g == 0:
                return 0
            return (TURN_USES // 2) * (g - 1) + FIRST_USES // 2

        def out_half(g):
            return (TURN_USES // 2) * g + FIRST_USES // 2

        def out_use(g):
            return 0 if isinstance(g, int) and g == GROUPS - 1 else V_OUT

        @block.sync
        def _(sp):
            sp.dma_start(gate_raw[:, :, :], w_gate).then_inc(small_loaded, 16)
            sp.dma_start(bias[:, :], biases).then_inc(small_loaded, 16)
            def wait_drained(half, k):
                wait_alone(sp, work_free[k % 2], half + k // 2 + 1, sp_passed)

            def load_x(g, before):
                if before is not None:
                    wait_drained(front_half(before), V_XT + 2)
                    wait_drained(front_half(before), V_XT + 3)
                sp.dma_start(x[:, :, :], h2[bass.ds(g * TOK, TOK), :].rearrange(
                    "(t p) d -> p t d", p=P)).then_inc(x_loaded, 16)

            def load_res(g):
                wait_alone(sp, out_stored, 16 * TILES * g, sp_passed)
                sp.dma_start(res[:, :, :], h2[bass.ds(g * TOK, TOK), :].rearrange(
                    "(t p) d -> p t d", p=P)).then_inc(fres_loaded, 16)

            def store(g):
                for i in range(TILES):
                    wait_drained(out_half(g), out_use(g) + i)
                    sp.dma_start(out[bass.ds(g * TOK + i * P, P), :], res[:, i, :]).then_inc(out_stored, 16)

            def load_piece(i):
                if i >= 4:
                    sp.wait_ge(piece_lo, 1 + (i - 4 if i < 6 else i - 2))
                sp.dma_start(staged(i), piece(w_ffn, i)).then_inc(s_piece[i], 16)

            def store_rows(g):
                wait_drained(front_half(g), V_WT)
                sp.dma_start(w_rows[bass.ds(g * EXPERTS, EXPERTS), :], wT[:, :]).then_inc(rows_stored, 16)

            def spread(g, e):
                if e == 0:
                    wait_alone(sp, rows_stored, 16 * (g + 1), sp_passed)
                wait_alone(sp, t_done, UNITS * g + HC * (e - 1), sp_passed)
                sp.dma_start(w_all[:, e % 2, :], w_rows[bass.ds(g * EXPERTS + e, 1), :].to_broadcast(
                    [P, TOK])).then_inc(w_spread[e % 2], 16)

            load_x(0, None)
            for i in range(EARLY_PIECES + 2):
                load_piece(i)
            store_rows(0)
            spread(0, 0)
            spread(0, 1)

            def group(g, more):
                if more:
                    load_x(g + 1, g)
                first = isinstance(g, int) and g == 0
                if not first:
                    load_res(g)
                for e in range(2, EXPERTS):
                    spread(g, e)
                    if first and EARLY_PIECES + e < PIECES:
                        load_piece(EARLY_PIECES + e)
                if first:
                    sp.wait_ge(piece_lo, PIECES)
                    load_res(g)
                if more:
                    store_rows(g + 1)
                    spread(g + 1, 0)
                    spread(g + 1, 1)
                store(g)

            group(0, True)
            with sp.Fori(1, GROUPS - 1) as g:
                group(g, True)
            group(GROUPS - 1, False)
            sp.wait_ge(out_stored, 16 * TILES * GROUPS)

        @block.gpsimd
        def _(pool):
            pool.memset(fident[:, :], 0.0).then_inc(f_ident, 1)
            pool.wait_ge(f_ident, 1)
            pool.affine_select(out=fident[:, :], in_=fident[:, :], compare_op=ALU.not_equal, fill=1.0,
                               base=0, pattern=[[-1, P]], channel_multiplier=1).then_inc(f_ident, 1)

            def hidden_lo(g, j):
                pool.wait_ge(t_hi_done, ALL_UNITS * g + j + 1)
                lo, hi = (sh_lo[:, j, :], sh_hi[:, j, :]) if j < HC else (t_lo[:, j % 2, :], t_hi[:, j % 2, :])
                pool.tensor_tensor(lo, t[:, j % 2, :], hi.bitcast(F32), ALU.subtract).then_inc(t_lo_done, 1)

            def group(g):
                for j in range(ALL_UNITS):
                    hidden_lo(g, j)

            group(0)
            with pool.Fori(1, GROUPS) as g:
                group(g)

        @block.tensor
        def _(pe):
            def split_matmul(o, lhs, rhs, first, last):
                (a_hi, a_lo), (b_hi, b_lo) = lhs, rhs
                pe.matmul(o, a_hi, b_hi, start=first, stop=False)
                pe.matmul(o, a_hi, b_lo, start=False, stop=False)
                return pe.matmul(o, a_lo, b_hi, start=False, stop=last)

            def wts(col, n):
                return f_hi[:, col:col + n], f_lo[:, col:col + n]

            def xs(m):
                return xT_hi[:, m, :], xT_lo[:, m, :]

            def x_turn(g, half, i):
                pe.wait_ge(x_done, TILES * g + i + 1)
                empty(pe, half, V_XT + i)
                for m in range(DC):
                    mm = pe.transpose(work[:, i % 2, m * P:(m + 1) * P], x[:, i, m * P:(m + 1) * P],
                                      fident[:, :])
                mm.then_inc(work_full[i % 2], 1)

            def route_logits(g, half):
                drained(pe, half, V_XT + 2)
                drained(pe, half, V_XT + 3)
                empty(pe, half, V_LOGITS)
                for m in range(DC):
                    for part in (xT_hi, xT_lo):
                        mm = pe.matmul(work[:, V_LOGITS % 2, :], gate[:, m, :], part[:, m, :],
                                       start=(m == 0 and part is xT_hi), stop=(m == DC - 1 and part is xT_lo))
                mm.then_inc(work_full[V_LOGITS % 2], 1)

            def to_latent(g, half):
                empty(pe, half, V_XL)
                for m in range(DC):
                    mm = split_matmul(work[:, V_XL % 2, :], wts(F_DOWN + m * LAT, LAT), xs(m),
                                      m == 0, m == DC - 1)
                mm.then_inc(work_full[V_XL % 2], 1)

            def logits_turn(g, half):
                empty(pe, half, V_LT)
                wait_alone(pe, work_free[V_LOGITS % 2], half + V_LOGITS // 2 + 1, pe_passed)
                for i in range(TILES):
                    mm = pe.transpose(work[:, V_LT % 2, i * 2 * EXPERTS:(i + 1) * 2 * EXPERTS],
                                      logits[:, i * P:(i + 1) * P], fident[0:2 * EXPERTS, 0:2 * EXPERTS])
                mm.then_inc(work_full[V_LT % 2], 1)

            def weights_turn(g, half):
                k = V_WT
                pe.wait_ge(route_step, ROUTE_OPS * (g + 1))
                empty(pe, half, k)
                for i in range(TILES):
                    mm = pe.transpose(work[0:2 * EXPERTS, k % 2, i * P:(i + 1) * P], weights[:, i, :],
                                      fident[:, :])
                mm.then_inc(work_full[k % 2], 1)

            def shared(g, j):
                n = ALL_UNITS * g + j
                for bank, col, sem_free, sem_full in ((ps_g, F_SG, relu_done, g_full),
                                                      (ps_u, F_S1, t1_done, u_full)):
                    at_least(pe, sem_free, n - 1)
                    for m in range(DC):
                        mm = split_matmul(bank[:, j % 2, :], wts(col + m * HID + j * P, P), xs(m),
                                          m == 0, m == DC - 1)
                    mm.then_inc(sem_full, 1)

            def first_products(g, n):
                e, j = divmod(n, HC)
                b = (HC + n) % 2
                for bank, col, sem_free, sem_full in ((ps_g, HID, relu_done, g_full),
                                                      (ps_u, 0, t1_done, u_full)):
                    pe.wait_ge(sem_free, ALL_UNITS * g + HC + n - 1)
                    split_matmul(bank[:, b, :], wts(F_EXP + e * E_COLS + col + j * P, P),
                                 (xl_hi[:, :], xl_lo[:, :]), True, True).then_inc(sem_full, 1)

            def second_product(g, n):
                e, j = divmod(n, HC)
                if n == 0:
                    at_least(pe, acc_lo_done, g)
                pe.wait_ge(t_lo_done, ALL_UNITS * g + HC + n + 1)
                b = n % 2
                split_matmul(ps_y[:, :], wts(F_EXP + e * E_COLS + 2 * HID + j * LAT, LAT),
                             (t_hi[:, b, :], t_lo[:, b, :]), n == 0, n == UNITS - 1).then_inc(y_done, 1)

            def output(g, half, i):
                k = out_use(g) + i
                empty(pe, half, k)
                if i == 0:
                    pe.wait_ge(acc_lo_done, g + 1)
                for j in range(HC):
                    split_matmul(work[:, k % 2, :],
                                 (sh_hi[:, j, i * P:(i + 1) * P], sh_lo[:, j, i * P:(i + 1) * P]),
                                 wts(F_S2 + j * D, D), j == 0, False)
                split_matmul(work[:, k % 2, :], (acc_hi[:, i * P:(i + 1) * P], acc_lo[:, i * P:(i + 1) * P]),
                             wts(F_UP, D), False, True).then_inc(work_full[k % 2], 1)

            def group(g, more):
                half = front_half(g + 1)
                for n in range(UNITS + Y_LAG):
                    if n < UNITS:
                        if n == 0:
                            drained(pe, front_half(g), V_XL)
                        if isinstance(g, int) and g == 0:
                            pe.wait_ge(piece_lo, piece_of(F_EXP + (n // HC + 1) * E_COLS))
                        first_products(g, n)
                    if more:
                        if n in F_XT:
                            x_turn(g + 1, half, F_XT.index(n))
                        if n == UNITS:
                            route_logits(g + 1, half)
                        if n == UNITS + 1:
                            to_latent(g + 1, half)
                    if n >= Y_LAG:
                        second_product(g, n - Y_LAG)
                if more:
                    logits_turn(g + 1, half)
                    shared(g + 1, 0)
                    shared(g + 1, 1)
                    weights_turn(g + 1, half)
                for i in range(TILES):
                    output(g, out_half(g), i)

            def piece_of(col):
                return -(-col // PIECE)

            pe.wait_ge(f_ident, 2)
            for i in range(TILES):
                x_turn(0, 0, i)
            pe.wait_ge(small_step, 2)
            route_logits(0, 0)
            pe.wait_ge(piece_lo, piece_of(F_S1))
            to_latent(0, 0)
            logits_turn(0, 0)
            pe.wait_ge(piece_lo, piece_of(F_EXP))
            shared(0, 0)
            shared(0, 1)
            weights_turn(0, 0)
            group(0, True)
            with pe.Fori(1, GROUPS - 1) as g:
                group(g, True)
            group(GROUPS - 1, False)

        @block.scalar
        def _(act):
            def normalise(g, i):
                act.wait_ge(shift_done, 2 * (g + 1))
                act.activation(x[:, i, :], x[:, i, :], ACT.Identity, scale=nw[:, 4, i:i + 1],
                               bias=shift[:, i:i + 1]).then_inc(x_done, 1)

            def x_hi(g, half, i):
                full(act, half, V_XT + i)
                act.activation(xT_hi[:, :, i * P:(i + 1) * P],
                               work[:, i % 2, :].rearrange("p (m k) -> p m k", m=DC),
                               ACT.Copy).then_inc(xT_hi_done, 1)

            def logits_copy(g, half):
                full(act, half, V_LOGITS)
                act.activation(logits[:, :], work[0:2 * EXPERTS, V_LOGITS % 2, :],
                               ACT.Copy).then_inc(work_free[V_LOGITS % 2], 1)

            def latent_hi(g, half):
                full(act, half, V_XL)
                act.activation(xl_hi[:, :], work[:, V_XL % 2, :], ACT.Copy).then_inc(xl_hi_done, 1)

            def logits_back(g, half):
                full(act, half, V_LT)
                act.activation(weights[:, :, :],
                               work[:, V_LT % 2, 0:TILES * 2 * EXPERTS].rearrange("p (t e) -> p t e", t=TILES),
                               ACT.Copy).then_inc(work_free[V_LT % 2], 1)

            def sigmoid(g):
                act.wait_ge(route_step, ROUTE_OPS * g + 1)
                act.activation(route[:, 1, :, :], route[:, 0, :, :], ACT.Sigmoid).then_inc(sig_done, 1)

            def weights_copy(g, half):
                k = V_WT
                full(act, half, k)
                act.activation(wT[:, :], work[0:EXPERTS, k % 2, :], ACT.Copy).then_inc(work_free[k % 2], 1)

            def squares(g, j):
                n = ALL_UNITS * g + j
                act.wait_ge(g_full, n + 1)
                at_least(act, t1_done, n - 1)
                act.activation(square[:, j % 2, :], ps_g[:, j % 2, :], ACT.Relu).then_inc(relu_done, 1)

            def squares_end(g, j):
                act.wait_ge(relu_done, ALL_UNITS * g + j + 1)
                act.activation(square[:, j % 2, :], square[:, j % 2, :], ACT.Square).then_inc(square_done, 1)

            def hidden_hi(g, j):
                n = ALL_UNITS * g + j
                if j < HC:
                    if not (isinstance(g, int) and g == 0):
                        full(act, out_half(g - 1), out_use(g - 1) + TILES - 1)
                    act.wait_ge(t1_done, n + 1)
                    dst = sh_hi[:, j, :]
                else:
                    act.wait_ge(t_done, UNITS * g + j - HC + 1)
                    at_least(act, y_done, UNITS * g + j - HC - 1)
                    dst = t_hi[:, j % 2, :]
                act.activation(dst, t[:, j % 2, :], ACT.Copy).then_inc(t_hi_done, 1)

            def sum_hi(g):
                act.wait_ge(y_done, UNITS * (g + 1))
                act.activation(acc_hi, ps_y[:, :], ACT.Copy).then_inc(acc_hi_done, 1)

            def split(i):
                act.wait_ge(s_piece[i], 16)
                act.activation(piece(f_hi, i), staged(i), ACT.Copy).then_inc(piece_hi, 1)

            def group(g, more):
                half = front_half(g + 1)
                for n in range(UNITS):
                    squares(g, HC + n)
                    squares_end(g, HC + n)
                    hidden_hi(g, HC + n - 1)
                    if isinstance(g, int) and g == 0 and n in F_SPLIT:
                        split(EARLY_PIECES + F_SPLIT.index(n))
                    if more and n in F_XN:
                        normalise(g + 1, F_XN.index(n))
                    if more and n in F_XT:
                        x_hi(g + 1, half, F_XT.index(n))
                hidden_hi(g, HC + UNITS - 1)
                if more:
                    logits_copy(g + 1, half)
                    latent_hi(g + 1, half)
                sum_hi(g)
                if more:
                    logits_back(g + 1, half)
                    sigmoid(g + 1)
                    squares(g + 1, 0)
                    squares_end(g + 1, 0)
                    squares(g + 1, 1)
                    squares_end(g + 1, 1)
                    weights_copy(g + 1, half)
                    hidden_hi(g + 1, 0)

            split(0)
            for i in range(TILES):
                normalise(0, i)
            split(1)
            for i in range(TILES):
                x_hi(0, 0, i)
            split(2)
            split(3)
            logits_copy(0, 0)
            latent_hi(0, 0)
            split(4)
            logits_back(0, 0)
            sigmoid(0)
            split(5)
            squares(0, 0)
            squares_end(0, 0)
            split(6)
            squares(0, 1)
            squares_end(0, 1)
            split(7)
            weights_copy(0, 0)
            hidden_hi(0, 0)
            group(0, True)
            with act.Fori(1, GROUPS - 1) as g:
                group(g, True)
            group(GROUPS - 1, False)

        @block.vector
        def _(dve):
            def x_moments_of(g, part):
                if part < TILES:
                    dve.wait_ge(x_loaded, 16 * (g + 1))
                    dve.bn_stats(stats[:, part, :], x[:, part, :]).then_inc(x_stats, 1)
                else:
                    for i in range(TILES):
                        wait_alone(dve, x_stats, TILES * g + i + 1, dve_passed)
                        dve.bn_aggr(moments[:, i, :], stats[:, i, :]).then_inc(x_moments, 1)

            def x_seed(g):
                dve.wait_ge(x_moments, TILES * (g + 1))
                rsqrt_seed(dve, newton, NEWTON_OPS * g, moments[:, :, 1], nw[:, 0, :], nw[:, 1, :],
                           nw[:, 2, :].bitcast(I32), nw[:, 4, :])

            def x_rstd(g, k):
                rsqrt_steps(dve, newton, NEWTON_OPS * g, nw[:, 1, :], nw[:, 3, :], nw[:, 4, :],
                            dve_passed, (k,))

            def x_shift(g):
                dve.wait_ge(newton, NEWTON_OPS * (g + 1))
                at_least(dve, x_done, TILES * g)
                shift_of(dve, shift_done, g, moments[:, :, 0], nw[:, 4, :], nw[:, 3, :], shift[:, :],
                         dve_passed)

            def x_lo(g, half, i):
                dve.wait_ge(xT_hi_done, TILES * g + i + 1)
                dve.tensor_tensor(xT_lo[:, :, i * P:(i + 1) * P],
                                  work[:, i % 2, :].rearrange("p (m k) -> p m k", m=DC),
                                  xT_hi[:, :, i * P:(i + 1) * P].bitcast(F32),
                                  ALU.subtract).then_inc(work_free[i % 2], 1)

            def latent_lo(g, half):
                dve.wait_ge(xl_hi_done, g + 1)
                dve.tensor_tensor(xl_lo[:, :], work[:, V_XL % 2, :], xl_hi[:, :].bitcast(F32),
                                  ALU.subtract).then_inc(work_free[V_XL % 2], 1)

            def routing(g, half):
                base = ROUTE_OPS * g
                count = [0]

                def did(op):
                    op.then_inc(route_step, 1)
                    count[0] += 1

                def done(n):
                    dve.wait_ge(route_step, base + n)

                r = [route[:, i, :, :] for i in range(6)]
                drained(dve, half, V_LT)
                did(dve.tensor_tensor(r[0], weights[:, :, 0:EXPERTS], weights[:, :, EXPERTS:], ALU.add))
                dve.wait_ge(sig_done, g + 1)
                did(dve.tensor_tensor(r[2], r[1], bias[:, :].rearrange("p (o e) -> p o e", o=1)
                                      .to_broadcast([P, TILES, EXPERTS]), ALU.add))
                for i in range(TILES):
                    wait_alone(dve, route_step, base + 2, dve_passed)
                    did(dve.max(top[:, i, :], route[:, 2, i, :]))
                for i in range(TILES):
                    wait_alone(dve, route_step, base + 3 + i, dve_passed)
                    did(dve.match_replace(route[:, 3, i, :], top[:, i, :], route[:, 2, i, :], TAKEN))
                done(10)
                did(dve.tensor_tensor(r[4], r[3], r[2], ALU.not_equal))
                done(11)
                did(dve.tensor_tensor(r[5], r[4], r[1], ALU.mult))
                done(12)
                did(dve.tensor_reduce(wsum[:, 0, :], r[5], AX.X, ALU.add))
                done(13)
                did(dve.reciprocal(wsum[:, 1, :], wsum[:, 0, :]))
                done(14)
                did(dve.scalar_tensor_tensor(out=weights[:, :, 0:EXPERTS], in0=r[5], scalar=ROUTE_SCALE,
                                             in1=wsum[:, 1, :].rearrange("p (t o) -> p t o", o=1)
                                             .to_broadcast([P, TILES, EXPERTS]),
                                             op0=ALU.mult, op1=ALU.mult))
                assert count[0] == ROUTE_OPS

            def linear(g, j):
                n = ALL_UNITS * g + j
                dve.wait_ge(square_done, n + 1)
                dve.wait_ge(u_full, n + 1)
                at_least(dve, t_lo_done, n - 1)
                dve.tensor_tensor(t[:, j % 2, :], ps_u[:, j % 2, :], square[:, j % 2, :],
                                  ALU.mult).then_inc(t1_done, 1)

            def weigh(g, j):
                dve.wait_ge(t1_done, ALL_UNITS * g + j + 1)
                e = (j - HC) // HC
                dve.wait_ge(w_spread[e % 2], 16 * ((EXPERTS // 2) * g + e // 2 + 1))
                dve.tensor_tensor(t[:, j % 2, :], t[:, j % 2, :], w_all[:, e % 2, :], ALU.mult).then_inc(t_done, 1)

            def sum_lo(g):
                dve.wait_ge(acc_hi_done, g + 1)
                dve.tensor_tensor(acc_lo, ps_y[:, :], acc_hi.bitcast(F32),
                                  ALU.subtract).then_inc(acc_lo_done, 1)

            def add_out(g, i):
                k = out_use(g) + i
                full(dve, out_half(g), k)
                if i == 0:
                    dve.wait_ge(fres_loaded, 16 * (g + 1))
                dve.tensor_tensor(res[:, i, :], res[:, i, :], work[:, k % 2, :],
                                  ALU.add).then_inc(work_free[k % 2], 1)

            def split(i):
                dve.wait_ge(piece_hi, i + 1)
                dve.tensor_tensor(piece(f_lo, i), staged(i), piece(f_hi, i).bitcast(F32),
                                  ALU.subtract).then_inc(piece_lo, 1)

            def group(g, more):
                half = front_half(g + 1)
                for n in range(UNITS):
                    linear(g, HC + n)
                    weigh(g, HC + n)
                    if isinstance(g, int) and g == 0 and n in F_SPLIT:
                        split(EARLY_PIECES + F_SPLIT.index(n))
                    if more:
                        if n in F_STATS:
                            x_moments_of(g + 1, F_STATS.index(n))
                        if n == F_MOMENTS:
                            x_moments_of(g + 1, TILES)
                        if n == F_SEED:
                            x_seed(g + 1)
                        if n in F_RSTD:
                            x_rstd(g + 1, F_RSTD.index(n))
                        if n == F_SHIFT:
                            x_shift(g + 1)
                        if n in F_XT:
                            x_lo(g + 1, half, F_XT.index(n))
                if more:
                    latent_lo(g + 1, half)
                sum_lo(g)
                if more:
                    routing(g + 1, half)
                    linear(g + 1, 0)
                    linear(g + 1, 1)
                for i in range(TILES):
                    add_out(g, i)

            dve.memset(gate[:, :, :].bitcast(F32), 0.0).then_inc(f_zeroed, 1)
            dve.wait_ge(f_zeroed, 1)
            dve.wait_ge(small_loaded, 32)
            dve.tensor_copy(gate[:, :, 0:EXPERTS], gate_raw[:, :, :]).then_inc(small_step, 1)
            dve.wait_ge(small_step, 1)
            dve.tensor_tensor(gate[:, :, EXPERTS:2 * EXPERTS], gate_raw[:, :, :],
                              gate[:, :, 0:EXPERTS].bitcast(F32), ALU.subtract).then_inc(small_step, 1)
            for part in range(TILES + 1):
                x_moments_of(0, part)
            x_seed(0)
            for k in range(3):
                x_rstd(0, k)
            x_shift(0)
            split(0)
            split(1)
            for i in range(TILES):
                x_lo(0, 0, i)
            split(2)
            split(3)
            latent_lo(0, 0)
            split(4)
            routing(0, 0)
            split(5)
            linear(0, 0)
            split(6)
            linear(0, 1)
            split(7)
            group(0, True)
            with dve.Fori(1, GROUPS - 1) as g:
                group(g, True)
            group(GROUPS - 1, False)


_F = "L0_ffn_"
_A = "L0_attn_"


def _chunks(w):
    return w.reshape(w.shape[0] // P, P, w.shape[1]).transpose(1, 0, 2).reshape(P, -1)


def build(nc, table, tok, lora_b, w_attn, ln, w_ffn, w_gate, biases, out):
    h2 = nc.dram_tensor("h2", [GROUPS * TOK, D], F32, kind="Internal").ap()
    attention_phase(nc, table, tok, lora_b, w_attn, ln, h2)
    w_rows = nc.dram_tensor("w_rows", [GROUPS * EXPERTS, TOK], F32, kind="Internal").ap()
    ffn_phase(nc, h2, w_ffn, w_gate, biases, w_rows, out)


def kernel(**inputs):
    import numpy as np
    import concourse.bacc as bacc
    from concourse.bass_utils import run_bass_kernel_spmd

    a = {k: np.asarray(v) for k, v in inputs.items()}
    expert = []
    for e in range(EXPERTS):
        expert += [a[_F + "rw1"][e].T, a[_F + "rwg"][e].T, _chunks(a[_F + "rw2"][e].T)]
    laid_out = {
        "table": np.concatenate([a["L0_tok_base_weight"], a["L0_tok_lora_A"].T], 1),
        "tok": a["x"].T,
        "lora_b": a["L0_tok_lora_B"].T,
        "w_attn": np.concatenate([
            _chunks(np.concatenate([a[_A + "W_dq"], a[_A + "W_dkv"]], 1)),
            a[_A + "W_uq"], a[_A + "W_ukv"], _chunks(a[_A + "W_o"].T)], 1),
        "ln": np.stack([a[_A + "q_ln_g"], a[_A + "q_ln_b"], a[_A + "kv_ln_g"], a[_A + "kv_ln_b"]], 1),
        "w_ffn": np.concatenate([
            _chunks(a[_F + "Wdown"].T), _chunks(a[_F + "sw1"].T), _chunks(a[_F + "swg"].T),
            _chunks(a[_F + "sw2"].T), a[_F + "Wup"].T] + expert, 1),
        "w_gate": _chunks(a[_F + "Wg"].T).reshape(P, DC, EXPERTS),
        "biases": np.broadcast_to(a[_F + "biases"], (P, EXPERTS)),
    }
    nc = bacc.Bacc("TRN2", target_bir_lowering=False, num_devices=1)
    arrays, args = {}, []
    for name, array in laid_out.items():
        array = np.ascontiguousarray(array)
        arrays["in_" + name] = array
        args.append(nc.dram_tensor("in_" + name, array.shape, mybir.dt.from_np(array.dtype),
                                   kind="ExternalInput").ap())
    out = nc.dram_tensor("out_0", (SEQS * P, D), F32, kind="ExternalOutput").ap()
    build(nc, *args, out)
    r = run_bass_kernel_spmd(nc, [arrays], core_ids=[0])
    return r.results[0]["out_0"].reshape(SEQS, P, D)
```
